# Optimizing a Trainium2 kernel written in Bass

```python
import numpy as np
import jax
import jax.numpy as jnp

def _softmax(x, axis=-1):
    return jax.nn.softmax(x, axis=axis)

def _gelu(x):
    return jax.nn.gelu(x, approximate=True)

def _silu(x):
    return jax.nn.silu(x)

def _sigmoid(x):
    return jax.nn.sigmoid(x)

def _layernorm(x, axis=-1, eps=1e-05):
    m = jnp.mean(x, axis=axis, keepdims=True)
    v = jnp.var(x, axis=axis, keepdims=True)
    return (x - m) / jnp.sqrt(v + eps)

def _scatter_add(tgt, idx, src, axis=0):
    return tgt.at[idx].add(src)

def _segment_sum(src, seg, n):
    return jax.ops.segment_sum(src, seg, n)
kernel_name = 'mk_decoder_postln_d2_seqx_r4_3f0a8c'

def setup_inputs(seed: int=0):
    np.random.seed(seed)
    _w = jnp.asarray

    def _rec_inputs():
        import jax
        import jax.numpy as jnp
        _rk = jax.random.key(seed)
        x = 7.22e-05 + 1 * jax.random.normal(jax.random.fold_in(_rk, 1), (8, 256, 512), jnp.float32)
        _lenS = 256 - jax.random.randint(jax.random.fold_in(_rk, 7), (8,), 0, max(1, 256 // 4) + 1, jnp.int32)
        _lenS2 = 256 - jax.random.randint(jax.random.fold_in(_rk, 8), (8,), 0, max(1, 256 // 4) + 1, jnp.int32)
        _ctx_1024P = jax.random.normal(jax.random.fold_in(_rk, 11), (8, 16, 256), jnp.float32)
        _ctx_1024c = jax.random.dirichlet(jax.random.fold_in(_rk, 511), 0.3 * jnp.ones((16,), jnp.float32), (8, 256))
        _ctx_1024t = jnp.einsum('bsk,bkd->bsd', _ctx_1024c, _ctx_1024P)
        _ctx_1024t = _ctx_1024t * jax.lax.rsqrt(jnp.mean(jnp.square(_ctx_1024t)) + 1e-12) * 0.953939
        ctx_1024 = -1.39393e-06 + 0.999914 * (_ctx_1024t + 0.3 * jax.random.normal(jax.random.fold_in(_rk, 611), (8, 256, 256), jnp.float32))
        fside_BxSx2_0 = jax.random.uniform(jax.random.fold_in(_rk, 12), (8, 256, 2), jnp.float32, 0.0, 0.999707)
        _validS = jnp.arange(256)[None, :] < _lenS[:, None]
        _validS2 = jnp.arange(256)[None, :] < _lenS2[:, None]
        _causal = jnp.tril(jnp.ones((256, 256), dtype=bool))
        mask_BxS2_bf1 = jnp.ones((8, 256), dtype=bool)
        return (x, ctx_1024, fside_BxSx2_0, mask_BxS2_bf1)
    x, ctx_1024, fside_BxSx2_0, mask_BxS2_bf1 = _rec_inputs()

    def _L0_attn_setup():
        import jax, jax.numpy as jnp
        import numpy as np
        B, N, E = (2, 512, 512)
        H, D = (16, 128)
        BASE = 10000.0

        def rope(t, offset=0):
            d = t.shape[-1]
            pos = jnp.arange(t.shape[1], dtype=jnp.float32) + offset
            inv = BASE ** (-jnp.arange(0, d, 2, dtype=jnp.float32) / d)
            ang = pos[:, None] * inv[None, :]
            cos = jnp.cos(ang)[None, :, None, :]
            sin = jnp.sin(ang)[None, :, None, :]
            t1, t2 = (t[..., :d // 2], t[..., d // 2:])
            return jnp.concatenate([t1 * cos - t2 * sin, t2 * cos + t1 * sin], axis=-1)
        key = jax.random.key(seed)
        ks = jax.random.split(key, 6)
        s = lambda k, shape, fan: jax.random.normal(k, shape, jnp.float32) / np.sqrt(fan)
        return {'x': jax.random.normal(ks[0], (B, N, E), jnp.float32), 'Wq': s(ks[1], (H * D, E), E), 'Wkv': s(ks[2], (2 * D, E), E), 'Wkvh': s(ks[3], (2 * H, E), E), 'Wg': s(ks[4], (2 * H, E), E), 'Wout': s(ks[5], (E, H * D), H * D)}
    _L0_attn_all = _L0_attn_setup()
    _L0_attn_in = {k: v for k, v in _L0_attn_all.items() if k in ('Wq', 'Wkv', 'Wkvh', 'Wg', 'Wout')}
    del _L0_attn_all

    def _L0_xattn_setup():
        import jax, jax.numpy as jnp
        import numpy as np
        DIM = 512
        CTX_DIM = 256
        N_HEADS = 32
        HEAD_DIM = DIM // N_HEADS
        POS_DIM = 2
        B, N, CTXN = (2, 512, 512)
        ROPE_BASE = 10000.0

        def apply_axial_rope(x, pos):
            b, n, h, d = x.shape
            p = pos.shape[-1]
            dpa = d // p
            half = dpa // 2
            freqs = ROPE_BASE ** (-jnp.arange(half, dtype=x.dtype) / half)
            ang = pos[..., :, None] * freqs
            cos = jnp.cos(ang)[:, :, None, :, :]
            sin = jnp.sin(ang)[:, :, None, :, :]
            xr = x.reshape(b, n, h, p, half, 2)
            x1, x2 = (xr[..., 0], xr[..., 1])
            out = jnp.stack([x1 * cos - x2 * sin, x1 * sin + x2 * cos], axis=-1)
            return out.reshape(b, n, h, d)
        key = jax.random.key(seed)
        ks = jax.random.split(key, 8)
        x = jax.random.normal(ks[0], (B, N, DIM), jnp.float32)
        ctx = jax.random.normal(ks[1], (B, CTXN, CTX_DIM), jnp.float32)
        pos_map = jax.random.uniform(ks[2], (B, N, POS_DIM), jnp.float32)
        ctx_pos_map = jax.random.uniform(ks[3], (B, CTXN, POS_DIM), jnp.float32)
        Wq = jax.random.normal(ks[4], (DIM, DIM), jnp.float32) / np.sqrt(DIM)
        Wkv = jax.random.normal(ks[5], (CTX_DIM, 2 * DIM), jnp.float32) / np.sqrt(CTX_DIM)
        Wout = jax.random.normal(ks[6], (DIM, DIM), jnp.float32) / np.sqrt(DIM)
        bout = jnp.zeros((DIM,), jnp.float32)
        return {'x': x, 'ctx': ctx, 'pos_map': pos_map, 'ctx_pos_map': ctx_pos_map, 'Wq': Wq, 'Wkv': Wkv, 'Wout': Wout, 'bout': bout}
    _L0_xattn_all = _L0_xattn_setup()
    _L0_xattn_in = {k: v for k, v in _L0_xattn_all.items() if k in ('Wq', 'Wkv', 'Wout', 'bout')}
    del _L0_xattn_all

    def _L0_ffn_setup():
        import jax, jax.numpy as jnp
        import numpy as np
        NUM_EXPERTS = 8
        TOP_K = 2
        LORA_ALPHA = 2.0
        LORA_RANK = 16
        D_MODEL = 512
        D_HIDDEN = 1408
        key = jax.random.key(seed)
        ks = jax.random.split(key, 11)
        B, S, D, H, E, R = (2, 256, D_MODEL, D_HIDDEN, NUM_EXPERTS, LORA_RANK)
        sd = 1.0 / np.sqrt(D)
        sh = 1.0 / np.sqrt(H)
        x = jax.random.normal(ks[0], (B, S, D), jnp.float32)
        gate_w = jax.random.normal(ks[1], (E, D), jnp.float32) * sd
        w_up = jax.random.normal(ks[2], (H, D), jnp.float32) * sd
        w_gate = jax.random.normal(ks[3], (H, D), jnp.float32) * sd
        w_down = jax.random.normal(ks[4], (D, H), jnp.float32) * sh
        up_A = jax.random.normal(ks[5], (E, R, D), jnp.float32) * sd
        up_B = jax.random.normal(ks[6], (E, H, R), jnp.float32) * 0.02
        gate_A = jax.random.normal(ks[7], (E, R, D), jnp.float32) * sd
        gate_B = jax.random.normal(ks[8], (E, H, R), jnp.float32) * 0.02
        down_A = jax.random.normal(ks[9], (E, R, H), jnp.float32) * sh
        down_B = jax.random.normal(ks[10], (E, D, R), jnp.float32) * 0.02
        return {'x': x, 'gate_w': gate_w, 'w_up': w_up, 'w_gate': w_gate, 'w_down': w_down, 'up_A': up_A, 'up_B': up_B, 'gate_A': gate_A, 'gate_B': gate_B, 'down_A': down_A, 'down_B': down_B}
    _L0_ffn_all = _L0_ffn_setup()
    _L0_ffn_in = {k: v for k, v in _L0_ffn_all.items() if k in ('gate_w', 'w_up', 'w_gate', 'w_down', 'up_A', 'up_B', 'gate_A', 'gate_B', 'down_A', 'down_B')}
    del _L0_ffn_all

    def _L1_attn_setup():
        import jax, jax.numpy as jnp
        import numpy as np
        D_IN = 512
        D_OUT = 512
        NUM_HEADS = 16
        NUM_KV_GROUPS = 4
        GROUP_SIZE = NUM_HEADS // NUM_KV_GROUPS
        HEAD_DIM = D_OUT // NUM_HEADS
        key = jax.random.key(seed)
        ks = jax.random.split(key, 6)
        b, n = (2, 512)
        x = jax.random.normal(ks[0], (b, n, D_IN), dtype=jnp.float32)
        Wq = jax.random.normal(ks[1], (D_IN, D_OUT), dtype=jnp.float32) * (1.0 / np.sqrt(D_IN))
        Wk = jax.random.normal(ks[2], (D_IN, NUM_KV_GROUPS * HEAD_DIM), dtype=jnp.float32) * (1.0 / np.sqrt(D_IN))
        Wv = jax.random.normal(ks[3], (D_IN, NUM_KV_GROUPS * HEAD_DIM), dtype=jnp.float32) * (1.0 / np.sqrt(D_IN))
        Wo = jax.random.normal(ks[4], (D_OUT, D_OUT), dtype=jnp.float32) * (1.0 / np.sqrt(D_OUT))
        bo = jax.random.normal(ks[5], (D_OUT,), dtype=jnp.float32) * 0.01
        return {'x': x, 'Wq': Wq, 'Wk': Wk, 'Wv': Wv, 'Wo': Wo, 'bo': bo}
    _L1_attn_all = _L1_attn_setup()
    _L1_attn_in = {k: v for k, v in _L1_attn_all.items() if k in ('Wq', 'Wk', 'Wv', 'Wo', 'bo')}
    del _L1_attn_all

    def _L1_xattn_setup():
        import jax, jax.numpy as jnp
        import numpy as np
        N_HEADS = 16
        N_KV_HEADS = 8
        HEAD_DIM = 128
        D_TEXT = 512
        D_VISION = 256
        GROUPS = N_HEADS // N_KV_HEADS
        key = jax.random.key(seed)
        ks = jax.random.split(key, 6)
        B, T_text, T_vis = (4, 512, 144)
        text_hidden = jax.random.normal(ks[0], (B, T_text, D_TEXT), dtype=jnp.float32)
        vision_tokens = jax.random.normal(ks[1], (B, T_vis, D_VISION), dtype=jnp.float32)
        vision_mask = jnp.ones((B, T_vis), dtype=bool)
        s = 0.02
        Wq = jax.random.normal(ks[2], (D_TEXT, N_HEADS * HEAD_DIM), dtype=jnp.float32) * s
        Wk = jax.random.normal(ks[3], (D_VISION, N_KV_HEADS * HEAD_DIM), dtype=jnp.float32) * s
        Wv = jax.random.normal(ks[4], (D_VISION, N_KV_HEADS * HEAD_DIM), dtype=jnp.float32) * s
        Wo = jax.random.normal(ks[5], (N_HEADS * HEAD_DIM, D_TEXT), dtype=jnp.float32) * s
        return {'text_hidden': text_hidden, 'vision_tokens': vision_tokens, 'vision_mask': vision_mask, 'Wq': Wq, 'Wk': Wk, 'Wv': Wv, 'Wo': Wo}
    _L1_xattn_all = _L1_xattn_setup()
    _L1_xattn_in = {k: v for k, v in _L1_xattn_all.items() if k in ('Wq', 'Wk', 'Wv', 'Wo')}
    del _L1_xattn_all

    def _L1_ffn_setup():
        import jax, jax.numpy as jnp
        import numpy as np
        EPS = 1e-08

        def _rmsnorm(x, g):
            return g * (x * jax.lax.rsqrt(jnp.mean(x * x, axis=-1, keepdims=True) + EPS))

        def _act_quant(x):
            scale = 127.0 / jnp.clip(jnp.max(jnp.abs(x), axis=-1, keepdims=True), 0.0001, None)
            y = jnp.clip(jnp.round(x * scale), -128, 127) / scale
            return x + jax.lax.stop_gradient(y - x)

        def _ternary_quant(w):
            s = jnp.mean(jnp.abs(w))
            wq = jnp.round(jnp.tanh(w / (s + EPS))) * jnp.arctanh(s)
            return w + jax.lax.stop_gradient(wq - w)

        def _linear_bit(x, w, g):
            xq = _act_quant(_rmsnorm(x, g))
            wq = _ternary_quant(w)
            return jnp.einsum('bsd,od->bso', xq, wq)
        key = jax.random.key(seed)
        k = jax.random.split(key, 4)
        B, S, D, H = (4, 512, 512, 2048)
        std_up = float(np.sqrt(2.0 / (D + H)))
        std_dn = float(np.sqrt(2.0 / (H + D)))
        return {'x': jax.random.normal(k[0], (B, S, D), dtype=jnp.float32), 'w1': jax.random.normal(k[1], (H, D), dtype=jnp.float32) * std_up, 'g1': jnp.ones((D,), dtype=jnp.float32), 'w2': jax.random.normal(k[2], (H, D), dtype=jnp.float32) * std_up, 'g2': jnp.ones((D,), dtype=jnp.float32), 'w3': jax.random.normal(k[3], (D, H), dtype=jnp.float32) * std_dn, 'g3': jnp.ones((H,), dtype=jnp.float32)}
    _L1_ffn_all = _L1_ffn_setup()
    _L1_ffn_in = {k: v for k, v in _L1_ffn_all.items() if k in ('w1', 'g1', 'w2', 'g2', 'w3', 'g3')}
    del _L1_ffn_all
    return {'x': x, 'ctx_1024': ctx_1024, 'fside_BxSx2_0': fside_BxSx2_0, 'mask_BxS2_bf1': mask_BxS2_bf1, 'L0_attn_Wq': _L0_attn_in['Wq'], 'L0_attn_Wkv': _L0_attn_in['Wkv'], 'L0_attn_Wkvh': _L0_attn_in['Wkvh'], 'L0_attn_Wg': _L0_attn_in['Wg'], 'L0_attn_Wout': _L0_attn_in['Wout'], 'L0_xattn_Wq': _L0_xattn_in['Wq'], 'L0_xattn_Wkv': _L0_xattn_in['Wkv'], 'L0_xattn_Wout': _L0_xattn_in['Wout'], 'L0_xattn_bout': _L0_xattn_in['bout'], 'L0_ffn_gate_w': _L0_ffn_in['gate_w'], 'L0_ffn_w_up': _L0_ffn_in['w_up'], 'L0_ffn_w_gate': _L0_ffn_in['w_gate'], 'L0_ffn_w_down': _L0_ffn_in['w_down'], 'L0_ffn_up_A': _L0_ffn_in['up_A'], 'L0_ffn_up_B': _L0_ffn_in['up_B'], 'L0_ffn_gate_A': _L0_ffn_in['gate_A'], 'L0_ffn_gate_B': _L0_ffn_in['gate_B'], 'L0_ffn_down_A': _L0_ffn_in['down_A'], 'L0_ffn_down_B': _L0_ffn_in['down_B'], 'L1_attn_Wq': _L1_attn_in['Wq'], 'L1_attn_Wk': _L1_attn_in['Wk'], 'L1_attn_Wv': _L1_attn_in['Wv'], 'L1_attn_Wo': _L1_attn_in['Wo'], 'L1_attn_bo': _L1_attn_in['bo'], 'L1_xattn_Wq': _L1_xattn_in['Wq'], 'L1_xattn_Wk': _L1_xattn_in['Wk'], 'L1_xattn_Wv': _L1_xattn_in['Wv'], 'L1_xattn_Wo': _L1_xattn_in['Wo'], 'L1_ffn_w1': _L1_ffn_in['w1'], 'L1_ffn_g1': _L1_ffn_in['g1'], 'L1_ffn_w2': _L1_ffn_in['w2'], 'L1_ffn_g2': _L1_ffn_in['g2'], 'L1_ffn_w3': _L1_ffn_in['w3'], 'L1_ffn_g3': _L1_ffn_in['g3']}

def reference(x, ctx_1024, fside_BxSx2_0, mask_BxS2_bf1, L0_attn_Wq, L0_attn_Wkv, L0_attn_Wkvh, L0_attn_Wg, L0_attn_Wout, L0_xattn_Wq, L0_xattn_Wkv, L0_xattn_Wout, L0_xattn_bout, L0_ffn_gate_w, L0_ffn_w_up, L0_ffn_w_gate, L0_ffn_w_down, L0_ffn_up_A, L0_ffn_up_B, L0_ffn_gate_A, L0_ffn_gate_B, L0_ffn_down_A, L0_ffn_down_B, L1_attn_Wq, L1_attn_Wk, L1_attn_Wv, L1_attn_Wo, L1_attn_bo, L1_xattn_Wq, L1_xattn_Wk, L1_xattn_Wv, L1_xattn_Wo, L1_ffn_w1, L1_ffn_g1, L1_ffn_w2, L1_ffn_g2, L1_ffn_w3, L1_ffn_g3):
    import jax
    import jax.numpy as jnp

    def _L0_attn_ref(x, Wq, Wkv, Wkvh, Wg, Wout):
        import jax, jax.numpy as jnp
        import numpy as np
        B, N, E = (2, 512, 512)
        H, D = (16, 128)
        BASE = 10000.0

        def rope(t, offset=0):
            d = t.shape[-1]
            pos = jnp.arange(t.shape[1], dtype=jnp.float32) + offset
            inv = BASE ** (-jnp.arange(0, d, 2, dtype=jnp.float32) / d)
            ang = pos[:, None] * inv[None, :]
            cos = jnp.cos(ang)[None, :, None, :]
            sin = jnp.sin(ang)[None, :, None, :]
            t1, t2 = (t[..., :d // 2], t[..., d // 2:])
            return jnp.concatenate([t1 * cos - t2 * sin, t2 * cos + t1 * sin], axis=-1)
        b, n, _ = x.shape
        q = (x @ Wq.T).reshape(b, n, H, D)
        kv = x @ Wkv.T
        kv_head = x @ Wkvh.T
        g = x @ Wg.T
        log_f = jnp.concatenate([jnp.zeros((b, 1, 2 * H), jnp.float32), jax.nn.log_sigmoid(g)], axis=1)
        log_f_cumsum = jnp.cumsum(log_f, axis=1)[:, :-1]
        kv_head = kv_head * jnp.exp(log_f_cumsum)
        kv_head = jnp.cumsum(kv_head, axis=1)
        kp, vp = (kv[..., :D], kv[..., D:])
        kh, vh = (kv_head[..., :H], kv_head[..., H:])
        k = jnp.einsum('bnd,bnh->bnhd', kp, kh)
        v = jnp.einsum('bnd,bnh->bnhd', vp, vh)
        q = rope(q)
        k = rope(k)
        scale = 1.0 / np.sqrt(D)
        scores = jnp.einsum('bnhd,bmhd->bhnm', q, k) * scale
        mask = jnp.tril(jnp.ones((n, n), bool))
        scores = jnp.where(mask[None, None], scores, -jnp.inf)
        p = jax.nn.softmax(scores, axis=-1)
        o = jnp.einsum('bhnm,bmhd->bnhd', p, v).reshape(b, n, H * D)
        return o @ Wout.T

    def _L0_xattn_ref(x, ctx, pos_map, ctx_pos_map, Wq, Wkv, Wout, bout):
        import jax, jax.numpy as jnp
        import numpy as np
        DIM = 512
        CTX_DIM = 256
        N_HEADS = 32
        HEAD_DIM = DIM // N_HEADS
        POS_DIM = 2
        B, N, CTXN = (2, 512, 512)
        ROPE_BASE = 10000.0

        def apply_axial_rope(x, pos):
            b, n, h, d = x.shape
            p = pos.shape[-1]
            dpa = d // p
            half = dpa // 2
            freqs = ROPE_BASE ** (-jnp.arange(half, dtype=x.dtype) / half)
            ang = pos[..., :, None] * freqs
            cos = jnp.cos(ang)[:, :, None, :, :]
            sin = jnp.sin(ang)[:, :, None, :, :]
            xr = x.reshape(b, n, h, p, half, 2)
            x1, x2 = (xr[..., 0], xr[..., 1])
            out = jnp.stack([x1 * cos - x2 * sin, x1 * sin + x2 * cos], axis=-1)
            return out.reshape(b, n, h, d)
        b, n, _ = x.shape
        ctx_n = ctx.shape[1]
        q = (x @ Wq).reshape(b, n, N_HEADS, HEAD_DIM)
        k, v = jnp.split(ctx @ Wkv, 2, axis=-1)
        k = k.reshape(b, ctx_n, N_HEADS, HEAD_DIM)
        v = v.reshape(b, ctx_n, N_HEADS, HEAD_DIM)
        q = apply_axial_rope(q, pos_map)
        k = apply_axial_rope(k, ctx_pos_map)
        scale = 1.0 / np.sqrt(HEAD_DIM).astype(np.float32)
        logits = jnp.einsum('bqhd,bkhd->bhqk', q, k) * scale
        w = jax.nn.softmax(logits, axis=-1)
        attn = jnp.einsum('bhqk,bkhd->bqhd', w, v)
        attn = attn.reshape(b, n, N_HEADS * HEAD_DIM)
        return attn @ Wout + bout

    def _L0_ffn_ref(x, gate_w, w_up, w_gate, w_down, up_A, up_B, gate_A, gate_B, down_A, down_B):
        import jax, jax.numpy as jnp
        import numpy as np
        NUM_EXPERTS = 8
        TOP_K = 2
        LORA_ALPHA = 2.0
        LORA_RANK = 16
        D_MODEL = 512
        D_HIDDEN = 1408
        B, S, D = x.shape
        H = w_up.shape[0]
        gate_logits = jnp.einsum('bsd,ed->bse', x, gate_w)
        topw, sel = jax.lax.top_k(gate_logits, TOP_K)
        topw = jax.nn.softmax(topw.astype(jnp.float32), axis=1).astype(x.dtype)
        xt = x.reshape(-1, D)
        wf = topw.reshape(-1, TOP_K)
        sf = sel.reshape(-1, TOP_K)
        base_up = xt @ w_up.T
        base_gate = xt @ w_gate.T
        mixed_h = jnp.zeros((xt.shape[0], H), x.dtype)
        lora_down = jnp.zeros_like(xt)
        for e in range(NUM_EXPERTS):
            c = jnp.sum(jnp.where(sf == e, wf, 0.0), axis=1)
            lo_up = LORA_ALPHA * (xt @ up_A[e].T @ up_B[e].T)
            lo_gate = LORA_ALPHA * (xt @ gate_A[e].T @ gate_B[e].T)
            h_e = jax.nn.silu(base_up + lo_up) * (base_gate + lo_gate)
            ch = c[:, None] * h_e
            mixed_h = mixed_h + ch
            lora_down = lora_down + LORA_ALPHA * (ch @ down_A[e].T @ down_B[e].T)
        out = mixed_h @ w_down.T + lora_down
        return out.reshape(B, S, D)

    def _L1_attn_ref(x, Wq, Wk, Wv, Wo, bo):
        import jax, jax.numpy as jnp
        import numpy as np
        D_IN = 512
        D_OUT = 512
        NUM_HEADS = 16
        NUM_KV_GROUPS = 4
        GROUP_SIZE = NUM_HEADS // NUM_KV_GROUPS
        HEAD_DIM = D_OUT // NUM_HEADS
        b, n, _ = x.shape
        q = (x @ Wq).reshape(b, n, NUM_KV_GROUPS, GROUP_SIZE, HEAD_DIM)
        k = (x @ Wk).reshape(b, n, NUM_KV_GROUPS, HEAD_DIM)
        v = (x @ Wv).reshape(b, n, NUM_KV_GROUPS, HEAD_DIM)
        scale = 1.0 / np.sqrt(HEAD_DIM).astype(np.float32)
        scores = jnp.einsum('bqgsd,bkgd->bgsqk', q, k) * scale
        causal = jnp.arange(n)[:, None] < jnp.arange(n)[None, :]
        scores = jnp.where(causal, -jnp.inf, scores)
        attn = jax.nn.softmax(scores, axis=-1)
        ctx = jnp.einsum('bgsqk,bkgd->bqgsd', attn, v)
        ctx = ctx.reshape(b, n, D_OUT)
        return ctx @ Wo + bo

    def _L1_xattn_ref(text_hidden, vision_tokens, vision_mask, Wq, Wk, Wv, Wo):
        import jax, jax.numpy as jnp
        import numpy as np
        N_HEADS = 16
        N_KV_HEADS = 8
        HEAD_DIM = 128
        D_TEXT = 512
        D_VISION = 256
        GROUPS = N_HEADS // N_KV_HEADS
        B, T_text, _ = text_hidden.shape
        T_vis = vision_tokens.shape[1]
        scale = jnp.float32(np.sqrt(HEAD_DIM))
        q = (text_hidden @ Wq).reshape(B, T_text, N_HEADS, HEAD_DIM).transpose(0, 2, 1, 3)
        k = (vision_tokens @ Wk).reshape(B, T_vis, N_KV_HEADS, HEAD_DIM).transpose(0, 2, 1, 3)
        v = (vision_tokens @ Wv).reshape(B, T_vis, N_KV_HEADS, HEAD_DIM).transpose(0, 2, 1, 3)
        k = jnp.repeat(k, GROUPS, axis=1)
        v = jnp.repeat(v, GROUPS, axis=1)
        scores = jnp.einsum('bhtd,bhsd->bhts', q, k) / scale
        mask = vision_mask[:, None, None, :]
        scores = jnp.where(mask, scores, -jnp.inf)
        attn = jax.nn.softmax(scores, axis=-1)
        attn = jnp.nan_to_num(attn, nan=0.0)
        out = jnp.einsum('bhts,bhsd->bhtd', attn, v)
        out = out.transpose(0, 2, 1, 3).reshape(B, T_text, N_HEADS * HEAD_DIM)
        return out @ Wo

    def _L1_ffn_ref(x, w1, g1, w2, g2, w3, g3):
        import jax, jax.numpy as jnp
        import numpy as np
        EPS = 1e-08

        def _rmsnorm(x, g):
            return g * (x * jax.lax.rsqrt(jnp.mean(x * x, axis=-1, keepdims=True) + EPS))

        def _act_quant(x):
            scale = 127.0 / jnp.clip(jnp.max(jnp.abs(x), axis=-1, keepdims=True), 0.0001, None)
            y = jnp.clip(jnp.round(x * scale), -128, 127) / scale
            return x + jax.lax.stop_gradient(y - x)

        def _ternary_quant(w):
            s = jnp.mean(jnp.abs(w))
            wq = jnp.round(jnp.tanh(w / (s + EPS))) * jnp.arctanh(s)
            return w + jax.lax.stop_gradient(wq - w)

        def _linear_bit(x, w, g):
            xq = _act_quant(_rmsnorm(x, g))
            wq = _ternary_quant(w)
            return jnp.einsum('bsd,od->bso', xq, wq)
        swish = jax.nn.silu(_linear_bit(x, w1, g1))
        x_v = _linear_bit(x, w2, g2)
        h = swish * x_v
        return _linear_bit(h, w3, g3)
    x = _layernorm(x + _L0_attn_ref(x, L0_attn_Wq, L0_attn_Wkv, L0_attn_Wkvh, L0_attn_Wg, L0_attn_Wout), axis=-1)
    x = _layernorm(x + _L0_xattn_ref(x, ctx_1024, fside_BxSx2_0, fside_BxSx2_0, L0_xattn_Wq, L0_xattn_Wkv, L0_xattn_Wout, L0_xattn_bout), axis=-1)
    x = _layernorm(x + _L0_ffn_ref(x, L0_ffn_gate_w, L0_ffn_w_up, L0_ffn_w_gate, L0_ffn_w_down, L0_ffn_up_A, L0_ffn_up_B, L0_ffn_gate_A, L0_ffn_gate_B, L0_ffn_down_A, L0_ffn_down_B), axis=-1)
    x = _layernorm(x + _L1_attn_ref(x, L1_attn_Wq, L1_attn_Wk, L1_attn_Wv, L1_attn_Wo, L1_attn_bo), axis=-1)
    x = _layernorm(x + _L1_xattn_ref(x, ctx_1024, mask_BxS2_bf1, L1_xattn_Wq, L1_xattn_Wk, L1_xattn_Wv, L1_xattn_Wo), axis=-1)
    x = _layernorm(x + _L1_ffn_ref(x, L1_ffn_w1, L1_ffn_g1, L1_ffn_w2, L1_ffn_g2, L1_ffn_w3, L1_ffn_g3), axis=-1)
    return x

_drawn_inputs = setup_inputs


def setup_inputs(seed=0):
    import zlib

    import numpy as np

    out = dict(_drawn_inputs(seed))
    spreads = {'L0_xattn_bout': (0.0, 0.1),
     'L1_ffn_g1': (1.0, 0.2),
     'L1_ffn_g2': (1.0, 0.2),
     'L1_ffn_g3': (1.0, 0.2)}
    factors = {'L0_ffn_gate_w': 3.577,
     'L0_ffn_w_up': 2.913,
     'L0_ffn_w_gate': 2.86,
     'L0_ffn_w_down': 2.868,
     'L0_ffn_up_A': 5.223,
     'L0_ffn_up_B': 5.145,
     'L0_ffn_gate_A': 5.198,
     'L0_ffn_gate_B': 5.211,
     'L0_ffn_down_A': 5.288,
     'L0_ffn_down_B': 5.289,
     'L1_xattn_Wq': 2.677}
    for name, (base, spread) in spreads.items():
        noise = np.random.default_rng([zlib.crc32(name.encode()), seed]).standard_normal(out[name].shape)
        drawn = base * np.exp(spread * noise) if base else spread * noise
        out[name] = jnp.asarray(drawn.astype(out[name].dtype))
    for name, factor in factors.items():
        out[name] = (out[name] * factor).astype(out[name].dtype)
    return out
```

```python
from contextlib import ExitStack

import numpy as np

import concourse.bass as bass
from concourse import mybir

F32 = mybir.dt.float32
F16 = mybir.dt.float16
BF16 = mybir.dt.bfloat16
U8 = mybir.dt.uint8
U32 = mybir.dt.uint32
ALU = mybir.AluOpType
ACT = mybir.ActivationFunctionType
X_AXIS = mybir.AxisListType.X

P = 128
B = 8
N = 256
NT = N // P
E = 512
KE = E // P
C = 256
KC = C // P
EPS = 1e-5
MASKED = -1e30


class Names:
    pass


class Counter:

    def __init__(self, handle, per_seq):
        self.handle = handle
        self.per_seq = per_seq

    def count(self, b, n):
        return self.handle, b * self.per_seq + (max(n, 0) + 1)


class Steps:

    def __init__(self, eng, counter, b):
        self.eng, self.counter, self.b, self.n = eng, counter, b, 0

    def done(self, ins):
        ins.then_inc(self.counter.handle, 1)
        self.n += 1
        self.eng.wait_ge(*self.counter.count(self.b, self.n))

    def check(self):
        assert self.n == self.counter.per_seq, (self.n, self.counter.per_seq)


class Scope:

    def __init__(self, nc, tag):
        self.nc, self.tag, self.stack, self.counters, self.sems = nc, tag, ExitStack(), [], []

    def __enter__(self):
        return self

    def __exit__(self, *a):
        with self.nc.Block() as block:
            @block.gpsimd
            def _(pool):
                for handle in self.sems:
                    pool.sem_clear(handle)
        self.stack.close()

    def sb(self, name, shape, dt):
        return self.stack.enter_context(self.nc.sbuf_tensor(f"{self.tag}_{name}", shape, dt))

    def counter(self, name, per_seq):
        self.counters.append(Counter(self.sem(name), per_seq))
        return self.counters[-1]

    def sem(self, name):
        self.sems.append(self.stack.enter_context(self.nc.semaphore(f"{self.tag}_{name}")))
        return self.sems[-1]

    def start_counters(self):
        with self.nc.Block() as block:
            @block.sync
            def _(sp):
                for counter in self.counters:
                    sp.sem_inc(counter.handle, 1)


def three(pe, out, a_hi, a_lo, b_hi, b_lo, first, last):
    pe.matmul(out, a_hi, b_hi, start=first, stop=False, skip_group_check=True)
    pe.matmul(out, a_hi, b_lo, start=False, stop=False, skip_group_check=True)
    return pe.matmul(out, a_lo, b_hi, start=False, stop=last, skip_group_check=True)


def load_and_split(nc, sc, G, pieces):
    flat = []
    for src, hi, lo in pieces:
        p, k, n = src.shape
        cuts = next(c for c in range(-(-n // G.STAGE), n + 1) if n % c == 0)
        width = n // cuts
        step = max(1, G.STAGE // width)
        for k0 in range(0, k, step):
            for c0 in range(0, n, width):
                at = (slice(None), slice(k0, min(k, k0 + step)), slice(c0, c0 + width))
                flat.append((src[at], hi[at], lo[at], p, at[1].stop - k0, width))
    landed = [sc.sem(f"w_landed{i}") for i in range(G.NSTAGE)]
    hi_done, lo_done = sc.sem("w_hi"), sc.sem("w_lo")

    def staged(i, p, k, n):
        return G.stage[0:p, i % G.NSTAGE, 0:k * n].rearrange("p (k n) -> p k n", k=k)

    with nc.Block() as block:
        @block.sync
        def _(sp):
            for i, (src, hi, lo, p, k, n) in enumerate(flat):
                if i >= G.NSTAGE:
                    sp.wait_ge(lo_done, i - G.NSTAGE + 1)
                sp.dma_start(staged(i, p, k, n), src).then_inc(landed[i % G.NSTAGE], 16)

        @block.scalar
        def _(act):
            for i, (src, hi, lo, p, k, n) in enumerate(flat):
                act.wait_ge(landed[i % G.NSTAGE], 16 * (i // G.NSTAGE + 1))
                act.copy(hi, staged(i, p, k, n)).then_inc(hi_done, 1)

        @block.vector
        def _(dve):
            for i, (src, hi, lo, p, k, n) in enumerate(flat):
                dve.wait_ge(hi_done, i + 1)
                dve.tensor_tensor(lo, staged(i, p, k, n), hi, ALU.subtract).then_inc(lo_done, 1)


def kt_view(w):
    return w.rearrange("(k p) n -> p k n", p=P)


def turn_x(pe, b, s, G, xcur, banks):
    pe.wait_ge(*s.xcur_ready.count(b, 1))
    for n in range(NT):
        for k in range(KE):
            last = pe.transpose(banks[n][:, k * P:(k + 1) * P], xcur[:, n, k * P:(k + 1) * P], G.ident[:, :])
        last.then_inc(s.x_turned.handle, 1)


def x_high(act, b, s, xT, banks):
    for n in range(NT):
        act.wait_ge(*s.x_turned.count(b, n + 1))
        act.copy(xT[0][:, :, n * P:(n + 1) * P], banks[n][:, :].rearrange("p (k t) -> p k t", k=KE))\
            .then_inc(s.x_hi.handle, 1)


def x_low(dve, b, s, xT, banks):
    for n in range(NT):
        dve.wait_ge(*s.x_hi.count(b, n + 1))
        at = slice(n * P, (n + 1) * P)
        dve.tensor_tensor(xT[1][:, :, at], banks[n][:, :].rearrange("p (k t) -> p k t", k=KE), xT[0][:, :, at],
                          ALU.subtract).then_inc(s.x_lo.handle, 1)


def fetch_x(pool, b, s, G, xcur):
    pool.wait_ge(*s.x_turned.count(b, 0))
    pool.tensor_copy(xcur[:, :, :], G.x[:, bass.ds(b * NT, NT), :]).then_inc(s.xcur_ready.handle, 1)


def x_counters(sc, s):
    s.xcur_ready = sc.counter("xcur_ready", 1)
    s.x_turned = sc.counter("x_turned", NT)
    s.x_hi = sc.counter("x_hi", NT)
    s.x_lo = sc.counter("x_lo", NT)


def add_and_norm(dve, s, b, n, y, y_ready, G, steps, scale=None):
    dve.wait_ge(*y_ready.count(b, n + 1))
    x_tile = G.x[:, bass.ds(b * NT + n, 1), :]
    y = y.rearrange("p (a e) -> p a e", a=1)
    if scale is None:
        steps.done(dve.tensor_tensor(G.r[:, n:n + 1, :], y, x_tile, ALU.add))
    else:
        steps.done(dve.scalar_tensor_tensor(G.r[:, n:n + 1, :], y, scale, x_tile, ALU.mult, ALU.add))
    steps.done(dve.bn_stats(G.stats[:, n, :], G.r[:, n, :]))
    dve.memset(G.junk[:, :], 0.0)
    steps.done(dve.bn_aggr(G.mv[:, n, :], G.stats[:, n, :]))
    dve.tensor_scalar(G.ve[:, n:n + 1], G.mv[:, n, 1:2], EPS, None, ALU.add).then_inc(s.var_ready.handle, 1)
    dve.wait_ge(*s.rstd_ready.count(b, n + 1))
    dve.tensor_scalar(x_tile, G.r[:, n:n + 1, :], G.mv[:, n, 0:1], G.rstd[:, n:n + 1],
                      ALU.subtract, ALU.mult).then_inc(s.x_done.handle, 1)


LN_STEPS = 3


def rstd_on_pool(pool, s, b, n, G):
    pool.wait_ge(*s.var_ready.count(b, n + 1))
    pool.tensor_tensor(G.rstd[:, n:n + 1], G.ve[:, n:n + 1], G.minus_half[:, 0:1], ALU.pow)\
        .then_inc(s.rstd_ready.handle, 1)


def ln_counters(sc, s):
    s.var_ready = sc.counter("var_ready", NT)
    s.rstd_ready = sc.counter("rstd_ready", NT)
    s.x_done = sc.counter("x_done", NT)


def attn0(nc, G, W):
    H, D = 16, 128
    QC = 4
    HC = H // QC
    NS = 2
    NPB = 3
    with Scope(nc, "a0") as sc:
        wq = [sc.sb(f"wq{i}", [P, KE, H * D], F16) for i in range(2)]
        wkv = [sc.sb(f"wkv{i}", [P, KE, 2 * D], F16) for i in range(2)]
        wgh = [sc.sb(f"wgh{i}", [P, KE, 4 * H], F16) for i in range(2)]
        wo = [sc.sb(f"wo{i}", [P, H, E], F16) for i in range(2)]
        load_and_split(nc, sc, G, [
            (kt_view(W["L0_attn_WqT"]), wq[0][:, :, :], wq[1][:, :, :]),
            (kt_view(W["L0_attn_WkvT"]), wkv[0][:, :, :], wkv[1][:, :, :]),
            (kt_view(W["L0_attn_WhT"]), wgh[0][:, :, :], wgh[1][:, :, :]),
            (kt_view(W["L0_attn_WoutT"]), wo[0][:, :, :], wo[1][:, :, :])])

        xT = [sc.sb(f"xT{i}", [P, KE, N], F16) for i in range(2)]
        qT = [sc.sb(f"qT{i}", [P, H, N], F16) for i in range(2)]
        kT = [sc.sb(f"kT{i}", [P, H, N], F16) for i in range(2)]
        oT = qT
        v = [sc.sb(f"v{i}", [P, NT, D], F16) for i in range(2)]
        xcur = sc.sb("xcur", [P, NT, E], F32)
        rope_q = sc.sb("rope_q", [P, 2, NT, D], F32)
        rope_k = sc.sb("rope_k", [P, 2, NT, D], F32)
        q_cos = sc.sb("q_cos", [P, 1, E], F32)
        q_sin = sc.sb("q_sin", [P, 1, E], F32)
        q_rot = sc.sb("q_rot", [P, 2, E], F32)
        k_part = sc.sb("k_part", [P, 2, D], F32)
        k_rot = sc.sb("k_rot", [P, NT, D], F32)
        kh_rows = sc.sb("kh_rows", [P, 1, H * D], F32)
        g_abs = sc.sb("g_abs", [2 * H, N], F32)
        g_log = sc.sb("g_log", [2 * H, N], F32)
        g_cum = sc.sb("g_cum", [2 * H, N + 1], F32)
        g_fac = sc.sb("g_fac", [2 * H, N], F32)
        kvh = sc.sb("kvh", [2 * H, N], F32)
        kvh_t = sc.sb("kvh_t", [P, NT, 2 * H], F32)
        prob = sc.sb("prob", [P, NPB, NT, N], F32)
        sums = sc.sb("sums", [P, NPB, NT], F32)
        inv = sc.sb("inv", [P, NPB, NT], F32)
        negmax = sc.sb("negmax", [P, NPB, NT], F32)
        pT = [sc.sb(f"pT{i}", [P, 2, NT, N], F16) for i in range(2)]

        NG = 8 + 8 + H
        G_Q, G_K, G_P = 0, 8, 16
        s = Names()
        x_counters(sc, s)
        s.t_ready = sc.counter("t_ready", NG)
        s.t_hi = sc.counter("t_hi", NG)
        s.t_lo = sc.counter("t_lo", NG)
        s.pr_ready = sc.counter("pr_ready", 2 + 8)
        s.pr_free = sc.counter("pr_free", 2 + 8)
        s.v_hi = sc.counter("v_hi", NT)
        s.gates_ready = sc.counter("gates_ready", 1)
        s.g_ln = sc.counter("g_ln", 3)
        s.g_sum = sc.counter("g_sum", 1)
        s.g_exp = sc.counter("g_exp", 1)
        s.kvh_ready = sc.counter("kvh_ready", 1)
        s.kvh_turned = sc.counter("kvh_turned", 1)
        s.kvh_t_ready = sc.counter("kvh_t_ready", 1)
        s.k_rot_ready = sc.counter("k_rot_ready", NT)
        s.kh_ready = sc.counter("kh_ready", NT)
        s.q_parts = sc.counter("q_parts", 8)
        s.q_ready = sc.counter("q_ready", 8)
        s.s_ready = sc.counter("s_ready", H)
        s.m_ready = sc.counter("m_ready", H)
        s.e_ready = sc.counter("e_ready", H)
        s.i_ready = sc.counter("i_ready", H)
        s.p_ready = sc.counter("p_ready", H)
        s.o_ready = sc.counter("o_ready", H)
        s.o_hi = sc.counter("o_hi", H)
        s.o_lo = sc.counter("o_lo", H)
        s.y_ready = sc.counter("y_ready", NT)
        s.chain = sc.counter("chain", NT * 1 + 2 + NT * LN_STEPS)
        ln_counters(sc, s)
        consts = sc.sem("consts")
        SB, Y = G.psS, G.psP

        sc.start_counters()
        with nc.Block() as block:
            @block.sync
            def _(sp):
                sp.dma_start(rope_q[:, :, :, :], W["rope_q"].rearrange("a (n p) d -> p a n d", p=P)).then_inc(consts, 16)
                sp.dma_start(rope_k[:, :, :, :], W["rope_k"].rearrange("a (n p) d -> p a n d", p=P)).then_inc(consts, 16)

            @block.gpsimd
            def _(pool):
                fetch_x(pool, 0, s, G, xcur)
                with pool.Fori(0, B) as b:
                    for j in range(8):
                        pool.wait_ge(*s.q_parts.count(b, j + 1))
                        if j >= 2:
                            pool.wait_ge(*s.t_ready.count(b, G_Q + j - 1))
                        pool.tensor_tensor(q_rot[:, j % 2, :], q_cos[:, 0, :], q_sin[:, 0, :], ALU.add)\
                            .then_inc(s.q_ready.handle, 1)
                    for n in range(NT):
                        pool.wait_ge(*s.kvh_t_ready.count(b, 1))
                        pool.wait_ge(*s.k_rot_ready.count(b, n + 1))
                        if n:
                            pool.wait_ge(*s.t_ready.count(b, G_K + 4))
                        pool.tensor_tensor(
                            kh_rows[:, 0, :].rearrange("p (h d) -> p h d", h=H),
                            k_rot[:, n:n + 1, :].broadcast_to([P, H, D]),
                            kvh_t[:, n, 0:H].rearrange("p (h a) -> p h a", a=1).broadcast_to([P, H, D]),
                            ALU.mult).then_inc(s.kh_ready.handle, 1)
                    fetch_x(pool, b + 1, s, G, xcur)
                    for h in range(H):
                        pool.wait_ge(*s.i_ready.count(b, h + 1))
                        pool.tensor_tensor(prob[:, h % NPB, 0, 0:P], prob[:, h % NPB, 0, 0:P],
                                           inv[:, h % NPB, 0:1].broadcast_to([P, P]), ALU.mult)
                        pool.tensor_tensor(prob[:, h % NPB, 1, :], prob[:, h % NPB, 1, :],
                                           inv[:, h % NPB, 1:2].broadcast_to([P, N]), ALU.mult)\
                            .then_inc(s.p_ready.handle, 1)
                    for n in range(NT):
                        rstd_on_pool(pool, s, b, n, G)

            @block.tensor
            def _(pe):
                def turn(b, g, blocks):
                    pe.wait_ge(*s.t_lo.count(b, g - 1))
                    for out, src in blocks:
                        last = pe.transpose(out, src, G.ident[:, :])
                    last.then_inc(s.t_ready.handle, 1)

                turn_x(pe, 0, s, G, xcur, G.psS)
                with pe.Fori(0, B) as b:
                    pe.wait_ge(*s.x_lo.count(b, NT))
                    pe.wait_ge(*s.x_done.count(b, 0))
                    for n in range(NT):
                        for k in range(KE):
                            last = three(pe, G.psP[n][:, 0:2 * D], xT[0][:, k, n * P:(n + 1) * P],
                                         xT[1][:, k, n * P:(n + 1) * P], wkv[0][:, k, :], wkv[1][:, k, :],
                                         k == 0, k == KE - 1)
                        last.then_inc(s.pr_ready.handle, 1)
                    for i in range(2):
                        for k in range(KE):
                            last = three(pe, G.psO[0][0:2 * H, i * N:(i + 1) * N],
                                         wgh[0][:, k, i * 2 * H:(i + 1) * 2 * H], wgh[1][:, k, i * 2 * H:(i + 1) * 2 * H],
                                         xT[0][:, k, :], xT[1][:, k, :], k == 0, k == KE - 1)
                    last.then_inc(s.gates_ready.handle, 1)

                    def turn_q(j):
                        pe.wait_ge(*s.q_ready.count(b, j + 1))
                        turn(b, G_Q + j, [(G.psT[j % 2][:, i * P:(i + 1) * P], q_rot[:, j % 2, i * P:(i + 1) * P])
                                          for i in range(HC)])

                    for j in range(8):
                        n, c = divmod(j, QC)
                        pe.wait_ge(*s.pr_free.count(b, j + 1))
                        if j == 4:
                            pe.wait_ge(*s.kvh_ready.count(b, 1))
                        for k in range(KE):
                            last = three(pe, G.psP[j % 2][:, :], xT[0][:, k, n * P:(n + 1) * P],
                                         xT[1][:, k, n * P:(n + 1) * P], wq[0][:, k, c * E:(c + 1) * E],
                                         wq[1][:, k, c * E:(c + 1) * E], k == 0, k == KE - 1)
                        last.then_inc(s.pr_ready.handle, 1)
                        if j == 4:
                            for n2 in range(NT):
                                last = pe.transpose(G.psO[1][:, n2 * 2 * H:(n2 + 1) * 2 * H],
                                                    kvh[:, n2 * P:(n2 + 1) * P], G.ident[0:2 * H, 0:2 * H])
                            last.then_inc(s.kvh_turned.handle, 1)
                        if j >= 2:
                            turn_q(j - 2)
                    turn_q(6)
                    turn_q(7)
                    for n in range(NT):
                        pe.wait_ge(*s.kh_ready.count(b, n + 1))
                        for c in range(QC):
                            g = G_K + n * QC + c
                            turn(b, g, [(G.psT[g % 2][:, i * P:(i + 1) * P],
                                         kh_rows[:, 0, (c * HC + i) * P:(c * HC + i + 1) * P]) for i in range(HC)])

                    def scores(h):
                        if h >= NS:
                            pe.wait_ge(*s.e_ready.count(b, h - NS + 1))
                        S = SB[h % NS]
                        for n in range(NT):
                            w = (n + 1) * P
                            out = S[:, n * N:n * N + w]
                            three(pe, out, qT[0][:, h, n * P:(n + 1) * P], qT[1][:, h, n * P:(n + 1) * P],
                                  kT[0][:, h, 0:w], kT[1][:, h, 0:w], True, False)
                            last = pe.matmul(S[:, n * N + w - P:n * N + w], G.ident_b[:, :], G.causal[:, :],
                                             start=False, stop=True, skip_group_check=True)
                        last.then_inc(s.s_ready.handle, 1)

                    def turn_p(h):
                        g = G_P + h
                        T = G.psT[g % 2]
                        pe.wait_ge(*s.p_ready.count(b, h + 1))
                        pr = prob[:, h % NPB, :, :]
                        turn(b, g, [(T[:, 0:P], pr[:, 0, 0:P]), (T[:, P:2 * P], pr[:, 1, 0:P]),
                                    (T[:, 3 * P:4 * P], pr[:, 1, P:2 * P])])

                    def pv(h):
                        if h >= 2:
                            pe.wait_ge(*s.o_lo.count(b, h - 1))
                        pe.wait_ge(*s.t_lo.count(b, G_P + h + 1))
                        r = h % 2
                        for m in range(NT):
                            cols = slice(m * P, N)
                            last = three(pe, G.psO[r][:, cols], v[0][:, m, :], v[1][:, m, :],
                                         pT[0][:, r, m, cols], pT[1][:, r, m, cols], m == 0, m == NT - 1)
                        last.then_inc(s.o_ready.handle, 1)

                    def project(h):
                        pe.wait_ge(*s.o_lo.count(b, h + 1))
                        for n in range(NT):
                            last = three(pe, Y[n][:, :], oT[0][:, h, n * P:(n + 1) * P],
                                         oT[1][:, h, n * P:(n + 1) * P], wo[0][:, h, :], wo[1][:, h, :],
                                         h == 0, h == H - 1)
                            if h == H - 1:
                                last.then_inc(s.y_ready.handle, 1)

                    pe.wait_ge(*s.t_lo.count(b, G_P))
                    for i in range(H + 5):
                        if i < H:
                            scores(i)
                        if 2 <= i < H + 2:
                            turn_p(i - 2)
                        if 3 <= i < H + 3:
                            pv(i - 3)
                        if i == H + 2:
                            pe.wait_ge(*s.e_ready.count(b, H))
                            turn_x(pe, b + 1, s, G, xcur, G.psS)
                        if i >= 5:
                            project(i - 5)

            @block.scalar
            def _(act):
                x_high(act, 0, s, xT, G.psS)
                with act.Fori(0, B) as b:
                    for n in range(NT):
                        act.wait_ge(*s.pr_ready.count(b, n + 1))
                        act.copy(v[0][:, n, :], G.psP[n][:, D:2 * D]).then_inc(s.v_hi.handle, 1)
                    act.wait_ge(*s.gates_ready.count(b, 1))
                    act.activation(g_abs[:, :], G.psO[0][0:2 * H, N:2 * N], ACT.Abs).then_inc(s.g_ln.handle, 1)
                    act.wait_ge(*s.g_ln.count(b, 1))
                    act.activation(g_abs[:, :], g_abs[:, :], ACT.Exp, scale=-1.0).then_inc(s.g_ln.handle, 1)
                    act.wait_ge(*s.g_ln.count(b, 2))
                    act.activation(g_log[:, :], g_abs[:, :], ACT.Ln, bias=1.0).then_inc(s.g_ln.handle, 1)
                    act.wait_ge(*s.g_sum.count(b, 1))
                    act.activation(g_fac[:, :], g_cum[:, 0:N], ACT.Exp).then_inc(s.g_exp.handle, 1)

                    def hi_q(j):
                        n, c = divmod(j, QC)
                        act.wait_ge(*s.t_ready.count(b, G_Q + j + 1))
                        act.copy(qT[0][:, c * HC:(c + 1) * HC, n * P:(n + 1) * P],
                                 G.psT[j % 2][:, :].rearrange("p (k t) -> p k t", k=HC)).then_inc(s.t_hi.handle, 1)

                    for j in range(8):
                        hi_q(j)
                    for j in range(8):
                        n, c = divmod(j, QC)
                        act.wait_ge(*s.t_ready.count(b, G_K + j + 1))
                        act.copy(kT[0][:, c * HC:(c + 1) * HC, n * P:(n + 1) * P],
                                 G.psT[j % 2][:, :].rearrange("p (k t) -> p k t", k=HC)).then_inc(s.t_hi.handle, 1)

                    def expo(h):
                        act.wait_ge(*s.m_ready.count(b, h + 1))
                        if h >= NPB:
                            act.wait_ge(*s.t_ready.count(b, G_P + h - NPB + 1))
                        S, r = SB[h % NS], h % NPB
                        act.activation(prob[:, r, 0, 0:P], S[:, 0:P], ACT.Exp, bias=negmax[:, r, 0:1],
                                       accum_out=sums[:, r, 0:1])
                        act.activation(prob[:, r, 1, :], S[:, N:2 * N], ACT.Exp, bias=negmax[:, r, 1:2],
                                       accum_out=sums[:, r, 1:2]).then_inc(s.e_ready.handle, 1)

                    def hi_p(h):
                        T, r = G.psT[(G_P + h) % 2], h % 2
                        act.wait_ge(*s.t_ready.count(b, G_P + h + 1))
                        if h >= 2:
                            act.wait_ge(*s.o_ready.count(b, h - 1))
                        for m in range(NT):
                            last = act.mul(pT[0][:, r, m, m * P:N], T[:, m * N + m * P:(m + 1) * N],
                                           kvh_t[:, m, H + h:H + h + 1])
                        last.then_inc(s.t_hi.handle, 1)

                    def hi_o(h):
                        act.wait_ge(*s.o_ready.count(b, h + 1))
                        act.copy(oT[0][:, h, :], G.psO[h % 2][:, 0:N]).then_inc(s.o_hi.handle, 1)

                    for i in range(H + 3):
                        if 2 <= i < H + 2:
                            hi_p(i - 2)
                        if i < H:
                            expo(i)
                        if i >= 3:
                            hi_o(i - 3)
                    x_high(act, b + 1, s, xT, G.psS)

            @block.vector
            def _(dve):
                dve.memset(g_cum[:, 0:1], 0.0)
                dve.wait_ge(consts, 32)
                x_low(dve, 0, s, xT, G.psS)
                with dve.Fori(0, B) as b:
                    steps = Steps(dve, s.chain, b)

                    def lo(g, out_lo, out_hi, src):
                        dve.wait_ge(*s.t_hi.count(b, g + 1))
                        dve.tensor_tensor(out_lo, src, out_hi, ALU.subtract).then_inc(s.t_lo.handle, 1)

                    for n in range(NT):
                        dve.wait_ge(*s.v_hi.count(b, n + 1))
                        ps = G.psP[n]
                        if n == 0:
                            dve.wait_ge(*s.kh_ready.count(b, 0))
                        dve.tensor_tensor(v[1][:, n, :], ps[:, D:2 * D], v[0][:, n, :], ALU.subtract)
                        dve.tensor_tensor(k_part[:, 0, :], ps[:, 0:D], rope_k[:, 0, n, :], ALU.mult)
                        dve.tensor_tensor(k_part[:, 1, 0:D // 2], ps[:, D // 2:D], rope_k[:, 1, n, 0:D // 2], ALU.mult)
                        steps.done(dve.tensor_tensor(k_part[:, 1, D // 2:D], ps[:, 0:D // 2],
                                                     rope_k[:, 1, n, D // 2:D], ALU.mult))
                        dve.tensor_tensor(k_rot[:, n, :], k_part[:, 0, :], k_part[:, 1, :], ALU.add)\
                            .then_inc(s.k_rot_ready.handle, 1)
                        dve.wait_ge(*s.k_rot_ready.count(b, n + 1))
                        dve.memset(G.junk[:, :], 0.0).then_inc(s.pr_free.handle, 1)
                    dve.wait_ge(*s.g_ln.count(b, 3))
                    steps.done(dve.scalar_tensor_tensor(g_log[:, :], G.psO[0][0:2 * H, N:2 * N], 0.0, g_log[:, :],
                                                        ALU.min, ALU.subtract))
                    dve.tensor_tensor_scan(g_cum[:, 1:N + 1], G.ones[0:2 * H, :], g_log[:, :], 0.0, ALU.mult, ALU.add)\
                        .then_inc(s.g_sum.handle, 1)
                    dve.wait_ge(*s.g_exp.count(b, 1))
                    steps.done(dve.tensor_tensor(g_fac[:, :], G.psO[0][0:2 * H, 0:N], g_fac[:, :], ALU.mult))
                    dve.tensor_tensor_scan(kvh[:, :], G.ones[0:2 * H, :], g_fac[:, :], 0.0, ALU.mult, ALU.add)\
                        .then_inc(s.kvh_ready.handle, 1)

                    def lo_q(j):
                        n, c = divmod(j, QC)
                        at = (slice(None), slice(c * HC, (c + 1) * HC), slice(n * P, (n + 1) * P))
                        lo(G_Q + j, qT[1][at], qT[0][at], G.psT[j % 2][:, :].rearrange("p (k t) -> p k t", k=HC))

                    for j in range(8):
                        n, c = divmod(j, QC)
                        dve.wait_ge(*s.pr_ready.count(b, 2 + j + 1))
                        dve.wait_ge(*s.q_ready.count(b, j))
                        ps = G.psP[j % 2][:, :].rearrange("p (h d) -> p h d", h=HC)
                        cos = q_cos[:, 0, :].rearrange("p (h d) -> p h d", h=HC)
                        sin = q_sin[:, 0, :].rearrange("p (h d) -> p h d", h=HC)
                        dve.tensor_tensor(cos, ps, rope_q[:, 0, n:n + 1, :].broadcast_to([P, HC, D]), ALU.mult)
                        dve.tensor_tensor(sin[:, :, 0:D // 2], ps[:, :, D // 2:D],
                                          rope_q[:, 1, n:n + 1, 0:D // 2].broadcast_to([P, HC, D // 2]), ALU.mult)
                        dve.tensor_tensor(sin[:, :, D // 2:D], ps[:, :, 0:D // 2],
                                          rope_q[:, 1, n:n + 1, D // 2:D].broadcast_to([P, HC, D // 2]), ALU.mult)\
                            .then_inc(s.q_parts.handle, 1)
                        dve.wait_ge(*s.q_parts.count(b, j + 1))
                        dve.memset(G.junk[:, :], 0.0).then_inc(s.pr_free.handle, 1)
                        if j == 4:
                            dve.wait_ge(*s.kvh_turned.count(b, 1))
                            dve.tensor_copy(kvh_t[:, :, :],
                                            G.psO[1][:, 0:NT * 2 * H].rearrange("p (n h) -> p n h", n=NT))\
                                .then_inc(s.kvh_t_ready.handle, 1)
                        if j >= 2:
                            lo_q(j - 2)
                    lo_q(6)
                    lo_q(7)
                    for j in range(8):
                        n, c = divmod(j, QC)
                        at = (slice(None), slice(c * HC, (c + 1) * HC), slice(n * P, (n + 1) * P))
                        lo(G_K + j, kT[1][at], kT[0][at], G.psT[j % 2][:, :].rearrange("p (k t) -> p k t", k=HC))

                    def rowmax(h):
                        S, r = SB[h % NS], h % NPB
                        dve.wait_ge(*s.s_ready.count(b, h + 1))
                        if h >= NPB:
                            dve.wait_ge(*s.e_ready.count(b, h - NPB + 1))
                        dve.tensor_reduce(negmax[:, r, 0:1], S[:, 0:P], X_AXIS, ALU.max, negate=True)
                        dve.tensor_reduce(negmax[:, r, 1:2], S[:, N:2 * N], X_AXIS, ALU.max, negate=True)\
                            .then_inc(s.m_ready.handle, 1)

                    def invert(h):
                        dve.wait_ge(*s.e_ready.count(b, h + 1))
                        if h >= NPB:
                            dve.wait_ge(*s.p_ready.count(b, h - NPB + 1))
                        dve.reciprocal(inv[:, h % NPB, :], sums[:, h % NPB, :]).then_inc(s.i_ready.handle, 1)

                    def lo_p(h):
                        T, r = G.psT[(G_P + h) % 2], h % 2
                        dve.wait_ge(*s.t_hi.count(b, G_P + h + 1))
                        for m in range(NT):
                            last = dve.scalar_tensor_tensor(pT[1][:, r, m, m * P:N], T[:, m * N + m * P:(m + 1) * N],
                                                            kvh_t[:, m, H + h:H + h + 1], pT[0][:, r, m, m * P:N],
                                                            ALU.mult, ALU.subtract)
                        last.then_inc(s.t_lo.handle, 1)

                    def lo_o(h):
                        dve.wait_ge(*s.o_hi.count(b, h + 1))
                        dve.tensor_tensor(oT[1][:, h, :], G.psO[h % 2][:, 0:N], oT[0][:, h, :], ALU.subtract)\
                            .then_inc(s.o_lo.handle, 1)

                    for i in range(H + 3):
                        if i < H:
                            rowmax(i)
                        if 1 <= i <= H:
                            invert(i - 1)
                        if 2 <= i < H + 2:
                            lo_p(i - 2)
                        if i >= 3:
                            lo_o(i - 3)
                    x_low(dve, b + 1, s, xT, G.psS)
                    for n in range(NT):
                        add_and_norm(dve, s, b, n, Y[n][:, :], s.y_ready, G, steps)
                    steps.check()


def xattn0_tables(nc, sc, G, W, rope):
    TWO_PI_HI, TWO_PI_LO = 6.28125, 2 * np.pi - 6.28125
    ROUND = float(1.5 * 2 ** 23)
    pos = sc.sb("pos", [P, B * NT, 2], F32)
    ang = sc.sb("ang", [P, 2, B * NT, 8], F32)
    turns = sc.sb("turns", [P, 2, B * NT, 8], F32)
    trig = sc.sb("trig", [P, 2, B * NT, 8], F32)
    landed, step, sin_done = sc.sem("pos_landed"), sc.sem("tab_step"), sc.sem("sin_done")
    with nc.Block() as block:
        @block.sync
        def _(sp):
            sp.dma_start(pos[:, :, :], W["fside"].rearrange("b (n p) a -> p (b n) a", p=P)).then_inc(landed, 16)

        @block.vector
        def _(dve):
            count = 0
            dve.wait_ge(landed, 16)
            for j in range(4):
                out = ang[:, 0, :, :].rearrange("p t (a j) -> p t a j", a=2)[:, :, :, j]
                last = dve.tensor_scalar(out, pos[:, :, :], float(np.float32(10000.0) ** np.float32(-j / 4)), None,
                                         ALU.mult)
            def then(ins):
                nonlocal count
                count += 1
                ins.then_inc(step, 1)
                dve.wait_ge(step, count)
            then(last)
            then(dve.tensor_scalar(ang[:, 1, :, :], ang[:, 0, :, :], float(np.pi / 2), None, ALU.add))
            then(dve.tensor_scalar(turns[:, :, :, :], ang[:, :, :, :], float(1 / (2 * np.pi)), ROUND, ALU.mult, ALU.add))
            then(dve.tensor_scalar(turns[:, :, :, :], turns[:, :, :, :], ROUND, None, ALU.subtract))
            then(dve.scalar_tensor_tensor(ang[:, :, :, :].rearrange("p a t j -> p (a t j)"),
                                          turns[:, :, :, :].rearrange("p a t j -> p (a t j)"), -TWO_PI_HI,
                                          ang[:, :, :, :].rearrange("p a t j -> p (a t j)"), ALU.mult, ALU.add))
            then(dve.scalar_tensor_tensor(ang[:, :, :, :].rearrange("p a t j -> p (a t j)"),
                                          turns[:, :, :, :].rearrange("p a t j -> p (a t j)"), -TWO_PI_LO,
                                          ang[:, :, :, :].rearrange("p a t j -> p (a t j)"), ALU.mult, ALU.add))
            then(dve.tensor_scalar(ang[:, :, :, :], ang[:, :, :, :], float(np.float32(3.1415925)),
                                   float(np.float32(-3.1415925)), ALU.min, ALU.max))
            dve.wait_ge(sin_done, 1)
            for which, scale in ((0, 0.25), (1, 1.0)):
                t = rope[:, which, :, :, :].rearrange("p a t (j e) -> p a t j e", e=2)
                for e in range(2):
                    dve.tensor_scalar(t[:, 0, :, :, e], trig[:, 1, :, :], scale, None, ALU.mult)
                    dve.tensor_scalar(t[:, 1, :, :, e], trig[:, 0, :, :], scale * (2 * e - 1), None, ALU.mult)

        @block.scalar
        def _(act):
            act.wait_ge(step, 7)
            act.activation(trig[:, :, :, :], ang[:, :, :, :], ACT.Sin).then_inc(sin_done, 1)


def small_attention(nc, G, W, tag, H, D, KVH, causal, from_ctx, wq_dram, wkv_dram, wo_dram, bias_dram):
    GD = 4 * D
    HB = P // GD
    QB, KB = H // HB, KVH // HB
    KW = KVH * D
    NS, NPB = 4, 3
    SCALE = float(1.0 / np.sqrt(D))
    KSRC = KC if from_ctx else KE
    with Scope(nc, tag) as sc:
        wq = [sc.sb(f"wq{i}", [P, KE, E], F16) for i in range(2)]
        wkv = [sc.sb(f"wkv{i}", [P, KSRC, 2 * KW], F16) for i in range(2)]
        wo = [sc.sb(f"wo{i}", [P, KE, E], F16) for i in range(2)]
        bias = [sc.sb(f"bias{i}", [1, 1, E], F16) for i in range(2)]
        pieces = [(kt_view(wq_dram), wq[0][:, :, :], wq[1][:, :, :]),
                  (kt_view(wkv_dram), wkv[0][:, :, :], wkv[1][:, :, :]),
                  (kt_view(wo_dram), wo[0][:, :, :], wo[1][:, :, :]),
                  (bias_dram.rearrange("(a k n) -> a k n", a=1, k=1), bias[0][:, :, :], bias[1][:, :, :])]
        if from_ctx:
            cT = [sc.sb(f"cT{i}", [P, KC, B * N], F16) for i in range(2)]
            pieces.append((kt_view(W["ctxT"]), cT[0][:, :, :], cT[1][:, :, :]))
            rope = sc.sb("rope", [P, 2, 2, B * NT, D], F32)
        load_and_split(nc, sc, G, pieces)
        if from_ctx:
            xattn0_tables(nc, sc, G, W, rope)

        xT = [sc.sb(f"xT{i}", [P, KE, N], F16) for i in range(2)]
        oT = [sc.sb(f"oT{i}", [P, KE, N], F16) for i in range(2)]
        v = [sc.sb(f"v{i}", [P, NT, KW], F16) for i in range(2)]
        qS = sc.sb("qS", [P, QB, N], F16)
        kS = sc.sb("kS", [P, KB, N], F16)
        q_stack = sc.sb("q_stack", [P, NT, H, 4, D], F16)
        k_stack = sc.sb("k_stack", [P, NT, KVH, 4, D], F16)
        xcur = sc.sb("xcur", [P, NT, E], F32)
        c_part = sc.sb("c_part", [P, E], F32)
        s_part = sc.sb("s_part", [P, E], F32)
        rot = sc.sb("rot", [P, 2, E], F32)
        prob = sc.sb("prob", [P, NPB, NT, N], F32)
        sums = sc.sb("sums", [P, NT, H], F32)
        inv = sc.sb("inv", [P, NT, H], F32)
        negmax = sc.sb("negmax", [P, NPB, NT], F32)
        o_rows = sc.sb("o_rows", [P, NT, E], F32)
        pT = [sc.sb(f"pT{i}", [P, 2, NT, N], F16) for i in range(2)]

        projections = [("q", 0), ("q", 1)] + ([("k", 0), ("v", 0), ("k", 1), ("v", 1)] if from_ctx
                                              else [("kv", 0), ("kv", 1)])
        NP_ = len(projections)
        stacks = [("q", 0), ("q", 1), ("k", 0), ("k", 1)]
        def blocks_of(kind):
            return QB if kind == "q" else KB
        stack_groups = []
        for i, (kind, n) in enumerate(stacks):
            nb = blocks_of(kind)
            for b0 in range(0, nb, 8):
                stack_groups.append((i, kind, n, b0, min(8, nb - b0)))
        G_S = 2
        G_P = G_S + len(stack_groups)
        G_O = G_P + H
        NG = G_O + NT
        assert NG % 2 == 0
        HI_P, HI_O, NHI = 2, 2 + H, 2 + H + NT
        NV = NT
        s = Names()
        s.xcur_ready = sc.counter("xcur_ready", 1)
        s.t_ready = sc.counter("t_ready", NG)
        s.t_hi = sc.counter("t_hi", NHI)
        s.t_lo = sc.counter("t_lo", NG)
        s.pr_ready = sc.counter("pr_ready", NP_)
        s.pr_hi = sc.counter("pr_hi", NT if from_ctx else NP_)
        s.pr_done = sc.counter("pr_done", NP_)
        s.rot_ready = sc.counter("rot_ready", 4)
        s.rot_hi = sc.counter("rot_hi", 4)
        s.stack_ready = sc.counter("stack_ready", 4)
        s.s_ready = sc.counter("s_ready", H)
        s.m_ready = sc.counter("m_ready", H)
        s.e_ready = sc.counter("e_ready", H)
        s.pv_done = sc.counter("pv_done", H)
        s.o_ready = sc.counter("o_ready", NT)
        s.y_ready = sc.counter("y_ready", NT)
        s.chain = sc.counter("chain", 1 + NT * LN_STEPS)
        ln_counters(sc, s)
        SB = [G.psS[0], G.psS[1], G.psP[0], G.psP[1]]
        TH = [t[:, :].bitcast(F16) for t in G.psT]

        def tile_at(b, n):
            return bass.ds(b * N + n * P, P)

        sc.start_counters()
        with nc.Block() as block:
            @block.gpsimd
            def _(pool):
                pool.memset(q_stack[:, :, :, 3, :], 0.0)
                pool.memset(k_stack[:, :, :, 3, :], 0.0)
                with pool.Fori(0, B) as b:
                    pool.wait_ge(*s.t_ready.count(b, 0))
                    pool.tensor_copy(xcur[:, :, :], G.x[:, bass.ds(b * NT, NT), :]).then_inc(s.xcur_ready.handle, 1)
                    if from_ctx:
                        def stack_lo(i):
                            kind, n = stacks[i]
                            st, at = (q_stack, 1) if kind == "q" else (k_stack, 2)
                            pool.wait_ge(*s.rot_hi.count(b, i + 1))
                            pool.tensor_tensor(st[:, n, :, at, :], rot[:, i % 2, :].rearrange("p (h d) -> p h d", d=D),
                                               st[:, n, :, 0, :], ALU.subtract).then_inc(s.stack_ready.handle, 1)
                        of_proj = {"q": [0, 1], "k": [2, 4]}
                        for i, (kind, n) in enumerate(stacks):
                            pool.wait_ge(*s.pr_done.count(b, of_proj[kind][n] + 1))
                            pool.tensor_tensor(rot[:, i % 2, :], c_part[:, :], s_part[:, :], ALU.add)\
                                .then_inc(s.rot_ready.handle, 1)
                            stack_lo(i)
                    for n in range(NT):
                        rstd_on_pool(pool, s, b, n, G)

            @block.tensor
            def _(pe):
                def turn(b, g, blocks, ident):
                    if g >= 2:
                        pe.wait_ge(*s.t_lo.count(b, g - 1))
                    for out, src in blocks:
                        last = pe.transpose(out, src, ident[:, :])
                    last.then_inc(s.t_ready.handle, 1)

                with pe.Fori(0, B) as b:
                    pe.wait_ge(*s.xcur_ready.count(b, 1))
                    pe.wait_ge(*s.t_lo.count(b, 0))
                    for n in range(NT):
                        turn(b, n, [(G.psT[n][:, k * P:(k + 1) * P], xcur[:, n, k * P:(k + 1) * P])
                                    for k in range(KE)], G.ident)
                    pe.wait_ge(*s.t_lo.count(b, 2))
                    for i, (kind, n) in enumerate(projections):
                        if i >= 2:
                            pe.wait_ge(*s.pr_done.count(b, i - 1))
                        a = xT
                        at = slice(n * P, (n + 1) * P)
                        if kind == "q":
                            w, cols, K = wq, slice(0, E), KE
                        else:
                            w, K = wkv, KSRC
                            cols = {"k": slice(0, KW), "v": slice(KW, 2 * KW), "kv": slice(0, 2 * KW)}[kind]
                            if from_ctx:
                                a, at = cT, tile_at(b, n)
                        width = cols.stop - cols.start
                        for k in range(K):
                            last = three(pe, G.psP[i % 2][:, 0:width], a[0][:, k, at], a[1][:, k, at],
                                         w[0][:, k, cols], w[1][:, k, cols], k == 0, k == K - 1)
                        last.then_inc(s.pr_ready.handle, 1)
                    for g, (i, kind, n, b0, nb) in enumerate(stack_groups):
                        st = q_stack if kind == "q" else k_stack
                        flat = st[:, n, :, :, :].rearrange("p h a d -> p (h a d)")
                        pe.wait_ge(*(s.stack_ready if from_ctx else s.pr_done).count(b, i + 1))
                        turn(b, G_S + g, [(TH[(G_S + g) % 2][:, j * P:(j + 1) * P],
                                           flat[:, (b0 + j) * P:(b0 + j + 1) * P]) for j in range(nb)], G.ident_h)

                    def scores(h):
                        if h >= NS:
                            pe.wait_ge(*s.e_ready.count(b, h - NS + 1))
                        S = SB[h % NS]
                        hk = h * KVH // H
                        base, kbase = (h % HB) * GD, (hk % HB) * GD
                        assert base == kbase
                        for n in range(NT):
                            w = (n + 1) * P if causal else N
                            last = pe.matmul(S[:, n * N:n * N + w], qS[base:base + GD, h // HB, n * P:(n + 1) * P],
                                             kS[base:base + GD, hk // HB, 0:w], start=True, stop=not causal,
                                             skip_group_check=True)
                            if causal:
                                last = pe.matmul(S[:, n * N + w - P:n * N + w], G.ident_b[:, :], G.causal[:, :],
                                                 start=False, stop=True, skip_group_check=True)
                        last.then_inc(s.s_ready.handle, 1)

                    def turn_p(h):
                        T = G.psT[(G_P + h) % 2]
                        pe.wait_ge(*s.e_ready.count(b, h + 1))
                        pr = prob[:, h % NPB, :, :]
                        turn(b, G_P + h, [(T[:, m * N + n * P:m * N + (n + 1) * P], pr[:, n, m * P:(m + 1) * P])
                                          for m in range(NT) for n in range(m if causal else 0, NT)], G.ident)

                    def pv(h):
                        pe.wait_ge(*s.t_lo.count(b, G_P + h + 1))
                        hk, r = h * KVH // H, h % 2
                        for n in range(NT):
                            ms = range(n + 1 if causal else NT)
                            for m in ms:
                                last = three(pe, G.psO[n][:, h * D:(h + 1) * D], pT[0][:, r, m, n * P:(n + 1) * P],
                                             pT[1][:, r, m, n * P:(n + 1) * P], v[0][:, m, hk * D:(hk + 1) * D],
                                             v[1][:, m, hk * D:(hk + 1) * D], m == 0, m == ms[-1])
                        last.then_inc(s.pv_done.handle, 1)

                    pe.wait_ge(*s.t_lo.count(b, G_P))
                    pe.wait_ge(*s.pr_done.count(b, NP_))
                    for i in range(H + 3):
                        if i < H:
                            scores(i)
                        if 2 <= i < H + 2:
                            turn_p(i - 2)
                        if i >= 3:
                            pv(i - 3)
                    for n in range(NT):
                        pe.wait_ge(*s.o_ready.count(b, n + 1))
                        turn(b, G_O + n, [(G.psT[(G_O + n) % 2][:, k * P:(k + 1) * P], o_rows[:, n, k * P:(k + 1) * P])
                                          for k in range(KE)], G.ident)
                    pe.wait_ge(*s.t_lo.count(b, NG))
                    for n in range(NT):
                        for k in range(KE):
                            three(pe, G.psS[n][:, :], oT[0][:, k, n * P:(n + 1) * P],
                                  oT[1][:, k, n * P:(n + 1) * P], wo[0][:, k, :], wo[1][:, k, :], k == 0, False)
                        pe.matmul(G.psS[n][:, :], G.ones_h[0:1, :], bias[0][0:1, 0, :], start=False, stop=False,
                                  skip_group_check=True)
                        pe.matmul(G.psS[n][:, :], G.ones_h[0:1, :], bias[1][0:1, 0, :], start=False, stop=True,
                                  skip_group_check=True).then_inc(s.y_ready.handle, 1)

            @block.scalar
            def _(act):
                with act.Fori(0, B) as b:
                    def hi_x(i, g, out):
                        act.wait_ge(*s.t_ready.count(b, g + 1))
                        act.copy(out, G.psT[g % 2][:, :].rearrange("p (k t) -> p k t", k=KE))\
                            .then_inc(s.t_hi.handle, 1)

                    for n in range(NT):
                        hi_x(n, n, xT[0][:, :, n * P:(n + 1) * P])

                    def stack_hi(kind, n, src, scale):
                        heads = H if kind == "q" else KVH
                        out = q_stack[:, n, :, 0:3:2, :] if kind == "q" else k_stack[:, n, :, 0:2, :]
                        view = src.rearrange("p (h a d) -> p h a d", a=1, d=D)
                        for a in range(2):
                            last = act.mul(out[:, :, a, :], view[:, :, 0, :], scale)
                        return last

                    st = 0
                    for i, (kind, n) in enumerate(projections):
                        if from_ctx and kind in "qk":
                            act.wait_ge(*s.rot_ready.count(b, st + 1))
                            stack_hi(kind, n, rot[:, st % 2, :], 1.0).then_inc(s.rot_hi.handle, 1)
                            st += 1
                            continue
                        act.wait_ge(*s.pr_ready.count(b, i + 1))
                        ps = G.psP[i % 2]
                        if kind == "q":
                            last = stack_hi("q", n, ps[:, :], SCALE)
                        elif kind == "v":
                            last = act.copy(v[0][:, n, :], ps[:, 0:KW])
                        else:
                            stack_hi("k", n, ps[:, 0:KW], 1.0)
                            last = act.copy(v[0][:, n, :], ps[:, KW:2 * KW])
                        last.then_inc(s.pr_hi.handle, 1)

                    def expo(h):
                        act.wait_ge(*s.m_ready.count(b, h + 1))
                        if h >= NPB:
                            act.wait_ge(*s.t_ready.count(b, G_P + h - NPB + 1))
                        S, r = SB[h % NS], h % NPB
                        for n in range(NT):
                            w = (n + 1) * P if causal else N
                            last = act.activation(prob[:, r, n, 0:w], S[:, n * N:n * N + w], ACT.Exp,
                                                  bias=negmax[:, r, n:n + 1], accum_out=sums[:, n, h:h + 1])
                        last.then_inc(s.e_ready.handle, 1)

                    def hi_p(h):
                        T, r = G.psT[(G_P + h) % 2], h % 2
                        act.wait_ge(*s.t_ready.count(b, G_P + h + 1))
                        if h >= 2:
                            act.wait_ge(*s.pv_done.count(b, h - 1))
                        if causal:
                            act.copy(pT[0][:, r, 0, :], T[:, 0:N])
                            last = act.copy(pT[0][:, r, 1, P:N], T[:, N + P:2 * N])
                        else:
                            last = act.copy(pT[0][:, r, :, :], T[:, :].rearrange("p (m n) -> p m n", m=NT))
                        last.then_inc(s.t_hi.handle, 1)

                    for i in range(H + 2):
                        if i >= 2:
                            hi_p(i - 2)
                        if i < H:
                            expo(i)
                    for n in range(NT):
                        hi_x(HI_O + n, G_O + n, oT[0][:, :, n * P:(n + 1) * P])

            @block.vector
            def _(dve):
                with dve.Fori(0, B) as b:
                    steps = Steps(dve, s.chain, b)

                    def lo(g, hi_index, out_lo, out_hi, src):
                        dve.wait_ge(*s.t_hi.count(b, hi_index + 1))
                        dve.tensor_tensor(out_lo, src, out_hi, ALU.subtract).then_inc(s.t_lo.handle, 1)

                    def lo_x(g, hi_index, out, n):
                        at = slice(n * P, (n + 1) * P)
                        lo(g, hi_index, out[1][:, :, at], out[0][:, :, at],
                           G.psT[g % 2][:, :].rearrange("p (k t) -> p k t", k=KE))

                    for n in range(NT):
                        lo_x(n, n, xT, n)
                    st = n_hi = 0
                    for i, (kind, n) in enumerate(projections):
                        ps = G.psP[i % 2]
                        if from_ctx and kind in "qk":
                            which = 0 if kind == "q" else 1
                            dve.wait_ge(*s.pr_ready.count(b, i + 1))
                            dve.wait_ge(*s.rot_ready.count(b, st))
                            tab = rope[:, which, :, bass.ds(b * NT + n, 1), :]
                            dve.tensor_tensor(c_part[:, :].rearrange("p (h d) -> p h d", d=D),
                                              ps[:, :].rearrange("p (h d) -> p h d", d=D),
                                              tab[:, 0, :, :].broadcast_to([P, H, D]), ALU.mult)
                            pairs = ps[:, :].rearrange("p (h j e) -> p h j e", j=D // 2, e=2)
                            out = s_part[:, :].rearrange("p (h j e) -> p h j e", j=D // 2, e=2)
                            sin = tab[:, 1, :, :].rearrange("p a (j e) -> p a j e", e=2)
                            for e in range(2):
                                last = dve.tensor_tensor(out[:, :, :, e], pairs[:, :, :, 1 - e],
                                                         sin[:, :, :, e].broadcast_to([P, H, D // 2]), ALU.mult)
                            last.then_inc(s.pr_done.handle, 1)
                            st += 1
                            continue
                        n_hi += 1
                        dve.wait_ge(*s.pr_hi.count(b, n_hi))
                        view = ps[:, :].rearrange("p (h d) -> p h d", d=D)
                        if kind == "q":
                            dve.scalar_tensor_tensor(q_stack[:, n, :, 1, :], view, SCALE, q_stack[:, n, :, 0, :],
                                                     ALU.mult, ALU.subtract).then_inc(s.pr_done.handle, 1)
                        elif kind == "v":
                            dve.tensor_tensor(v[1][:, n, :], ps[:, 0:KW], v[0][:, n, :], ALU.subtract)\
                                .then_inc(s.pr_done.handle, 1)
                        else:
                            dve.tensor_tensor(v[1][:, n, :], ps[:, KW:2 * KW], v[0][:, n, :], ALU.subtract)
                            dve.tensor_tensor(k_stack[:, n, :, 2, :], view[:, 0:KVH, :], k_stack[:, n, :, 0, :],
                                              ALU.subtract).then_inc(s.pr_done.handle, 1)
                    for g, (i, kind, n, b0, nb) in enumerate(stack_groups):
                        out = qS if kind == "q" else kS
                        dve.wait_ge(*s.t_ready.count(b, G_S + g + 1))
                        dve.tensor_copy(out[:, b0:b0 + nb, n * P:(n + 1) * P],
                                        TH[(G_S + g) % 2][:, 0:nb * P].rearrange("p (k t) -> p k t", k=nb))\
                            .then_inc(s.t_lo.handle, 1)

                    def rowmax(h):
                        S, r = SB[h % NS], h % NPB
                        dve.wait_ge(*s.s_ready.count(b, h + 1))
                        if h >= NPB:
                            dve.wait_ge(*s.e_ready.count(b, h - NPB + 1))
                        if causal:
                            dve.tensor_reduce(negmax[:, r, 0:1], S[:, 0:P], X_AXIS, ALU.max, negate=True)
                            last = dve.tensor_reduce(negmax[:, r, 1:2], S[:, N:2 * N], X_AXIS, ALU.max, negate=True)
                        else:
                            last = dve.tensor_reduce(negmax[:, r, :], S[:, :].rearrange("p (n m) -> p n m", n=NT),
                                                     X_AXIS, ALU.max, negate=True)
                        last.then_inc(s.m_ready.handle, 1)

                    def lo_p(h):
                        T, r = G.psT[(G_P + h) % 2], h % 2
                        if causal:
                            dve.wait_ge(*s.t_hi.count(b, HI_P + h + 1))
                            dve.tensor_tensor(pT[1][:, r, 0, :], T[:, 0:N], pT[0][:, r, 0, :], ALU.subtract)
                            dve.tensor_tensor(pT[1][:, r, 1, P:N], T[:, N + P:2 * N], pT[0][:, r, 1, P:N],
                                              ALU.subtract).then_inc(s.t_lo.handle, 1)
                        else:
                            lo(G_P + h, HI_P + h, pT[1][:, r, :, :], pT[0][:, r, :, :],
                               T[:, :].rearrange("p (m n) -> p m n", m=NT))

                    for i in range(H + 2):
                        if i < H:
                            rowmax(i)
                        if i >= 2:
                            lo_p(i - 2)
                    dve.wait_ge(*s.e_ready.count(b, H))
                    steps.done(dve.reciprocal(inv[:, :, :], sums[:, :, :]))
                    dve.wait_ge(*s.pv_done.count(b, H))
                    for n in range(NT):
                        dve.tensor_tensor(o_rows[:, n, :].rearrange("p (h d) -> p h d", d=D),
                                          G.psO[n][:, :].rearrange("p (h d) -> p h d", d=D),
                                          inv[:, n, :].rearrange("p (h a) -> p h a", a=1).broadcast_to([P, H, D]),
                                          ALU.mult).then_inc(s.o_ready.handle, 1)
                    for n in range(NT):
                        lo_x(G_O + n, HI_O + n, oT, n)
                    for n in range(NT):
                        add_and_norm(dve, s, b, n, G.psS[n][:, :], s.y_ready, G, steps)
                    steps.check()


def xattn0(nc, G, W):
    small_attention(nc, G, W, "c0", 32, 16, 32, False, True, W["L0_xattn_Wq"], W["L0_xattn_Wkv"], W["L0_xattn_Wout"],
                    W["L0_xattn_bout"])


def attn1(nc, G, W):
    small_attention(nc, G, W, "a1", 16, 32, 4, True, False, W["L1_attn_Wq"], W["L1_attn_Wkv"], W["L1_attn_Wo"], W["L1_attn_bo"])


def ffn0(nc, G, W):
    HID = 1408
    TH_ = HID // P
    NE, R = 8, 16
    NU = 4
    with Scope(nc, "f0") as sc:
        def pair(name, shape):
            return [sc.sb(f"{name}{i}", shape, F16) for i in range(2)]

        wug = pair("wug", [P, KE, 2 * HID])
        wA = pair("wA", [P, KE, 2 * P])
        wB = pair("wB", [P, 1, 2 * HID])
        wd = pair("wd", [P, TH_, E])
        dA = pair("dA", [P, TH_, P])
        dB = pair("dB", [P, 1, E])
        wr = pair("wr", [P, KE, NE])
        load_and_split(nc, sc, G, [(kt_view(d), w[0][:, :, :], w[1][:, :, :]) for d, w in (
            (W["f0_up_gateT"], wug), (W["f0_A"], wA), (W["f0_B"], wB), (W["f0_downT"], wd), (W["f0_dA"], dA), (W["f0_dB"], dB),
            (W["f0_router"], wr))])

        xT = pair("xT", [P, KE, N])
        xcur = sc.sb("xcur", [P, NT, E], F32)
        expert_of = sc.sb("expert_of", [P, P], F32)
        row_pick = sc.sb("row_pick", [2, 2, P], F16)
        logits = sc.sb("logits", [P, NT, NE], F32)
        top = sc.sb("top", [P, NT, 8], F32)
        top_at = sc.sb("top_at", [P, NT, 8], U32)
        top_f = sc.sb("top_f", [P, NT, 8], F32)
        picked = sc.sb("picked", [P, 2, NT, P], F16)
        mask = sc.sb("mask", [P, 2, N], F16)
        dmask = sc.sb("dmask", [P, N], F16)
        wneg = sc.sb("wneg", [2, 1], F32)
        wexp = sc.sb("wexp", [2, N], F32)
        wsum = sc.sb("wsum", [2, 1], F32)
        winv = sc.sb("winv", [2, 1], F32)
        wts = pair("wts", [2, N])
        c = sc.sb("c", [P, 2, N], F32)
        act_a = sc.sb("act_a", [P, 2, N], F32)
        am = sc.sb("am", [P, 2, 2, N], F32)
        a_part = pair("a_part", [P, 2, 2, N])
        sil = sc.sb("sil", [P, 2, 2, N], F32)
        h = sc.sb("h", [P, 2, 2, N], F32)
        ch = sc.sb("ch", [P, 2, 3, N], F32)
        chs = pair("chs", [P, 2, 3, N])
        zm = sc.sb("zm", [P, 2, N], F32)
        zs = pair("zs", [P, N])

        U = [G.psS[0], G.psS[1], G.psP[1], G.psP[0]]
        Z, Y = G.psO[1], G.psT
        TM = G.psP[0][:, :].bitcast(F16)
        s = Names()
        x_counters(sc, s)
        s.logits_ready = sc.counter("logits_ready", 1)
        s.a_ready = sc.counter("a_ready", 1)
        s.top_ready = sc.counter("top_ready", 1)
        s.top_turned = sc.counter("top_turned", 1)
        s.wneg_ready = sc.counter("wneg_ready", 1)
        s.wexp_ready = sc.counter("wexp_ready", 1)
        s.wts_ready = sc.counter("wts_ready", 1)
        s.c_wide = sc.counter("c_wide", 1)
        s.c_ready = sc.counter("c_ready", 1)
        s.picked_ready = sc.counter("picked_ready", 1)
        s.mask_turned = sc.counter("mask_turned", 1)
        s.mask_ready = sc.counter("mask_ready", 1)
        s.act_a_ready = sc.counter("act_a_ready", 1)
        s.a_split0 = sc.counter("a_split0", 1)
        s.a_split1 = sc.counter("a_split1", 1)
        s.base_ready = sc.counter("base_ready", TH_)
        s.delta_ready = sc.counter("delta_ready", TH_)
        s.sil0 = sc.counter("sil0", TH_)
        s.sil1 = sc.counter("sil1", TH_)
        s.h0 = sc.counter("h0", TH_)
        s.h1 = sc.counter("h1", TH_)
        s.ch_ready = sc.counter("ch_ready", TH_)
        s.ch_hi = sc.counter("ch_hi", TH_)
        s.ch_lo = sc.counter("ch_lo", TH_)
        s.down_done = sc.counter("down_done", TH_)
        s.z_ready = sc.counter("z_ready", 1)
        s.z_parts = sc.counter("z_parts", 1)
        s.y_ready = sc.counter("y_ready", NT)
        s.chain = sc.counter("chain", 1 + 2 * NT + 2 + 3 + 3 + NT * LN_STEPS)
        s.pool_chain = sc.counter("pool_chain", 1 + TH_)
        ln_counters(sc, s)
        consts = sc.sem("consts")
        sc.start_counters()

        with nc.Block() as block:
            @block.sync
            def _(sp):
                sp.dma_start(expert_of[:, :], W["expert_of"]).then_inc(consts, 16)
                sp.dma_start(row_pick[:, :, :], W["row_pick"]).then_inc(consts, 16)

            @block.gpsimd
            def _(pool):
                fetch_x(pool, 0, s, G, xcur)
                with pool.Fori(0, B) as b:
                    steps = Steps(pool, s.pool_chain, b)
                    pool.wait_ge(*s.act_a_ready.count(b, 1))
                    pool.wait_ge(*s.mask_ready.count(b, 1))
                    m = mask[:, 0:1, :].broadcast_to([P, 2, N])
                    pool.tensor_tensor(am[:, 0, :, :], act_a[:, :, :], m, ALU.mult)
                    steps.done(pool.tensor_tensor(a_part[0][:, 0, :, :], act_a[:, :, :], m, ALU.mult))
                    pool.tensor_tensor(a_part[1][:, 0, :, :], am[:, 0, :, :], a_part[0][:, 0, :, :], ALU.subtract)\
                        .then_inc(s.a_split0.handle, 1)
                    fetch_x(pool, b + 1, s, G, xcur)
                    pool.wait_ge(*s.c_ready.count(b, 1))
                    for t in range(TH_):
                        r = t % 2
                        pool.wait_ge(*s.ch_lo.count(b, t - 1))
                        pool.wait_ge(*s.h0.count(b, t + 1))
                        pool.tensor_tensor(ch[:, r, 0, :], h[:, 0, r, :], c[:, 0, :], ALU.mult)
                        pool.wait_ge(*s.h1.count(b, t + 1))
                        steps.done(pool.tensor_tensor(ch[:, r, 1, :], h[:, 1, r, :], c[:, 1, :], ALU.mult))
                        pool.tensor_tensor(ch[:, r, 2, :], ch[:, r, 0, :], ch[:, r, 1, :], ALU.add)\
                            .then_inc(s.ch_ready.handle, 1)
                    steps.check()
                    for n in range(NT):
                        rstd_on_pool(pool, s, b, n, G)

            @block.tensor
            def _(pe):
                turn_x(pe, 0, s, G, xcur, G.psS)
                with pe.Fori(0, B) as b:
                    def base(t):
                        for u in range(2):
                            cols = slice(u * HID + t * P, u * HID + (t + 1) * P)
                            for k in range(KE):
                                three(pe, U[t % NU][:, u * N:(u + 1) * N], wug[0][:, k, cols], wug[1][:, k, cols],
                                      xT[0][:, k, :], xT[1][:, k, :], k == 0 and u == 0, False)

                    def low_rank(t, i):
                        for u in range(2):
                            cols = slice(u * HID + t * P, u * HID + (t + 1) * P)
                            last = three(pe, U[t % NU][:, u * N:(u + 1) * N], wB[0][:, 0, cols], wB[1][:, 0, cols],
                                         a_part[0][:, i, u, :], a_part[1][:, i, u, :], False, True)
                        return last

                    pe.wait_ge(*s.x_lo.count(b, NT))
                    for n in range(NT):
                        at = slice(n * P, (n + 1) * P)
                        for k in range(KE):
                            three(pe, G.psP[0][:, n * NE:(n + 1) * NE], xT[0][:, k, at], xT[1][:, k, at],
                                  wr[0][:, k, :], wr[1][:, k, :], k == 0, False)
                            last = pe.matmul(G.psP[0][:, n * NE:(n + 1) * NE], xT[1][:, k, at], wr[1][:, k, :],
                                             start=False, stop=k == KE - 1, skip_group_check=True)
                    last.then_inc(s.logits_ready.handle, 1)
                    for u in range(2):
                        for k in range(KE):
                            last = three(pe, G.psP[1][:, u * N:(u + 1) * N], wA[0][:, k, u * P:(u + 1) * P],
                                         wA[1][:, k, u * P:(u + 1) * P], xT[0][:, k, :], xT[1][:, k, :],
                                         k == 0, k == KE - 1)
                    last.then_inc(s.a_ready.handle, 1)
                    base(0)
                    pe.wait_ge(*s.top_ready.count(b, 1))
                    pe.matmul(G.psO[1][:, 0:NE], G.ident_h[:, :], G.ident_h[:, 0:NE], start=True, stop=True)
                    for n in range(NT):
                        last = pe.transpose(G.psO[0][0:2, n * P:(n + 1) * P], top[:, n, 0:2], G.ident[:, :])
                    last.then_inc(s.top_turned.handle, 1)
                    base(1)
                    pe.wait_ge(*s.picked_ready.count(b, 1))
                    for j in range(2):
                        for n in range(NT):
                            last = pe.transpose(TM[:, (j * NT + n) * P:(j * NT + n + 1) * P], picked[:, j, n, :],
                                                G.ident_h[:, :])
                    last.then_inc(s.mask_turned.handle, 1)
                    pe.wait_ge(*s.act_a_ready.count(b, 1))
                    base(2)
                    pe.wait_ge(*s.mask_ready.count(b, 1))
                    base(3)
                    pe.wait_ge(*s.a_split0.count(b, 1))
                    for i in range(TH_ + 3):
                        if i < TH_:
                            low_rank(i, 0).then_inc(s.base_ready.handle, 1)
                        if i == 1:
                            pe.wait_ge(*s.a_split1.count(b, 1))
                        if 1 <= i <= TH_:
                            pe.wait_ge(*s.h0.count(b, i))
                            low_rank(i - 1, 1).then_inc(s.delta_ready.handle, 1)
                        if i == 1:
                            pe.wait_ge(*s.wts_ready.count(b, 1))
                            pe.matmul(G.psO[1][:, 0:NE], G.ident_h[:, :], G.ident_h[:, 0:NE], start=True, stop=True)
                            for j in range(2):
                                for part in range(2):
                                    last = pe.matmul(G.psO[1][:, j * N:(j + 1) * N], row_pick[:, j, :],
                                                     wts[part][:, :], start=part == 0, stop=part == 1,
                                                     skip_group_check=True)
                            last.then_inc(s.c_wide.handle, 1)
                        if i >= 2 and i + 2 < TH_:
                            pe.wait_ge(*s.h1.count(b, i - 1))
                            base(i + 2)
                        if i == TH_ + 2:
                            pe.wait_ge(*s.h1.count(b, TH_))
                            turn_x(pe, b + 1, s, G, xcur, G.psS)
                        if i == 3:
                            pe.wait_ge(*s.c_ready.count(b, 1))
                            pe.wait_ge(*s.x_done.count(b, 0))
                        if i >= 3:
                            t = i - 3
                            pe.wait_ge(*s.ch_lo.count(b, t + 1))
                            for j in range(2):
                                last = three(pe, Z[:, j * N:(j + 1) * N], dA[0][:, t, :], dA[1][:, t, :],
                                             chs[0][:, t % 2, j, :], chs[1][:, t % 2, j, :], t == 0 and j == 0,
                                             t == TH_ - 1)
                            if t == TH_ - 1:
                                last.then_inc(s.z_ready.handle, 1)
                            for n in range(NT):
                                at = slice(n * P, (n + 1) * P)
                                last = three(pe, Y[n][:, :], chs[0][:, t % 2, 2, at], chs[1][:, t % 2, 2, at],
                                             wd[0][:, t, :], wd[1][:, t, :], t == 0, False)
                            last.then_inc(s.down_done.handle, 1)
                    pe.wait_ge(*s.z_parts.count(b, 1))
                    for n in range(NT):
                        at = slice(n * P, (n + 1) * P)
                        three(pe, Y[n][:, :], zs[0][:, at], zs[1][:, at], dB[0][:, 0, :], dB[1][:, 0, :], False, True)\
                            .then_inc(s.y_ready.handle, 1)

            @block.scalar
            def _(act):
                x_high(act, 0, s, xT, G.psS)
                with act.Fori(0, B) as b:
                    act.wait_ge(*s.a_ready.count(b, 1))
                    act.copy(act_a[:, :, :], G.psP[1][:, :].rearrange("p (u n) -> p u n", u=2))\
                        .then_inc(s.act_a_ready.handle, 1)
                    act.wait_ge(*s.wneg_ready.count(b, 1))
                    act.activation(wexp[:, :], G.psO[0][0:2, 0:N], ACT.Exp, bias=wneg[:, :], accum_out=wsum[:, :])\
                        .then_inc(s.wexp_ready.handle, 1)
                    for i in range(TH_ + 2):
                        if i < TH_:
                            act.wait_ge(*s.base_ready.count(b, i + 1))
                            act.wait_ge(*s.h0.count(b, i - 1))
                            act.activation(sil[:, 0, i % 2, :], U[i % NU][:, 0:N], ACT.Silu)\
                                .then_inc(s.sil0.handle, 1)
                        if 1 <= i <= TH_:
                            t = i - 1
                            act.wait_ge(*s.delta_ready.count(b, t + 1))
                            act.wait_ge(*s.h1.count(b, t - 1))
                            act.activation(sil[:, 1, t % 2, :], U[t % NU][:, 0:N], ACT.Silu)\
                                .then_inc(s.sil1.handle, 1)
                        if i == 1:
                            act.wait_ge(*s.c_wide.count(b, 1))
                            act.copy(c[:, :, :], G.psO[1][:, :].rearrange("p (j n) -> p j n", j=2))\
                                .then_inc(s.c_ready.handle, 1)
                        if i >= 2:
                            t = i - 2
                            act.wait_ge(*s.ch_ready.count(b, t + 1))
                            act.wait_ge(*s.down_done.count(b, t - 1))
                            act.copy(chs[0][:, t % 2, :, :], ch[:, t % 2, :, :]).then_inc(s.ch_hi.handle, 1)
                    x_high(act, b + 1, s, xT, G.psS)

            @block.vector
            def _(dve):
                dve.wait_ge(consts, 32)
                x_low(dve, 0, s, xT, G.psS)
                with dve.Fori(0, B) as b:
                    steps = Steps(dve, s.chain, b)
                    dve.wait_ge(*s.logits_ready.count(b, 1))
                    steps.done(dve.tensor_copy(logits[:, :, :], G.psP[0][:, 0:NT * NE].rearrange("p (n e) -> p n e", n=NT)))
                    for n in range(NT):
                        dve.memset(G.junk[:, :], 0.0)
                        steps.done(dve.max(top[:, n, :], logits[:, n, :]))
                        dve.memset(G.junk[:, :], 0.0)
                        steps.done(dve.max_index(top_at[:, n, :], top[:, n, :], logits[:, n, :]))
                    dve.tensor_copy(top_f[:, :, :], top_at[:, :, :]).then_inc(s.top_ready.handle, 1)
                    dve.wait_ge(*s.top_ready.count(b, 1))
                    for j in range(2):
                        for n in range(NT):
                            last = dve.tensor_scalar(picked[:, j, n, :], expert_of[:, :], top_f[:, n, j:j + 1], 2.0,
                                                     ALU.is_equal, ALU.mult)
                    last.then_inc(s.picked_ready.handle, 1)
                    dve.wait_ge(*s.top_turned.count(b, 1))
                    dve.tensor_reduce(wneg[:, :], G.psO[0][0:2, 0:N], X_AXIS, ALU.max, negate=True)\
                        .then_inc(s.wneg_ready.handle, 1)
                    dve.wait_ge(*s.mask_turned.count(b, 1))
                    dve.tensor_copy(mask[:, :, :], TM[:, 0:2 * N].rearrange("p (j n) -> p j n", j=2))\
                        .then_inc(s.mask_ready.handle, 1)
                    dve.wait_ge(*s.mask_ready.count(b, 1))
                    steps.done(dve.tensor_tensor(dmask[:, :], mask[:, 1, :], mask[:, 0, :], ALU.subtract))
                    dve.wait_ge(*s.act_a_ready.count(b, 1))
                    m = dmask[:, :].rearrange("p (a n) -> p a n", a=1).broadcast_to([P, 2, N])
                    dve.tensor_tensor(am[:, 1, :, :], act_a[:, :, :], m, ALU.mult)
                    steps.done(dve.tensor_tensor(a_part[0][:, 1, :, :], act_a[:, :, :], m, ALU.mult))
                    dve.tensor_tensor(a_part[1][:, 1, :, :], am[:, 1, :, :], a_part[0][:, 1, :, :], ALU.subtract)\
                        .then_inc(s.a_split1.handle, 1)
                    dve.wait_ge(*s.wexp_ready.count(b, 1))
                    steps.done(dve.reciprocal(winv[:, :], wsum[:, :]))
                    steps.done(dve.tensor_scalar(wexp[:, :], wexp[:, :], winv[:, 0:1], None, ALU.mult))
                    steps.done(dve.tensor_copy(wts[0][:, :], wexp[:, :]))
                    dve.tensor_tensor(wts[1][:, :], wexp[:, :], wts[0][:, :], ALU.subtract)\
                        .then_inc(s.wts_ready.handle, 1)
                    for i in range(TH_ + 2):
                        if i < TH_:
                            dve.wait_ge(*s.sil0.count(b, i + 1))
                            dve.wait_ge(*s.ch_ready.count(b, i - 1))
                            dve.tensor_tensor(h[:, 0, i % 2, :], U[i % NU][:, N:2 * N], sil[:, 0, i % 2, :], ALU.mult)\
                                .then_inc(s.h0.handle, 1)
                        if 1 <= i <= TH_:
                            t = i - 1
                            dve.wait_ge(*s.sil1.count(b, t + 1))
                            dve.tensor_tensor(h[:, 1, t % 2, :], U[t % NU][:, N:2 * N], sil[:, 1, t % 2, :], ALU.mult)\
                                .then_inc(s.h1.handle, 1)
                        if i >= 2:
                            t = i - 2
                            dve.wait_ge(*s.ch_hi.count(b, t + 1))
                            dve.tensor_tensor(chs[1][:, t % 2, :, :], ch[:, t % 2, :, :], chs[0][:, t % 2, :, :],
                                              ALU.subtract).then_inc(s.ch_lo.handle, 1)
                    x_low(dve, b + 1, s, xT, G.psS)
                    dve.wait_ge(*s.z_ready.count(b, 1))
                    steps.done(dve.tensor_tensor(zm[:, :, :], Z[:, :].rearrange("p (j n) -> p j n", j=2),
                                                 mask[:, :, :], ALU.mult))
                    steps.done(dve.tensor_tensor(zm[:, 0, :], zm[:, 0, :], zm[:, 1, :], ALU.add))
                    steps.done(dve.tensor_copy(zs[0][:, :], zm[:, 0, :]))
                    dve.tensor_tensor(zs[1][:, :], zm[:, 0, :], zs[0][:, :], ALU.subtract)\
                        .then_inc(s.z_parts.handle, 1)
                    for n in range(NT):
                        add_and_norm(dve, s, b, n, Y[n][:, :], s.y_ready, G, steps)
                    steps.check()


def xattn1(nc, G, W):
    H, KVH, D = 16, 8, 128
    NS, NPB = 2, 3
    SCALE = float(1.0 / np.sqrt(np.float32(D)))
    with Scope(nc, "c1") as sc:
        def pair(name, shape):
            return [sc.sb(f"{name}{i}", shape, F16) for i in range(2)]

        wq = pair("wq", [P, KE, H * D])
        wk = pair("wk", [P, KC, KVH * D])
        wv = pair("wv", [P, KC, KVH * D])
        wo = pair("wo", [P, H, E])
        cT = pair("cT", [P, KC, B * N])
        load_and_split(nc, sc, G, [(kt_view(d), w[0][:, :, :], w[1][:, :, :]) for d, w in (
            (W["L1_xattn_Wq"], wq), (W["L1_xattn_Wk"], wk), (W["L1_xattn_Wv"], wv), (W["L1_xattn_Wo"], wo), (W["ctxT"], cT))])

        xT = pair("xT", [P, KE, N])
        qT = pair("qT", [P, H, N])
        oT = qT
        kT = pair("kT", [P, KVH, N])
        v = pair("v", [P, NT, KVH * D])
        xcur = sc.sb("xcur", [P, NT, E], F32)
        prob = sc.sb("prob", [P, NPB, NT, N], F32)
        sums = sc.sb("sums", [P, NPB, NT], F32)
        inv = sc.sb("inv", [P, NPB, NT], F32)
        negmax = sc.sb("negmax", [P, NPB, NT], F32)
        pT = pair("pT", [P, 2, NT, N])
        seen_col8 = sc.sb("seen_col8", [P, B * NT], U8)
        seen_row8 = sc.sb("seen_row8", [1, B * N], U8)
        seen_col = sc.sb("seen_col", [P, (B + 1) * NT], F32)
        seen_now = sc.sb("seen_now", [P, NT], F32)
        hide_row = sc.sb("hide_row", [1, B * N], BF16)
        ones_b = sc.sb("ones_b", [1, P], BF16)

        NQ, NK, NV = H // 2, KVH // 2, NT * 2
        NPR = NQ + NK + NV
        s = Names()
        x_counters(sc, s)
        s.t_ready = sc.counter("t_ready", H)
        s.t_hi = sc.counter("t_hi", H)
        s.t_lo = sc.counter("t_lo", H)
        s.pr_ready = sc.counter("pr_ready", NPR)
        s.pr_hi = sc.counter("pr_hi", NPR)
        s.pr_lo = sc.counter("pr_lo", NPR)
        s.s_ready = sc.counter("s_ready", H)
        s.m_ready = sc.counter("m_ready", H)
        s.e_ready = sc.counter("e_ready", H)
        s.i_ready = sc.counter("i_ready", H)
        s.p_ready = sc.counter("p_ready", H)
        s.o_ready = sc.counter("o_ready", H)
        s.o_hi = sc.counter("o_hi", H)
        s.o_lo = sc.counter("o_lo", H)
        s.y_ready = sc.counter("y_ready", NT)
        s.chain = sc.counter("chain", NT * LN_STEPS)
        ln_counters(sc, s)
        landed, masks_ready = sc.sem("landed"), sc.sem("masks_ready")
        SB, Y = G.psS, G.psP
        PR = [G.psO[0], G.psO[1], G.psP[0], G.psP[1]]
        sc.start_counters()

        with nc.Block() as block:
            @block.sync
            def _(sp):
                sp.dma_start(seen_row8[0:1, :], W["seen"].rearrange("(a b) n -> a (b n)", a=1)).then_inc(landed, 16)
                sp.dma_start(seen_col8[:, :], W["seen_cols"]).then_inc(landed, 16)

            @block.gpsimd
            def _(pool):
                pool.wait_ge(masks_ready, 3)

                def fetch(b):
                    pool.wait_ge(*s.pr_lo.count(b, 0))
                    pool.tensor_copy(seen_now[:, :], seen_col[:, bass.ds(b * NT, NT)])
                    fetch_x(pool, b, s, G, xcur)

                fetch(0)
                with pool.Fori(0, B) as b:
                    fetch(b + 1)
                    for h in range(H):
                        pool.wait_ge(*s.i_ready.count(b, h + 1))
                        pool.tensor_tensor(
                            prob[:, h % NPB, :, :], prob[:, h % NPB, :, :],
                            inv[:, h % NPB, :].rearrange("p (n a) -> p n a", a=1).broadcast_to([P, NT, N]),
                            ALU.mult).then_inc(s.p_ready.handle, 1)
                    for n in range(NT):
                        rstd_on_pool(pool, s, b, n, G)

            @block.tensor
            def _(pe):
                def turn(b, g, blocks):
                    pe.wait_ge(*s.t_lo.count(b, g - 1))
                    for out, src in blocks:
                        last = pe.transpose(out, src, G.ident[:, :])
                    last.then_inc(s.t_ready.handle, 1)

                pe.wait_ge(masks_ready, 3)
                turn_x(pe, 0, s, G, xcur, G.psS)
                with pe.Fori(0, B) as b:
                    ctx_at = bass.ds(b * N, N)
                    for i in range(NPR):
                        if i == 2:
                            pe.wait_ge(*s.x_done.count(b, 0))
                        if i >= 4:
                            pe.wait_ge(*s.pr_lo.count(b, i - 3))
                        out = PR[i % 4]
                        if i < NK:
                            for j in range(2):
                                cols = slice((2 * i + j) * D, (2 * i + j + 1) * D)
                                for k in range(KC):
                                    last = three(pe, out[:, j * N:(j + 1) * N], wk[0][:, k, cols], wk[1][:, k, cols],
                                                 cT[0][:, k, ctx_at], cT[1][:, k, ctx_at], k == 0, k == KC - 1)
                        elif i < NK + NV:
                            n, cc = divmod(i - NK, 2)
                            at = bass.ds(b * N + n * P, P)
                            cols = slice(cc * E, (cc + 1) * E)
                            for k in range(KC):
                                last = three(pe, out[:, :], cT[0][:, k, at], cT[1][:, k, at], wv[0][:, k, cols],
                                             wv[1][:, k, cols], k == 0, k == KC - 1)
                        else:
                            if i == NK + NV:
                                pe.wait_ge(*s.x_lo.count(b, NT))
                            for j in range(2):
                                hq = 2 * (i - NK - NV) + j
                                for k in range(KE):
                                    last = three(pe, out[:, j * N:(j + 1) * N], wq[0][:, k, hq * D:(hq + 1) * D],
                                                 wq[1][:, k, hq * D:(hq + 1) * D], xT[0][:, k, :], xT[1][:, k, :],
                                                 k == 0, k == KE - 1)
                        last.then_inc(s.pr_ready.handle, 1)

                    def scores(h):
                        if h >= NS:
                            pe.wait_ge(*s.e_ready.count(b, h - NS + 1))
                        S, hk = SB[h % NS], h // 2
                        for n in range(NT):
                            out = S[:, n * N:(n + 1) * N]
                            three(pe, out, qT[0][:, h, n * P:(n + 1) * P], qT[1][:, h, n * P:(n + 1) * P],
                                  kT[0][:, hk, :], kT[1][:, hk, :], True, False)
                            last = pe.matmul(out, ones_b[0:1, :], hide_row[0:1, ctx_at], start=False, stop=True,
                                             skip_group_check=True)
                        last.then_inc(s.s_ready.handle, 1)

                    def turn_p(h):
                        T = G.psT[h % 2]
                        pe.wait_ge(*s.p_ready.count(b, h + 1))
                        turn(b, h, [(T[:, m * N + n * P:m * N + (n + 1) * P], prob[:, h % NPB, n, m * P:(m + 1) * P])
                                    for m in range(NT) for n in range(NT)])

                    def pv(h):
                        if h >= 2:
                            pe.wait_ge(*s.o_lo.count(b, h - 1))
                        pe.wait_ge(*s.t_lo.count(b, h + 1))
                        r, cols = h % 2, slice((h // 2) * D, (h // 2 + 1) * D)
                        for m in range(NT):
                            last = three(pe, G.psO[r][:, 0:N], v[0][:, m, cols], v[1][:, m, cols],
                                         pT[0][:, r, m, :], pT[1][:, r, m, :], m == 0, m == NT - 1)
                        last.then_inc(s.o_ready.handle, 1)

                    def project(h):
                        pe.wait_ge(*s.o_lo.count(b, h + 1))
                        for n in range(NT):
                            last = three(pe, Y[n][:, :], oT[0][:, h, n * P:(n + 1) * P],
                                         oT[1][:, h, n * P:(n + 1) * P], wo[0][:, h, :], wo[1][:, h, :],
                                         h == 0, h == H - 1)
                            if h == H - 1:
                                last.then_inc(s.y_ready.handle, 1)

                    pe.wait_ge(*s.pr_lo.count(b, NPR))
                    for i in range(H + 5):
                        if i < H:
                            scores(i)
                        if 2 <= i < H + 2:
                            turn_p(i - 2)
                        if 3 <= i < H + 3:
                            pv(i - 3)
                        if i == H + 2:
                            pe.wait_ge(*s.e_ready.count(b, H))
                            turn_x(pe, b + 1, s, G, xcur, G.psS)
                        if i >= 5:
                            project(i - 5)

            @block.scalar
            def _(act):
                act.wait_ge(masks_ready, 3)
                x_high(act, 0, s, xT, G.psS)
                with act.Fori(0, B) as b:
                    act.wait_ge(*s.xcur_ready.count(b, 1))
                    for i in range(NPR):
                        act.wait_ge(*s.pr_ready.count(b, i + 1))
                        out = PR[i % 4][:, :]
                        two = out.rearrange("p (j n) -> p j n", j=2)
                        if i < NK:
                            last = act.copy(kT[0][:, 2 * i:2 * i + 2, :], two)
                        elif i < NK + NV:
                            n, cc = divmod(i - NK, 2)
                            last = act.mul(v[0][:, n, cc * E:(cc + 1) * E], out, seen_now[:, n:n + 1])
                        else:
                            j = i - NK - NV
                            last = act.mul(qT[0][:, 2 * j:2 * j + 2, :], two, SCALE)
                        last.then_inc(s.pr_hi.handle, 1)

                    def expo(h):
                        act.wait_ge(*s.m_ready.count(b, h + 1))
                        if h >= NPB:
                            act.wait_ge(*s.t_ready.count(b, h - NPB + 1))
                        S, r = SB[h % NS], h % NPB
                        for n in range(NT):
                            last = act.activation(prob[:, r, n, :], S[:, n * N:(n + 1) * N], ACT.Exp,
                                                  bias=negmax[:, r, n:n + 1], accum_out=sums[:, r, n:n + 1])
                        last.then_inc(s.e_ready.handle, 1)

                    def hi_p(h):
                        act.wait_ge(*s.t_ready.count(b, h + 1))
                        if h >= 2:
                            act.wait_ge(*s.o_ready.count(b, h - 1))
                        act.copy(pT[0][:, h % 2, :, :], G.psT[h % 2][:, :].rearrange("p (m n) -> p m n", m=NT))\
                            .then_inc(s.t_hi.handle, 1)

                    def hi_o(h):
                        act.wait_ge(*s.o_ready.count(b, h + 1))
                        act.copy(oT[0][:, h, :], G.psO[h % 2][:, 0:N]).then_inc(s.o_hi.handle, 1)

                    for i in range(H + 3):
                        if 2 <= i < H + 2:
                            hi_p(i - 2)
                        if i < H:
                            expo(i)
                        if i >= 3:
                            hi_o(i - 3)
                    x_high(act, b + 1, s, xT, G.psS)

            @block.vector
            def _(dve):
                dve.wait_ge(landed, 32)
                dve.memset(seen_col[:, B * NT:(B + 1) * NT], 0.0)
                dve.tensor_copy(seen_col[:, 0:B * NT], seen_col8[:, :]).then_inc(masks_ready, 1)
                dve.tensor_scalar(hide_row[:, :], seen_row8[:, :], -1.0, -MASKED, ALU.add, ALU.mult)\
                    .then_inc(masks_ready, 1)
                dve.memset(ones_b[:, :], 1.0).then_inc(masks_ready, 1)
                dve.wait_ge(masks_ready, 3)
                x_low(dve, 0, s, xT, G.psS)
                with dve.Fori(0, B) as b:
                    steps = Steps(dve, s.chain, b)
                    dve.wait_ge(*s.xcur_ready.count(b, 1))
                    for i in range(NPR):
                        dve.wait_ge(*s.pr_hi.count(b, i + 1))
                        out = PR[i % 4][:, :]
                        two = out.rearrange("p (j n) -> p j n", j=2)
                        if i < NK:
                            at = (slice(None), slice(2 * i, 2 * i + 2), slice(None))
                            last = dve.tensor_tensor(kT[1][at], two, kT[0][at], ALU.subtract)
                        elif i < NK + NV:
                            n, cc = divmod(i - NK, 2)
                            cols = slice(cc * E, (cc + 1) * E)
                            last = dve.scalar_tensor_tensor(v[1][:, n, cols], out, seen_now[:, n:n + 1],
                                                            v[0][:, n, cols], ALU.mult, ALU.subtract)
                        else:
                            j = i - NK - NV
                            at = (slice(None), slice(2 * j, 2 * j + 2), slice(None))
                            last = dve.scalar_tensor_tensor(qT[1][at], two, SCALE, qT[0][at], ALU.mult, ALU.subtract)
                        last.then_inc(s.pr_lo.handle, 1)

                    def rowmax(h):
                        dve.wait_ge(*s.s_ready.count(b, h + 1))
                        if h >= NPB:
                            dve.wait_ge(*s.e_ready.count(b, h - NPB + 1))
                        dve.tensor_reduce(negmax[:, h % NPB, :], SB[h % NS][:, :].rearrange("p (n m) -> p n m", n=NT),
                                          X_AXIS, ALU.max, negate=True).then_inc(s.m_ready.handle, 1)

                    def invert(h):
                        dve.wait_ge(*s.e_ready.count(b, h + 1))
                        if h >= NPB:
                            dve.wait_ge(*s.p_ready.count(b, h - NPB + 1))
                        dve.reciprocal(inv[:, h % NPB, :], sums[:, h % NPB, :]).then_inc(s.i_ready.handle, 1)

                    def lo_p(h):
                        dve.wait_ge(*s.t_hi.count(b, h + 1))
                        dve.tensor_tensor(pT[1][:, h % 2, :, :], G.psT[h % 2][:, :].rearrange("p (m n) -> p m n", m=NT),
                                          pT[0][:, h % 2, :, :], ALU.subtract).then_inc(s.t_lo.handle, 1)

                    def lo_o(h):
                        dve.wait_ge(*s.o_hi.count(b, h + 1))
                        dve.tensor_tensor(oT[1][:, h, :], G.psO[h % 2][:, 0:N], oT[0][:, h, :], ALU.subtract)\
                            .then_inc(s.o_lo.handle, 1)

                    for i in range(H + 3):
                        if i < H:
                            rowmax(i)
                        if 1 <= i <= H:
                            invert(i - 1)
                        if 2 <= i < H + 2:
                            lo_p(i - 2)
                        if i >= 3:
                            lo_o(i - 3)
                    x_low(dve, b + 1, s, xT, G.psS)
                    for n in range(NT):
                        add_and_norm(dve, s, b, n, Y[n][:, :], s.y_ready, G, steps)
                    steps.check()


def ternary_weights(nc, sc, G, drams, out, cneg):
    WORDS = 8192
    with ExitStack() as stack:
        raw = stack.enter_context(nc.sbuf_tensor("f1_raw", [P, 3, WORDS], F32))

        def small(name, shape):
            return stack.enter_context(nc.sbuf_tensor(f"f1_{name}", shape, F32))

        part = small("part", [P, 3, 16])
        total = small("total", [P, 4])
        s_mean = small("s_mean", [P, 3])
        thr = small("thr", [P, 2, 3])
        logs = small("logs", [P, 2, 3])
        sem = {k: sc.sem(k) for k in ("raw0", "raw1", "raw2", "w_step", "total_done", "logs_done", "above_done", "w_done")}
        with nc.Block() as block:
            @block.sync
            def _(sp):
                for i, d in enumerate(drams):
                    v = kt_view(d)
                    k = v.shape[1]
                    sp.dma_start(raw[:, i, :].rearrange("p (k n) -> p k n", k=k), v).then_inc(sem[f"raw{i}"], 16)

            @block.gpsimd
            def _(pool):
                pool.wait_ge(sem["w_step"], 10)
                for i in range(3):
                    pool.tensor_scalar(out[i], raw[:, i, :], thr[:, 0, i:i + 1], None, ALU.is_gt)\
                        .then_inc(sem["above_done"], 1)

            @block.tensor
            def _(pe):
                pe.wait_ge(sem["w_step"], 7)
                pe.matmul(G.psP[0][:, 0:4], G.ones[:, 0:P], total[:, :], start=True, stop=True)\
                    .then_inc(sem["total_done"], 1)

            @block.scalar
            def _(act):
                act.wait_ge(sem["w_step"], 8)
                act.activation(logs[:, 0, :], s_mean[:, :], ACT.Ln, bias=1.0)
                act.activation(logs[:, 1, :], s_mean[:, :], ACT.Ln, bias=1.0, scale=-1.0)\
                    .then_inc(sem["logs_done"], 1)

            @block.vector
            def _(dve):
                n = 0

                def then(ins):
                    nonlocal n
                    n += 1
                    ins.then_inc(sem["w_step"], 1)
                    dve.wait_ge(sem["w_step"], n)
                then(dve.memset(total[:, :], 0.0))
                for i in range(3):
                    dve.wait_ge(sem[f"raw{i}"], 16)
                    then(dve.tensor_reduce(part[:, i, :], raw[:, i, :].rearrange("p (a n) -> p a n", a=16), X_AXIS,
                                           ALU.add, apply_absolute_value=True))
                    then(dve.tensor_reduce(total[:, i:i + 1], part[:, i, :], X_AXIS, ALU.add))
                dve.wait_ge(sem["total_done"], 1)
                then(dve.tensor_scalar(s_mean[:, :], G.psP[0][:, 0:3], 1.0 / (P * WORDS), None, ALU.mult))
                for j, sign in enumerate((1.0, -1.0)):
                    then(dve.tensor_scalar(thr[:, j, :], s_mean[:, :], 1e-8, sign * float(np.arctanh(0.5)),
                                           ALU.add, ALU.mult))
                for i in range(3):
                    dve.wait_ge(sem["above_done"], i + 1)
                    dve.scalar_tensor_tensor(out[i], raw[:, i, :], thr[:, 1, i:i + 1], out[i],
                                             ALU.is_lt, ALU.subtract).then_inc(sem["w_done"], 1)
                dve.wait_ge(sem["logs_done"], 1)
                then(dve.tensor_tensor(logs[:, 0, :], logs[:, 1, :], logs[:, 0, :], ALU.subtract))
                dve.tensor_scalar(cneg[:, :], logs[:, 0, :], 0.5 / 127.0, None, ALU.mult)


def ffn1(nc, G, W):
    HID = 2048
    NCH = HID // E
    KH = HID // P
    ROUND = float(1.5 * 2 ** 23)
    with Scope(nc, "f1") as sc:
        wq = [sc.sb(f"wq{i}", [P, 8192], F16) for i in range(3)]
        w12 = [w[:, :].rearrange("p (k n) -> p k n", k=KE) for w in wq[:2]]
        w3 = wq[2][:, :].rearrange("p (k n) -> p k n", k=KH)
        cneg = sc.sb("cneg", [P, 3], F32)
        ternary_weights(nc, sc, G, (W["L1_ffn_w1T"], W["L1_ffn_w2T"], W["L1_ffn_w3T"]), [w[:, :] for w in wq], cneg)

        g12 = sc.sb("g12", [P, 2, E], F32)
        g3 = sc.sb("g3", [P, HID], F32)
        xcur = sc.sb("xcur", [P, NT, E], F32)
        squares = sc.sb("squares", [P, E], F32)
        ssx = sc.sb("ssx", [P, NT], F32)
        msx = sc.sb("msx", [P, NT], F32)
        rx = sc.sb("rx", [P, NT], F32)
        xn = sc.sb("xn", [P, NT, 2, E], F32)
        xr = sc.sb("xr", [P, NT, 2 * E], F16)
        mx = sc.sb("mx", [P, NT, 2], F32)
        qx = sc.sb("qx", [P, NT, 2], F32)
        ax = sc.sb("ax", [P, NT, 2], F32)
        xq = sc.sb("xq", [P, 2, KE, N], F16)
        sil = sc.sb("sil", [P, 2, E], F32)
        h = sc.sb("h", [P, 2, E], F32)
        hg = sc.sb("hg", [P, NT, HID], F32)
        hr = sc.sb("hr", [P, NT, HID], F16)
        ssh = sc.sb("ssh", [P, NT, NCH], F32)
        mxh = sc.sb("mxh", [P, NT, NCH], F32)
        hs = sc.sb("hs", [P, NT, 8], F32)
        rh = sc.sb("rh", [P, NT], F32)
        hq = sc.sb("hq", [P, KH, N], F16)

        U = [G.psS[0], G.psS[1], G.psP[0], G.psP[1]]
        NJ = NT * NCH
        s = Names()
        s.xcur_ready = sc.counter("xcur_ready", 1)
        s.ssx_ready = sc.counter("ssx_ready", NT)
        s.msx_ready = sc.counter("msx_ready", NT)
        s.rx_ready = sc.counter("rx_ready", NT)
        s.xn_ready = sc.counter("xn_ready", NT)
        s.xr_ready = sc.counter("xr_ready", NT)
        s.xt_ready = sc.counter("xt_ready", NT)
        s.xq_ready = sc.counter("xq_ready", NT)
        s.u_ready = sc.counter("u_ready", NJ)
        s.sil_ready = sc.counter("sil_ready", NJ)
        s.h_ready = sc.counter("h_ready", NJ)
        s.sq_ready = sc.counter("sq_ready", NJ)
        s.hg_ready = sc.counter("hg_ready", NJ)
        s.mh_ready = sc.counter("mh_ready", NT)
        s.rh_ready = sc.counter("rh_ready", NT)
        s.hm_ready = sc.counter("hm_ready", NT)
        s.hr_ready = sc.counter("hr_ready", NT)
        s.ht_ready = sc.counter("ht_ready", 2 * NT)
        s.hq_ready = sc.counter("hq_ready", 2 * NT)
        s.y_ready = sc.counter("y_ready", NT)
        s.chain = sc.counter("chain", NT * 5 + NT * 7 + NT * LN_STEPS)
        ln_counters(sc, s)
        landed = sc.sem("landed")
        sc.start_counters()
        TH16 = [t[:, :].bitcast(F16) for t in G.psT]

        with nc.Block() as block:
            @block.sync
            def _(sp):
                for i, g in enumerate((W["L1_ffn_g1"], W["L1_ffn_g2"])):
                    sp.dma_start(g12[:, i, :], g.rearrange("(a n) -> a n", a=1).broadcast_to([P, E]))\
                        .then_inc(landed, 16)
                sp.dma_start(g3[:, :], W["L1_ffn_g3"].rearrange("(a n) -> a n", a=1).broadcast_to([P, HID]))\
                    .then_inc(landed, 16)

            @block.gpsimd
            def _(pool):
                pool.wait_ge(landed, 48)
                with pool.Fori(0, B) as b:
                    pool.wait_ge(*s.ssx_ready.count(b, 0))
                    pool.tensor_copy(xcur[:, :, :], G.x[:, bass.ds(b * NT, NT), :]).then_inc(s.xcur_ready.handle, 1)
                    for n in range(NT):
                        pool.wait_ge(*s.msx_ready.count(b, n + 1))
                        pool.tensor_tensor(rx[:, n:n + 1], msx[:, n:n + 1], G.minus_half[:, 0:1], ALU.pow)\
                            .then_inc(s.rx_ready.handle, 1)
                    for j in range(NJ):
                        n, c = divmod(j, NCH)
                        pool.wait_ge(*s.h_ready.count(b, j + 1))
                        at = slice(c * E, (c + 1) * E)
                        pool.tensor_tensor(hg[:, n, at], h[:, j % 2, :], g3[:, at], ALU.mult)\
                            .then_inc(s.hg_ready.handle, 1)
                        if c == NCH - 1:
                            pool.wait_ge(*s.mh_ready.count(b, n + 1))
                            pool.tensor_tensor(rh[:, n:n + 1], hs[:, n, 1:2], G.minus_half[:, 0:1], ALU.pow)\
                                .then_inc(s.rh_ready.handle, 1)
                    for n in range(NT):
                        rstd_on_pool(pool, s, b, n, G)

            @block.tensor
            def _(pe):
                with pe.Fori(0, B) as b:
                    pe.wait_ge(*s.x_done.count(b, 0))
                    for n in range(NT):
                        pe.wait_ge(*s.xr_ready.count(b, n + 1))
                        for k in range(2 * KE):
                            last = pe.transpose(TH16[n][:, k * P:(k + 1) * P], xr[:, n, k * P:(k + 1) * P],
                                                G.ident_h[:, :])
                        last.then_inc(s.xt_ready.handle, 1)
                    for j in range(NJ):
                        n, c = divmod(j, NCH)
                        pe.wait_ge(*s.xq_ready.count(b, n + 1))
                        if j >= 2:
                            pe.wait_ge(*s.h_ready.count(b, j - 1))
                        for i in range(2):
                            for k in range(KE):
                                last = pe.matmul(U[2 * (j % 2) + i][:, :], xq[:, i, k, n * P:(n + 1) * P],
                                                 w12[i][:, k, c * E:(c + 1) * E], start=k == 0, stop=k == KE - 1)
                        last.then_inc(s.u_ready.handle, 1)
                    for n in range(NT):
                        pe.wait_ge(*s.hr_ready.count(b, n + 1))
                        for g in range(2):
                            if n:
                                pe.wait_ge(*s.hq_ready.count(b, g + 1))
                            for k in range(8):
                                kk = g * 8 + k
                                last = pe.transpose(TH16[g][:, k * P:(k + 1) * P], hr[:, n, kk * P:(kk + 1) * P],
                                                    G.ident_h[:, :])
                            last.then_inc(s.ht_ready.handle, 1)
                        pe.wait_ge(*s.hq_ready.count(b, 2 * n + 2))
                        for k in range(KH):
                            last = pe.matmul(G.psO[n][:, :], hq[:, k, n * P:(n + 1) * P], w3[:, k, :],
                                             start=k == 0, stop=k == KH - 1)
                        last.then_inc(s.y_ready.handle, 1)

            @block.scalar
            def _(act):
                with act.Fori(0, B) as b:
                    for n in range(NT):
                        if n:
                            act.wait_ge(*s.ssx_ready.count(b, n))
                        else:
                            act.wait_ge(*s.sq_ready.count(b, 0))
                            act.wait_ge(*s.xcur_ready.count(b, 1))
                        act.activation(squares[:, :], xcur[:, n, :], ACT.Square, accum_out=ssx[:, n:n + 1]).then_inc(s.ssx_ready.handle, 1)

                    def square(j):
                        n, c = divmod(j, NCH)
                        act.wait_ge(*(s.sq_ready if j else s.ssx_ready).count(b, j or NT))
                        act.wait_ge(*s.h_ready.count(b, j + 1))
                        act.activation(squares[:, :], h[:, j % 2, :], ACT.Square, accum_out=ssh[:, n, c:c + 1])\
                            .then_inc(s.sq_ready.handle, 1)

                    for j in range(NJ):
                        n = j // NCH
                        act.wait_ge(*s.u_ready.count(b, j + 1))
                        if j >= 2:
                            act.wait_ge(*s.h_ready.count(b, j - 1))
                        act.activation(sil[:, j % 2, :], U[2 * (j % 2)][:, :], ACT.Silu, scale=ax[:, n, 0:1])\
                            .then_inc(s.sil_ready.handle, 1)
                        if j:
                            square(j - 1)
                    square(NJ - 1)

            @block.vector
            def _(dve):
                dve.wait_ge(landed, 48)
                with dve.Fori(0, B) as b:
                    steps = Steps(dve, s.chain, b)
                    for n in range(NT):
                        dve.wait_ge(*s.ssx_ready.count(b, n + 1))
                        dve.tensor_scalar(msx[:, n:n + 1], ssx[:, n:n + 1], 1.0 / E, 1e-8, ALU.mult, ALU.add)\
                            .then_inc(s.msx_ready.handle, 1)
                    for n in range(NT):
                        dve.wait_ge(*s.rx_ready.count(b, n + 1))
                        for i in range(2):
                            last = dve.scalar_tensor_tensor(xn[:, n, i:i + 1, :], G.x[:, bass.ds(b * NT + n, 1), :],
                                                            rx[:, n:n + 1], g12[:, i:i + 1, :], ALU.mult, ALU.mult)
                        steps.done(last)
                        steps.done(dve.tensor_reduce(mx[:, n, :], xn[:, n, :, :], X_AXIS, ALU.max,
                                                     apply_absolute_value=True))
                        steps.done(dve.tensor_scalar(mx[:, n, :], mx[:, n, :], 1e-4, None, ALU.max))
                        dve.tensor_tensor(ax[:, n, :], mx[:, n, :], cneg[:, 0:2], ALU.mult)
                        steps.done(dve.reciprocal(qx[:, n, :], mx[:, n, :]))
                        steps.done(dve.tensor_scalar(qx[:, n, :], qx[:, n, :], 127.0, None, ALU.mult))
                        for i in range(2):
                            last = dve.tensor_scalar(xn[:, n, i, :], xn[:, n, i, :], qx[:, n, i:i + 1], ROUND,
                                                     ALU.mult, ALU.add)
                        last.then_inc(s.xn_ready.handle, 1)
                        dve.wait_ge(*s.xn_ready.count(b, n + 1))
                        dve.tensor_scalar(xr[:, n, :], xn[:, n, :, :].rearrange("p i e -> p (i e)"), ROUND, None,
                                          ALU.subtract).then_inc(s.xr_ready.handle, 1)
                    for n in range(NT):
                        dve.wait_ge(*s.xt_ready.count(b, n + 1))
                        for i in range(2):
                            last = dve.tensor_scalar(
                                xq[:, i, :, n * P:(n + 1) * P],
                                TH16[n][:, i * E:(i + 1) * E].rearrange("p (k t) -> p k t", k=KE),
                                127.0, -128.0, ALU.min, ALU.max)
                        last.then_inc(s.xq_ready.handle, 1)

                    def absmax(j):
                        n, c = divmod(j, NCH)
                        dve.wait_ge(*s.hg_ready.count(b, j + 1))
                        last = dve.tensor_reduce(mxh[:, n, c:c + 1], hg[:, n, c * E:(c + 1) * E], X_AXIS, ALU.max,
                                                 apply_absolute_value=True)
                        if c == NCH - 1:
                            m = hs[:, n, :]
                            steps.done(last)
                            dve.wait_ge(*s.sq_ready.count(b, j + 1))
                            steps.done(dve.tensor_reduce(m[:, 0:1], ssh[:, n, :], X_AXIS, ALU.add))
                            dve.tensor_scalar(m[:, 1:2], m[:, 0:1], 1.0 / HID, 1e-8, ALU.mult, ALU.add)\
                                .then_inc(s.mh_ready.handle, 1)
                            steps.done(dve.tensor_reduce(m[:, 2:3], mxh[:, n, :], X_AXIS, ALU.max))
                            dve.wait_ge(*s.rh_ready.count(b, n + 1))
                            steps.done(dve.tensor_scalar(m[:, 3:4], m[:, 2:3], rh[:, n:n + 1], 1e-4, ALU.mult, ALU.max))
                            dve.tensor_tensor(m[:, 4:5], m[:, 3:4], cneg[:, 2:3], ALU.mult)
                            steps.done(dve.reciprocal(m[:, 5:6], m[:, 3:4]))
                            steps.done(dve.tensor_scalar(m[:, 6:7], m[:, 5:6], rh[:, n:n + 1], 127.0, ALU.mult, ALU.mult))
                            steps.done(dve.tensor_scalar(hg[:, n, :], hg[:, n, :], m[:, 6:7], ROUND, ALU.mult, ALU.add))
                            dve.tensor_scalar(hr[:, n, :], hg[:, n, :], ROUND, None, ALU.subtract)\
                                .then_inc(s.hr_ready.handle, 1)

                    for j in range(NJ):
                        dve.wait_ge(*s.sil_ready.count(b, j + 1))
                        if j >= 2:
                            dve.wait_ge(*s.hg_ready.count(b, j - 1))
                            dve.wait_ge(*s.sq_ready.count(b, j - 1))
                        dve.scalar_tensor_tensor(h[:, j % 2, :], U[2 * (j % 2) + 1][:, :], ax[:, j // NCH, 1:2],
                                                 sil[:, j % 2, :], ALU.mult, ALU.mult).then_inc(s.h_ready.handle, 1)
                        if j:
                            absmax(j - 1)
                    absmax(NJ - 1)
                    for n in range(NT):
                        for g in range(2):
                            dve.wait_ge(*s.ht_ready.count(b, 2 * n + g + 1))
                            dve.tensor_scalar(hq[:, g * 8:(g + 1) * 8, n * P:(n + 1) * P],
                                              TH16[g][:, :].rearrange("p (k t) -> p k t", k=8), 127.0, -128.0,
                                              ALU.min, ALU.max).then_inc(s.hq_ready.handle, 1)
                    for n in range(NT):
                        add_and_norm(dve, s, b, n, G.psO[n][:, :], s.y_ready, G, steps, hs[:, n, 4:5])
                    steps.check()


def more_inputs(a):
    def stack_B(w):
        return w.transpose(0, 2, 1).reshape(P, -1)

    seen = a["mask_BxS2_bf1"].view(np.uint8)
    return {
        "L1_ffn_w1T": a["L1_ffn_w1"].T, "L1_ffn_w2T": a["L1_ffn_w2"].T, "L1_ffn_w3T": a["L1_ffn_w3"].T,
        "L1_ffn_g1": a["L1_ffn_g1"], "L1_ffn_g2": a["L1_ffn_g2"], "L1_ffn_g3": a["L1_ffn_g3"],
        "f0_up_gateT": np.concatenate([a["L0_ffn_w_up"], a["L0_ffn_w_gate"]], 0).T,
        "f0_A": np.concatenate([a["L0_ffn_up_A"].reshape(P, E), a["L0_ffn_gate_A"].reshape(P, E)], 0).T,
        "f0_B": np.concatenate([stack_B(a["L0_ffn_up_B"]), stack_B(a["L0_ffn_gate_B"])], 1),
        "f0_downT": a["L0_ffn_w_down"].T, "f0_dA": a["L0_ffn_down_A"].reshape(P, -1).T,
        "f0_dB": stack_B(a["L0_ffn_down_B"]), "f0_router": a["L0_ffn_gate_w"].T,
        "expert_of": np.tile(np.repeat(np.arange(8, dtype=np.float32), 16), (P, 1)),
        "row_pick": np.repeat(np.eye(2, dtype=np.float16)[:, :, None], P, axis=2),
        "seen": seen, "seen_cols": seen.reshape(B * NT, P).T,
        "L1_xattn_Wq": a["L1_xattn_Wq"], "L1_xattn_Wk": a["L1_xattn_Wk"], "L1_xattn_Wv": a["L1_xattn_Wv"],
        "L1_xattn_Wo": a["L1_xattn_Wo"],
        "ctxT": a["ctx_1024"].reshape(B * N, C).T, "fside": a["fside_BxSx2_0"],
        "L0_xattn_Wq": a["L0_xattn_Wq"], "L0_xattn_Wkv": a["L0_xattn_Wkv"],
        "L0_xattn_Wout": a["L0_xattn_Wout"], "L0_xattn_bout": a["L0_xattn_bout"],
        "L1_attn_Wq": a["L1_attn_Wq"], "L1_attn_Wkv": np.concatenate([a["L1_attn_Wk"], a["L1_attn_Wv"]], 1),
        "L1_attn_Wo": a["L1_attn_Wo"], "L1_attn_bo": a["L1_attn_bo"],
    }


def build(nc, W, out, layers=6):
    with ExitStack() as stack:
        G = Names()
        G.STAGE, G.NSTAGE = 1024, 3

        def sb(name, shape, dt):
            return stack.enter_context(nc.sbuf_tensor(name, shape, dt))

        G.x = sb("x_all", [P, (B + 1) * NT, E], F32)
        G.stage = sb("stage", [P, G.NSTAGE, G.STAGE], F32)
        G.ident = sb("ident", [P, P], F32)
        G.ident_b = sb("ident_b", [P, P], BF16)
        G.ident_h = sb("ident_h", [P, P], F16)
        G.causal = sb("causal", [P, P], BF16)
        G.ones = sb("ones", [P, N], F32)
        G.ones_h = sb("ones_h", [P, P], F16)
        G.minus_half = sb("minus_half", [P, 1], F32)
        G.junk = sb("junk", [P, 1], F32)
        G.r = sb("ln_r", [P, NT, E], F32)
        G.stats = sb("ln_stats", [P, NT, 6], F32)
        G.mv = sb("ln_mv", [P, NT, 2], F32)
        G.ve = sb("ln_ve", [P, NT], F32)
        G.rstd = sb("ln_rstd", [P, NT], F32)
        bank = lambda name: stack.enter_context(nc.psum_tensor(name, [P, 512], F32))
        G.psS = [bank("psS0"), bank("psS1")]
        G.psT = [bank("psT0"), bank("psT1")]
        G.psO = [bank("psO0"), bank("psO1")]
        G.psP = [bank("psP0"), bank("psP1")]

        in_done = stack.enter_context(nc.semaphore("in_done"))
        const_step = stack.enter_context(nc.semaphore("const_step"))
        out_done = stack.enter_context(nc.semaphore("out_done"))
        with nc.Block() as block:
            @block.sync
            def _(sp):
                sp.dma_start(G.x[:, 0:B * NT, :], W["x"].rearrange("b (n p) e -> p (b n) e", p=P)).then_inc(in_done, 16)
                sp.wait_ge(in_done, 16)

            @block.gpsimd
            def _(pool):
                pool.memset(G.ident[:, :], 0.0).then_inc(const_step, 1)
                pool.memset(G.causal[:, :], 0.0).then_inc(const_step, 1)
                pool.memset(G.ones[:, :], 1.0)
                pool.memset(G.x[:, B * NT:(B + 1) * NT, :], 0.0)
                pool.memset(G.ones_h[:, :], 1.0)
                pool.memset(G.minus_half[:, :], -0.5)
                pool.wait_ge(const_step, 2)
                pool.affine_select(out=G.ident[:, :], in_=G.ident[:, :], compare_op=ALU.not_equal, fill=1.0,
                                   base=0, pattern=[[-1, P]], channel_multiplier=1).then_inc(const_step, 1)
                pool.affine_select(out=G.causal[:, :], in_=G.causal[:, :], compare_op=ALU.is_ge, fill=MASKED,
                                   base=0, pattern=[[-1, P]], channel_multiplier=1)
                pool.wait_ge(const_step, 3)
                pool.tensor_copy(G.ident_b[:, :], G.ident[:, :])
                pool.tensor_copy(G.ident_h[:, :], G.ident[:, :])

        for layer in LAYERS[:layers]:
            layer(nc, G, W)

        with nc.Block() as block:
            @block.sync
            def _(sp):
                sp.dma_start(out.rearrange("b (n p) e -> p (b n) e", p=P), G.x[:, 0:B * NT, :]).then_inc(out_done, 16)
                sp.wait_ge(out_done, 16)


LAYERS = [attn0, xattn0, ffn0, attn1, xattn1, ffn1]


def kernel(**inputs):
    import concourse.bacc as bacc
    from concourse.bass_utils import run_bass_kernel_spmd as run

    def rope_tables(scale):
        half = 64
        inv = 10000.0 ** (-np.arange(0, 2 * half, 2, dtype=np.float32) / np.float32(2 * half))
        ang = np.arange(N, dtype=np.float32)[:, None] * inv.astype(np.float32)[None, :]
        cos, sin = np.cos(ang), np.sin(ang)
        return (np.stack([np.concatenate([cos, cos], 1), np.concatenate([-sin, sin], 1)]) * scale).astype(np.float32)

    nc = bacc.Bacc("TRN2", target_bir_lowering=False, num_devices=1)
    a = {k: np.asarray(v) for k, v in inputs.items()}
    host = {
        "x": a["x"],
        "L0_attn_WqT": a["L0_attn_Wq"].T, "L0_attn_WkvT": a["L0_attn_Wkv"].T,
        "L0_attn_WhT": np.concatenate([a["L0_attn_Wkvh"], a["L0_attn_Wg"]], 0).T,
        "L0_attn_WoutT": a["L0_attn_Wout"].T,
        "rope_q": rope_tables(1.0 / np.sqrt(128.0)), "rope_k": rope_tables(1.0),
    }
    host.update(more_inputs(a))
    arrays, W = {}, {}
    for name, value in host.items():
        value = np.ascontiguousarray(value)
        arrays[f"in_{name}"] = value
        W[name] = nc.dram_tensor(f"in_{name}", value.shape, mybir.dt.from_np(value.dtype),
                                          kind="ExternalInput").ap()
    out = nc.dram_tensor("out_dram", (B, N, E), F32, kind="ExternalOutput").ap()
    build(nc, W, out)
    r = run(nc, [arrays], core_ids=[0])
    return r.results[0]["out_dram"]
```

```python
from contextlib import ExitStack

import numpy as np

import concourse.bass as bass
from concourse import mybir

F32 = mybir.dt.float32
F16 = mybir.dt.float16
BF16 = mybir.dt.bfloat16
U8 = mybir.dt.uint8
U32 = mybir.dt.uint32
ALU = mybir.AluOpType
ACT = mybir.ActivationFunctionType
X_AXIS = mybir.AxisListType.X

P = 128
B = 8
N = 256
NT = N // P
E = 512
KE = E // P
C = 256
KC = C // P
EPS = 1e-5
MASKED = -1e30


class Names:
    pass


class Counter:

    def __init__(self, handle, per_seq):
        self.handle = handle
        self.per_seq = per_seq

    def count(self, b, n):
        return self.handle, b * self.per_seq + (max(n, 0) + 1)


class Steps:

    def __init__(self, eng, counter, b):
        self.eng, self.counter, self.b, self.n = eng, counter, b, 0

    def done(self, ins):
        ins.then_inc(self.counter.handle, 1)
        self.n += 1
        self.eng.wait_ge(*self.counter.count(self.b, self.n))

    def check(self):
        assert self.n == self.counter.per_seq, (self.n, self.counter.per_seq)


class Scope:

    def __init__(self, nc, tag):
        self.nc, self.tag, self.stack, self.counters, self.sems = nc, tag, ExitStack(), [], []

    def __enter__(self):
        return self

    def __exit__(self, *a):
        with self.nc.Block() as block:
            @block.gpsimd
            def _(pool):
                for handle in self.sems:
                    pool.sem_clear(handle)
        self.stack.close()

    def sb(self, name, shape, dt):
        return self.stack.enter_context(self.nc.sbuf_tensor(f"{self.tag}_{name}", shape, dt))

    def counter(self, name, per_seq):
        self.counters.append(Counter(self.sem(name), per_seq))
        return self.counters[-1]

    def sem(self, name):
        self.sems.append(self.stack.enter_context(self.nc.semaphore(f"{self.tag}_{name}")))
        return self.sems[-1]

    def start_counters(self):
        with self.nc.Block() as block:
            @block.sync
            def _(sp):
                for counter in self.counters:
                    sp.sem_inc(counter.handle, 1)


def three(pe, out, a_hi, a_lo, b_hi, b_lo, first, last):
    pe.matmul(out, a_hi, b_hi, start=first, stop=False, skip_group_check=True)
    pe.matmul(out, a_hi, b_lo, start=False, stop=False, skip_group_check=True)
    return pe.matmul(out, a_lo, b_hi, start=False, stop=last, skip_group_check=True)


def load_and_split(nc, sc, G, pieces):
    flat = []
    for src, hi, lo in pieces:
        p, k, n = src.shape
        cuts = next(c for c in range(-(-n // G.STAGE), n + 1) if n % c == 0)
        width = n // cuts
        step = max(1, G.STAGE // width)
        for k0 in range(0, k, step):
            for c0 in range(0, n, width):
                at = (slice(None), slice(k0, min(k, k0 + step)), slice(c0, c0 + width))
                flat.append((src[at], hi[at], lo[at], p, at[1].stop - k0, width))
    landed = [sc.sem(f"w_landed{i}") for i in range(G.NSTAGE)]
    hi_done, lo_done = sc.sem("w_hi"), sc.sem("w_lo")

    def staged(i, p, k, n):
        return G.stage[0:p, i % G.NSTAGE, 0:k * n].rearrange("p (k n) -> p k n", k=k)

    with nc.Block() as block:
        @block.sync
        def _(sp):
            for i, (src, hi, lo, p, k, n) in enumerate(flat):
                if i >= G.NSTAGE:
                    sp.wait_ge(lo_done, i - G.NSTAGE + 1)
                sp.dma_start(staged(i, p, k, n), src).then_inc(landed[i % G.NSTAGE], 16)

        @block.scalar
        def _(act):
            for i, (src, hi, lo, p, k, n) in enumerate(flat):
                act.wait_ge(landed[i % G.NSTAGE], 16 * (i // G.NSTAGE + 1))
                act.copy(hi, staged(i, p, k, n)).then_inc(hi_done, 1)

        @block.vector
        def _(dve):
            for i, (src, hi, lo, p, k, n) in enumerate(flat):
                dve.wait_ge(hi_done, i + 1)
                dve.tensor_tensor(lo, staged(i, p, k, n), hi, ALU.subtract).then_inc(lo_done, 1)


def kt_view(w):
    return w.rearrange("(k p) n -> p k n", p=P)


def turn_x(pe, b, s, G, xcur, banks):
    pe.wait_ge(*s.xcur_ready.count(b, 16))
    for n in range(NT):
        for k in range(KE):
            last = pe.transpose(banks[n][:, k * P:(k + 1) * P], xcur[:, n, k * P:(k + 1) * P], G.ident[:, :])
        last.then_inc(s.x_turned.handle, 1)


def fetch_x(sp, b, s, G, xcur):
    sp.wait_ge(*s.x_turned.count(b, 0))
    sp.dma_start(xcur[:, :, :], G.x[:, bass.ds(b * NT, NT), :]).then_inc(s.xcur_ready.handle, 16)


def fetch_all_x(sp, s, G, xcur):
    fetch_x(sp, 0, s, G, xcur)
    with sp.Fori(0, B) as b:
        fetch_x(sp, b + 1, s, G, xcur)
    sp.wait_ge(*s.xcur_ready.count(B, 16))


def x_high(act, b, s, xT, banks):
    for n in range(NT):
        act.wait_ge(*s.x_turned.count(b, n + 1))
        act.copy(xT[0][:, :, n * P:(n + 1) * P], banks[n][:, :].rearrange("p (k t) -> p k t", k=KE))\
            .then_inc(s.x_hi.handle, 1)


def x_low(dve, b, s, xT, banks):
    for n in range(NT):
        dve.wait_ge(*s.x_hi.count(b, n + 1))
        at = slice(n * P, (n + 1) * P)
        dve.tensor_tensor(xT[1][:, :, at], banks[n][:, :].rearrange("p (k t) -> p k t", k=KE), xT[0][:, :, at],
                          ALU.subtract).then_inc(s.x_lo.handle, 1)


def x_counters(sc, s):
    s.xcur_ready = sc.counter("xcur_ready", 16)
    s.x_turned = sc.counter("x_turned", NT)
    s.x_hi = sc.counter("x_hi", NT)
    s.x_lo = sc.counter("x_lo", NT)


def add_and_norm(dve, s, b, n, y, y_ready, G, steps, scale=None):
    add_and_measure(dve, s, b, n, y, y_ready, G, steps, scale)
    normalize(dve, s, b, n, G)


def add_and_measure(dve, s, b, n, y, y_ready, G, steps, scale=None):
    dve.wait_ge(*y_ready.count(b, n + 1))
    x_tile = G.x[:, bass.ds(b * NT + n, 1), :]
    y = y.rearrange("p (a e) -> p a e", a=1)
    if scale is None:
        steps.done(dve.tensor_tensor(G.r[:, n:n + 1, :], y, x_tile, ALU.add))
    else:
        steps.done(dve.scalar_tensor_tensor(G.r[:, n:n + 1, :], y, scale, x_tile, ALU.mult, ALU.add))
    steps.done(dve.bn_stats(G.stats[:, n, :], G.r[:, n, :]))
    dve.memset(G.junk[:, :], 0.0)
    steps.done(dve.bn_aggr(G.mv[:, n, :], G.stats[:, n, :]))
    dve.tensor_scalar(G.ve[:, n:n + 1], G.mv[:, n, 1:2], EPS, None, ALU.add).then_inc(s.var_ready.handle, 1)


def normalize(dve, s, b, n, G):
    x_tile = G.x[:, bass.ds(b * NT + n, 1), :]
    dve.wait_ge(*s.rstd_ready.count(b, n + 1))
    dve.tensor_scalar(x_tile, G.r[:, n:n + 1, :], G.mv[:, n, 0:1], G.rstd[:, n:n + 1],
                      ALU.subtract, ALU.mult).then_inc(s.x_done.handle, 1)


LN_STEPS = 3


def rstd_on_pool(pool, s, b, n, G):
    pool.wait_ge(*s.var_ready.count(b, n + 1))
    pool.tensor_tensor(G.rstd[:, n:n + 1], G.ve[:, n:n + 1], G.minus_half[:, 0:1], ALU.pow)\
        .then_inc(s.rstd_ready.handle, 1)


def ln_counters(sc, s):
    s.var_ready = sc.counter("var_ready", NT)
    s.rstd_ready = sc.counter("rstd_ready", NT)
    s.x_done = sc.counter("x_done", NT)


def attn0(nc, G, W):
    H, D = 16, 128
    QC = 4
    HC = H // QC
    NS = 2
    NPB = 3
    with Scope(nc, "a0") as sc:
        wq = [sc.sb(f"wq{i}", [P, KE, H * D], F16) for i in range(2)]
        wkv = [sc.sb(f"wkv{i}", [P, KE, 2 * D], F16) for i in range(2)]
        wgh = [sc.sb(f"wgh{i}", [P, KE, 4 * H], F16) for i in range(2)]
        wo = [sc.sb(f"wo{i}", [P, H, E], F16) for i in range(2)]
        load_and_split(nc, sc, G, [
            (kt_view(W["L0_attn_WqT"]), wq[0][:, :, :], wq[1][:, :, :]),
            (kt_view(W["L0_attn_WkvT"]), wkv[0][:, :, :], wkv[1][:, :, :]),
            (kt_view(W["L0_attn_WhT"]), wgh[0][:, :, :], wgh[1][:, :, :]),
            (kt_view(W["L0_attn_WoutT"]), wo[0][:, :, :], wo[1][:, :, :])])

        xT = [sc.sb(f"xT{i}", [P, KE, N], F16) for i in range(2)]
        qT = [sc.sb(f"qT{i}", [P, H, N], F16) for i in range(2)]
        kT = [sc.sb(f"kT{i}", [P, H, N], F16) for i in range(2)]
        oT = qT
        v = [sc.sb(f"v{i}", [P, NT, D], F16) for i in range(2)]
        xcur = sc.sb("xcur", [P, NT, E], F32)
        rope_q = sc.sb("rope_q", [P, 2, NT, D], F32)
        rope_k = sc.sb("rope_k", [P, 2, NT, D], F32)
        q_cos = sc.sb("q_cos", [P, 1, E], F32)
        q_sin = sc.sb("q_sin", [P, 1, E], F32)
        q_rot = sc.sb("q_rot", [P, 2, E], F32)
        k_part = sc.sb("k_part", [P, 2, D], F32)
        k_rot = sc.sb("k_rot", [P, NT, D], F32)
        kh_rows = sc.sb("kh_rows", [P, 1, H * D], F32)
        g_abs = sc.sb("g_abs", [2 * H, N], F32)
        g_log = sc.sb("g_log", [2 * H, N], F32)
        g_cum = sc.sb("g_cum", [2 * H, N + 1], F32)
        g_fac = sc.sb("g_fac", [2 * H, N], F32)
        kvh = sc.sb("kvh", [2 * H, N], F32)
        kvh_t = sc.sb("kvh_t", [P, NT, 2 * H], F32)
        prob = sc.sb("prob", [P, NPB, NT, N], F32)
        sums = sc.sb("sums", [P, NPB, NT], F32)
        inv = sc.sb("inv", [P, NPB, NT], F32)
        negmax = sc.sb("negmax", [P, NPB, NT], F32)
        pT = [sc.sb(f"pT{i}", [P, 2, NT, N], F16) for i in range(2)]

        NG = 8 + 8 + H
        G_Q, G_K, G_P = 0, 8, 16
        s = Names()
        x_counters(sc, s)
        s.t_ready = sc.counter("t_ready", NG)
        s.t_hi = sc.counter("t_hi", NG)
        s.t_lo = sc.counter("t_lo", NG)
        s.pr_ready = sc.counter("pr_ready", 2 + 8)
        s.pr_free = sc.counter("pr_free", 2 + 8)
        s.v_hi = sc.counter("v_hi", NT)
        s.gates_ready = sc.counter("gates_ready", 1)
        s.g_ln = sc.counter("g_ln", 3)
        s.g_sum = sc.counter("g_sum", 1)
        s.g_exp = sc.counter("g_exp", 1)
        s.kvh_ready = sc.counter("kvh_ready", 1)
        s.kvh_turned = sc.counter("kvh_turned", 1)
        s.kvh_t_ready = sc.counter("kvh_t_ready", 1)
        s.k_rot_ready = sc.counter("k_rot_ready", NT)
        s.kh_ready = sc.counter("kh_ready", 8)
        s.q_parts = sc.counter("q_parts", 8)
        s.q_ready = sc.counter("q_ready", 8)
        s.s_ready = sc.counter("s_ready", H)
        s.m_ready = sc.counter("m_ready", H)
        s.e_ready = sc.counter("e_ready", H)
        s.i_ready = sc.counter("i_ready", H)
        s.p_ready = sc.counter("p_ready", H)
        s.o_ready = sc.counter("o_ready", H)
        s.o_hi = sc.counter("o_hi", H)
        s.o_lo = sc.counter("o_lo", H)
        s.y_ready = sc.counter("y_ready", NT)
        s.chain = sc.counter("chain", NT * 1 + 2 + NT * LN_STEPS)
        ln_counters(sc, s)
        consts = sc.sem("consts")
        SB, Y = G.psS, G.psP

        sc.start_counters()
        with nc.Block() as block:
            @block.sync
            def _(sp):
                sp.dma_start(rope_q[:, :, :, :], W["rope_q"].rearrange("a (n p) d -> p a n d", p=P)).then_inc(consts, 16)
                sp.dma_start(rope_k[:, :, :, :], W["rope_k"].rearrange("a (n p) d -> p a n d", p=P)).then_inc(consts, 16)
                fetch_all_x(sp, s, G, xcur)

            @block.gpsimd
            def _(pool):
                with pool.Fori(0, B) as b:
                    def head_keys(j):
                        n, c = divmod(j, QC)
                        pool.wait_ge(*s.kvh_t_ready.count(b, 1))
                        pool.wait_ge(*s.k_rot_ready.count(b, n + 1))
                        if n:
                            pool.wait_ge(*s.t_ready.count(b, G_K + c + 1))
                        pool.tensor_tensor(
                            kh_rows[:, 0, c * E:(c + 1) * E].rearrange("p (h d) -> p h d", h=HC),
                            k_rot[:, n:n + 1, :].broadcast_to([P, HC, D]),
                            kvh_t[:, n, c * HC:(c + 1) * HC].rearrange("p (h a) -> p h a", a=1)
                            .broadcast_to([P, HC, D]), ALU.mult).then_inc(s.kh_ready.handle, 1)

                    for j in range(8):
                        pool.wait_ge(*s.q_parts.count(b, j + 1))
                        if j >= 2:
                            pool.wait_ge(*s.t_ready.count(b, G_Q + j - 1))
                        pool.tensor_tensor(q_rot[:, j % 2, :], q_cos[:, 0, :], q_sin[:, 0, :], ALU.add)\
                            .then_inc(s.q_ready.handle, 1)
                        if j >= 5:
                            head_keys(j - 5)
                    for j in range(3, 8):
                        head_keys(j)
                    for h in range(H):
                        pool.wait_ge(*s.i_ready.count(b, h + 1))
                        pool.tensor_tensor(prob[:, h % NPB, 0, 0:P], prob[:, h % NPB, 0, 0:P],
                                           inv[:, h % NPB, 0:1].broadcast_to([P, P]), ALU.mult)
                        pool.tensor_tensor(prob[:, h % NPB, 1, :], prob[:, h % NPB, 1, :],
                                           inv[:, h % NPB, 1:2].broadcast_to([P, N]), ALU.mult)\
                            .then_inc(s.p_ready.handle, 1)
                    for n in range(NT):
                        rstd_on_pool(pool, s, b, n, G)

            @block.tensor
            def _(pe):
                def turn(b, g, blocks):
                    pe.wait_ge(*s.t_lo.count(b, g - 1))
                    for out, src in blocks:
                        last = pe.transpose(out, src, G.ident[:, :])
                    last.then_inc(s.t_ready.handle, 1)

                turn_x(pe, 0, s, G, xcur, G.psS)
                with pe.Fori(0, B) as b:
                    pe.wait_ge(*s.x_lo.count(b, NT))
                    for n in range(NT):
                        for k in range(KE):
                            last = three(pe, G.psS[n][:, 0:2 * D], xT[0][:, k, n * P:(n + 1) * P],
                                         xT[1][:, k, n * P:(n + 1) * P], wkv[0][:, k, :], wkv[1][:, k, :],
                                         k == 0, k == KE - 1)
                        last.then_inc(s.pr_ready.handle, 1)
                    for i in range(2):
                        for k in range(KE):
                            last = three(pe, G.psO[0][0:2 * H, i * N:(i + 1) * N],
                                         wgh[0][:, k, i * 2 * H:(i + 1) * 2 * H], wgh[1][:, k, i * 2 * H:(i + 1) * 2 * H],
                                         xT[0][:, k, :], xT[1][:, k, :], k == 0, k == KE - 1)
                    last.then_inc(s.gates_ready.handle, 1)

                    def turn_q(j):
                        pe.wait_ge(*s.q_ready.count(b, j + 1))
                        turn(b, G_Q + j, [(G.psT[j % 2][:, i * P:(i + 1) * P], q_rot[:, j % 2, i * P:(i + 1) * P])
                                          for i in range(HC)])

                    for j in range(8):
                        n, c = divmod(j, QC)
                        if j == 0:
                            pe.wait_ge(*s.x_done.count(b, 0))
                        pe.wait_ge(*s.pr_free.count(b, j + 1))
                        if j == 4:
                            pe.wait_ge(*s.kvh_ready.count(b, 1))
                        for k in range(KE):
                            last = three(pe, G.psP[j % 2][:, :], xT[0][:, k, n * P:(n + 1) * P],
                                         xT[1][:, k, n * P:(n + 1) * P], wq[0][:, k, c * E:(c + 1) * E],
                                         wq[1][:, k, c * E:(c + 1) * E], k == 0, k == KE - 1)
                        last.then_inc(s.pr_ready.handle, 1)
                        if j == 4:
                            for n2 in range(NT):
                                last = pe.transpose(G.psO[1][:, n2 * 2 * H:(n2 + 1) * 2 * H],
                                                    kvh[:, n2 * P:(n2 + 1) * P], G.ident[0:2 * H, 0:2 * H])
                            last.then_inc(s.kvh_turned.handle, 1)
                        if j >= 2:
                            turn_q(j - 2)
                    turn_q(6)
                    turn_q(7)
                    for n in range(NT):
                        for c in range(QC):
                            g = G_K + n * QC + c
                            pe.wait_ge(*s.kh_ready.count(b, n * QC + c + 1))
                            turn(b, g, [(G.psT[g % 2][:, i * P:(i + 1) * P],
                                         kh_rows[:, 0, (c * HC + i) * P:(c * HC + i + 1) * P]) for i in range(HC)])

                    def scores(h):
                        if h >= NS:
                            pe.wait_ge(*s.e_ready.count(b, h - NS + 1))
                        S = SB[h % NS]
                        for n in range(NT):
                            w = (n + 1) * P
                            out = S[:, n * N:n * N + w]
                            three(pe, out, qT[0][:, h, n * P:(n + 1) * P], qT[1][:, h, n * P:(n + 1) * P],
                                  kT[0][:, h, 0:w], kT[1][:, h, 0:w], True, False)
                            last = pe.matmul(S[:, n * N + w - P:n * N + w], G.ident_b[:, :], G.causal[:, :],
                                             start=False, stop=True, skip_group_check=True)
                        last.then_inc(s.s_ready.handle, 1)

                    def turn_p(h):
                        g = G_P + h
                        T = G.psT[g % 2]
                        pe.wait_ge(*s.p_ready.count(b, h + 1))
                        pr = prob[:, h % NPB, :, :]
                        turn(b, g, [(T[:, 0:P], pr[:, 0, 0:P]), (T[:, P:2 * P], pr[:, 1, 0:P]),
                                    (T[:, 3 * P:4 * P], pr[:, 1, P:2 * P])])

                    def pv(h):
                        if h >= 2:
                            pe.wait_ge(*s.o_lo.count(b, h - 1))
                        pe.wait_ge(*s.t_lo.count(b, G_P + h + 1))
                        r = h % 2
                        for m in range(NT):
                            cols = slice(m * P, N)
                            last = three(pe, G.psO[r][:, cols], v[0][:, m, :], v[1][:, m, :],
                                         pT[0][:, r, m, cols], pT[1][:, r, m, cols], m == 0, m == NT - 1)
                        last.then_inc(s.o_ready.handle, 1)

                    def project(h):
                        pe.wait_ge(*s.o_lo.count(b, h + 1))
                        for n in range(NT):
                            last = three(pe, Y[n][:, :], oT[0][:, h, n * P:(n + 1) * P],
                                         oT[1][:, h, n * P:(n + 1) * P], wo[0][:, h, :], wo[1][:, h, :],
                                         h == 0, h == H - 1)
                            if h == H - 1:
                                last.then_inc(s.y_ready.handle, 1)

                    pe.wait_ge(*s.t_lo.count(b, G_P))
                    for i in range(H + 5):
                        if i < H:
                            scores(i)
                        if 2 <= i < H + 2:
                            turn_p(i - 2)
                        if 3 <= i < H + 3:
                            pv(i - 3)
                        if i == H + 2:
                            pe.wait_ge(*s.e_ready.count(b, H))
                            turn_x(pe, b + 1, s, G, xcur, G.psS)
                        if i >= 5:
                            project(i - 5)

            @block.scalar
            def _(act):
                x_high(act, 0, s, xT, G.psS)
                with act.Fori(0, B) as b:
                    for n in range(NT):
                        act.wait_ge(*s.pr_ready.count(b, n + 1))
                        act.copy(v[0][:, n, :], G.psS[n][:, D:2 * D]).then_inc(s.v_hi.handle, 1)
                    act.wait_ge(*s.gates_ready.count(b, 1))
                    act.activation(g_abs[:, :], G.psO[0][0:2 * H, N:2 * N], ACT.Abs).then_inc(s.g_ln.handle, 1)
                    act.wait_ge(*s.g_ln.count(b, 1))
                    act.activation(g_abs[:, :], g_abs[:, :], ACT.Exp, scale=-1.0).then_inc(s.g_ln.handle, 1)
                    act.wait_ge(*s.g_ln.count(b, 2))
                    act.activation(g_log[:, :], g_abs[:, :], ACT.Ln, bias=1.0).then_inc(s.g_ln.handle, 1)
                    act.wait_ge(*s.g_sum.count(b, 1))
                    act.activation(g_fac[:, :], g_cum[:, 0:N], ACT.Exp).then_inc(s.g_exp.handle, 1)

                    def hi_q(j):
                        n, c = divmod(j, QC)
                        act.wait_ge(*s.t_ready.count(b, G_Q + j + 1))
                        act.copy(qT[0][:, c * HC:(c + 1) * HC, n * P:(n + 1) * P],
                                 G.psT[j % 2][:, :].rearrange("p (k t) -> p k t", k=HC)).then_inc(s.t_hi.handle, 1)

                    for j in range(8):
                        hi_q(j)
                    for j in range(8):
                        n, c = divmod(j, QC)
                        act.wait_ge(*s.t_ready.count(b, G_K + j + 1))
                        act.copy(kT[0][:, c * HC:(c + 1) * HC, n * P:(n + 1) * P],
                                 G.psT[j % 2][:, :].rearrange("p (k t) -> p k t", k=HC)).then_inc(s.t_hi.handle, 1)

                    def expo(h):
                        act.wait_ge(*s.m_ready.count(b, h + 1))
                        if h >= NPB:
                            act.wait_ge(*s.t_ready.count(b, G_P + h - NPB + 1))
                        S, r = SB[h % NS], h % NPB
                        act.activation(prob[:, r, 0, 0:P], S[:, 0:P], ACT.Exp, bias=negmax[:, r, 0:1],
                                       accum_out=sums[:, r, 0:1])
                        act.activation(prob[:, r, 1, :], S[:, N:2 * N], ACT.Exp, bias=negmax[:, r, 1:2],
                                       accum_out=sums[:, r, 1:2]).then_inc(s.e_ready.handle, 1)

                    def hi_p(h):
                        T, r = G.psT[(G_P + h) % 2], h % 2
                        act.wait_ge(*s.t_ready.count(b, G_P + h + 1))
                        if h >= 2:
                            act.wait_ge(*s.o_ready.count(b, h - 1))
                        for m in range(NT):
                            last = act.mul(pT[0][:, r, m, m * P:N], T[:, m * N + m * P:(m + 1) * N],
                                           kvh_t[:, m, H + h:H + h + 1])
                        last.then_inc(s.t_hi.handle, 1)

                    def hi_o(h):
                        act.wait_ge(*s.o_ready.count(b, h + 1))
                        act.copy(oT[0][:, h, :], G.psO[h % 2][:, 0:N]).then_inc(s.o_hi.handle, 1)

                    for i in range(H + 3):
                        if 2 <= i < H + 2:
                            hi_p(i - 2)
                        if i < H:
                            expo(i)
                        if i >= 3:
                            hi_o(i - 3)
                    x_high(act, b + 1, s, xT, G.psS)

            @block.vector
            def _(dve):
                dve.memset(g_cum[:, 0:1], 0.0)
                dve.wait_ge(consts, 32)
                x_low(dve, 0, s, xT, G.psS)
                with dve.Fori(0, B) as b:
                    steps = Steps(dve, s.chain, b)

                    def lo(g, out_lo, out_hi, src):
                        dve.wait_ge(*s.t_hi.count(b, g + 1))
                        dve.tensor_tensor(out_lo, src, out_hi, ALU.subtract).then_inc(s.t_lo.handle, 1)

                    for n in range(NT):
                        dve.wait_ge(*s.v_hi.count(b, n + 1))
                        ps = G.psS[n]
                        if n == 0:
                            dve.wait_ge(*s.kh_ready.count(b, 0))
                        dve.tensor_tensor(v[1][:, n, :], ps[:, D:2 * D], v[0][:, n, :], ALU.subtract)
                        dve.tensor_tensor(k_part[:, 0, :], ps[:, 0:D], rope_k[:, 0, n, :], ALU.mult)
                        dve.tensor_tensor(k_part[:, 1, 0:D // 2], ps[:, D // 2:D], rope_k[:, 1, n, 0:D // 2], ALU.mult)
                        steps.done(dve.tensor_tensor(k_part[:, 1, D // 2:D], ps[:, 0:D // 2],
                                                     rope_k[:, 1, n, D // 2:D], ALU.mult))
                        dve.tensor_tensor(k_rot[:, n, :], k_part[:, 0, :], k_part[:, 1, :], ALU.add)\
                            .then_inc(s.k_rot_ready.handle, 1)
                        dve.wait_ge(*s.k_rot_ready.count(b, n + 1))
                        dve.memset(G.junk[:, :], 0.0).then_inc(s.pr_free.handle, 1)
                    dve.wait_ge(*s.g_ln.count(b, 3))
                    steps.done(dve.scalar_tensor_tensor(g_log[:, :], G.psO[0][0:2 * H, N:2 * N], 0.0, g_log[:, :],
                                                        ALU.min, ALU.subtract))
                    dve.tensor_tensor_scan(g_cum[:, 1:N + 1], G.ones[0:2 * H, :], g_log[:, :], 0.0, ALU.mult, ALU.add)\
                        .then_inc(s.g_sum.handle, 1)
                    dve.wait_ge(*s.g_exp.count(b, 1))
                    steps.done(dve.tensor_tensor(g_fac[:, :], G.psO[0][0:2 * H, 0:N], g_fac[:, :], ALU.mult))
                    dve.tensor_tensor_scan(kvh[:, :], G.ones[0:2 * H, :], g_fac[:, :], 0.0, ALU.mult, ALU.add)\
                        .then_inc(s.kvh_ready.handle, 1)

                    def lo_q(j):
                        n, c = divmod(j, QC)
                        at = (slice(None), slice(c * HC, (c + 1) * HC), slice(n * P, (n + 1) * P))
                        lo(G_Q + j, qT[1][at], qT[0][at], G.psT[j % 2][:, :].rearrange("p (k t) -> p k t", k=HC))

                    for j in range(8):
                        n, c = divmod(j, QC)
                        dve.wait_ge(*s.pr_ready.count(b, 2 + j + 1))
                        dve.wait_ge(*s.q_ready.count(b, j))
                        ps = G.psP[j % 2][:, :].rearrange("p (h d) -> p h d", h=HC)
                        cos = q_cos[:, 0, :].rearrange("p (h d) -> p h d", h=HC)
                        sin = q_sin[:, 0, :].rearrange("p (h d) -> p h d", h=HC)
                        dve.tensor_tensor(cos, ps, rope_q[:, 0, n:n + 1, :].broadcast_to([P, HC, D]), ALU.mult)
                        dve.tensor_tensor(sin[:, :, 0:D // 2], ps[:, :, D // 2:D],
                                          rope_q[:, 1, n:n + 1, 0:D // 2].broadcast_to([P, HC, D // 2]), ALU.mult)
                        dve.tensor_tensor(sin[:, :, D // 2:D], ps[:, :, 0:D // 2],
                                          rope_q[:, 1, n:n + 1, D // 2:D].broadcast_to([P, HC, D // 2]), ALU.mult)\
                            .then_inc(s.q_parts.handle, 1)
                        dve.wait_ge(*s.q_parts.count(b, j + 1))
                        dve.memset(G.junk[:, :], 0.0).then_inc(s.pr_free.handle, 1)
                        if j == 4:
                            dve.wait_ge(*s.kvh_turned.count(b, 1))
                            dve.tensor_copy(kvh_t[:, :, :],
                                            G.psO[1][:, 0:NT * 2 * H].rearrange("p (n h) -> p n h", n=NT))\
                                .then_inc(s.kvh_t_ready.handle, 1)
                        if j >= 2:
                            lo_q(j - 2)
                    lo_q(6)
                    lo_q(7)
                    for j in range(8):
                        n, c = divmod(j, QC)
                        at = (slice(None), slice(c * HC, (c + 1) * HC), slice(n * P, (n + 1) * P))
                        lo(G_K + j, kT[1][at], kT[0][at], G.psT[j % 2][:, :].rearrange("p (k t) -> p k t", k=HC))

                    def rowmax(h):
                        S, r = SB[h % NS], h % NPB
                        dve.wait_ge(*s.s_ready.count(b, h + 1))
                        if h >= NPB:
                            dve.wait_ge(*s.e_ready.count(b, h - NPB + 1))
                        dve.tensor_reduce(negmax[:, r, 0:1], S[:, 0:P], X_AXIS, ALU.max, negate=True)
                        dve.tensor_reduce(negmax[:, r, 1:2], S[:, N:2 * N], X_AXIS, ALU.max, negate=True)\
                            .then_inc(s.m_ready.handle, 1)

                    def invert(h):
                        dve.wait_ge(*s.e_ready.count(b, h + 1))
                        if h >= NPB:
                            dve.wait_ge(*s.p_ready.count(b, h - NPB + 1))
                        dve.reciprocal(inv[:, h % NPB, :], sums[:, h % NPB, :]).then_inc(s.i_ready.handle, 1)

                    def lo_p(h):
                        T, r = G.psT[(G_P + h) % 2], h % 2
                        dve.wait_ge(*s.t_hi.count(b, G_P + h + 1))
                        for m in range(NT):
                            last = dve.scalar_tensor_tensor(pT[1][:, r, m, m * P:N], T[:, m * N + m * P:(m + 1) * N],
                                                            kvh_t[:, m, H + h:H + h + 1], pT[0][:, r, m, m * P:N],
                                                            ALU.mult, ALU.subtract)
                        last.then_inc(s.t_lo.handle, 1)

                    def lo_o(h):
                        dve.wait_ge(*s.o_hi.count(b, h + 1))
                        dve.tensor_tensor(oT[1][:, h, :], G.psO[h % 2][:, 0:N], oT[0][:, h, :], ALU.subtract)\
                            .then_inc(s.o_lo.handle, 1)

                    for i in range(H + 3):
                        if i < H:
                            rowmax(i)
                        if 1 <= i <= H:
                            invert(i - 1)
                        if 2 <= i < H + 2:
                            lo_p(i - 2)
                        if i >= 3:
                            lo_o(i - 3)
                    x_low(dve, b + 1, s, xT, G.psS)
                    for n in range(NT):
                        add_and_measure(dve, s, b, n, Y[n][:, :], s.y_ready, G, steps)
                    for n in range(NT):
                        normalize(dve, s, b, n, G)
                    steps.check()


def xattn0_tables(nc, sc, G, W, rope):
    TWO_PI_HI, TWO_PI_LO = 6.28125, 2 * np.pi - 6.28125
    ROUND = float(1.5 * 2 ** 23)
    pos = sc.sb("pos", [P, B * NT, 2], F32)
    ang = sc.sb("ang", [P, 2, B * NT, 8], F32)
    turns = sc.sb("turns", [P, 2, B * NT, 8], F32)
    trig = sc.sb("trig", [P, 2, B * NT, 8], F32)
    landed, step, sin_done = sc.sem("pos_landed"), sc.sem("tab_step"), sc.sem("sin_done")
    with nc.Block() as block:
        @block.sync
        def _(sp):
            sp.dma_start(pos[:, :, :], W["fside"].rearrange("b (n p) a -> p (b n) a", p=P)).then_inc(landed, 16)

        @block.vector
        def _(dve):
            count = 0
            dve.wait_ge(landed, 16)
            for j in range(4):
                out = ang[:, 0, :, :].rearrange("p t (a j) -> p t a j", a=2)[:, :, :, j]
                last = dve.tensor_scalar(out, pos[:, :, :], float(np.float32(10000.0) ** np.float32(-j / 4)), None,
                                         ALU.mult)
            def then(ins):
                nonlocal count
                count += 1
                ins.then_inc(step, 1)
                dve.wait_ge(step, count)
            then(last)
            then(dve.tensor_scalar(ang[:, 1, :, :], ang[:, 0, :, :], float(np.pi / 2), None, ALU.add))
            then(dve.tensor_scalar(turns[:, :, :, :], ang[:, :, :, :], float(1 / (2 * np.pi)), ROUND, ALU.mult, ALU.add))
            then(dve.tensor_scalar(turns[:, :, :, :], turns[:, :, :, :], ROUND, None, ALU.subtract))
            then(dve.scalar_tensor_tensor(ang[:, :, :, :].rearrange("p a t j -> p (a t j)"),
                                          turns[:, :, :, :].rearrange("p a t j -> p (a t j)"), -TWO_PI_HI,
                                          ang[:, :, :, :].rearrange("p a t j -> p (a t j)"), ALU.mult, ALU.add))
            then(dve.scalar_tensor_tensor(ang[:, :, :, :].rearrange("p a t j -> p (a t j)"),
                                          turns[:, :, :, :].rearrange("p a t j -> p (a t j)"), -TWO_PI_LO,
                                          ang[:, :, :, :].rearrange("p a t j -> p (a t j)"), ALU.mult, ALU.add))
            then(dve.tensor_scalar(ang[:, :, :, :], ang[:, :, :, :], float(np.float32(3.1415925)),
                                   float(np.float32(-3.1415925)), ALU.min, ALU.max))
            dve.wait_ge(sin_done, 1)
            for which, scale in ((0, 0.25), (1, 1.0)):
                t = rope[:, which, :, 0:B * NT, :].rearrange("p a t (j e) -> p a t j e", e=2)
                for e in range(2):
                    dve.tensor_scalar(t[:, 0, :, :, e], trig[:, 1, :, :], scale, None, ALU.mult)
                    dve.tensor_scalar(t[:, 1, :, :, e], trig[:, 0, :, :], scale * (2 * e - 1), None, ALU.mult)

        @block.scalar
        def _(act):
            act.wait_ge(step, 7)
            act.activation(trig[:, :, :, :], ang[:, :, :, :], ACT.Sin).then_inc(sin_done, 1)


def small_attention(nc, G, W, tag, H, D, KVH, causal, from_ctx, wq_dram, wkv_dram, wo_dram, bias_dram):
    GD = 4 * D
    HB = P // GD
    QB, KB = H // HB, KVH // HB
    KW = KVH * D
    NS, NPB = 2, 3
    SCALE = float(1.0 / np.sqrt(D))
    KSRC = KC if from_ctx else KE
    with Scope(nc, tag) as sc:
        wq = [sc.sb(f"wq{i}", [P, KE, E], F16) for i in range(2)]
        wkv = [sc.sb(f"wkv{i}", [P, KSRC, 2 * KW], F16) for i in range(2)]
        wo = [sc.sb(f"wo{i}", [P, KE, E], F16) for i in range(2)]
        bias = [sc.sb(f"bias{i}", [1, 1, E], F16) for i in range(2)]
        pieces = [(kt_view(wq_dram), wq[0][:, :, :], wq[1][:, :, :]),
                  (kt_view(wkv_dram), wkv[0][:, :, :], wkv[1][:, :, :]),
                  (kt_view(wo_dram), wo[0][:, :, :], wo[1][:, :, :]),
                  (bias_dram.rearrange("(a k n) -> a k n", a=1, k=1), bias[0][:, :, :], bias[1][:, :, :])]
        if from_ctx:
            cT = [sc.sb(f"cT{i}", [P, KC, (B + 1) * N], F16) for i in range(2)]
            pieces.append((kt_view(W["ctxT"]), cT[0][:, :, 0:B * N], cT[1][:, :, 0:B * N]))
            rope = sc.sb("rope", [P, 2, 2, (B + 1) * NT, D], F32)
        load_and_split(nc, sc, G, pieces)
        if from_ctx:
            xattn0_tables(nc, sc, G, W, rope)

        xT = [sc.sb(f"xT{i}", [P, KE, N], F16) for i in range(2)]
        oT = [sc.sb(f"oT{i}", [P, KE, N], F16) for i in range(2)]
        v = [sc.sb(f"v{i}", [P, NT, KW], F16) for i in range(2)]
        v_next = [sc.sb(f"v_next{i}", [P, NT, KW], F16) for i in range(2)]
        qS = sc.sb("qS", [P, QB, N], F16)
        kS = sc.sb("kS", [P, KB, N], F16)
        q_stack = sc.sb("q_stack", [P, NT, H, 4, D], F16)
        k_stack = sc.sb("k_stack", [P, NT, KVH, 4, D], F16)
        xcur = sc.sb("xcur", [P, NT, E], F32)
        c_part = sc.sb("c_part", [P, E], F32)
        s_part = sc.sb("s_part", [P, E], F32)
        rot = sc.sb("rot", [P, 2, E], F32)
        prob = sc.sb("prob", [P, NPB, NT, N], F32)
        sums = sc.sb("sums", [P, NT, H], F32)
        inv = sc.sb("inv", [P, NT, H], F32)
        negmax = sc.sb("negmax", [P, NPB, NT], F32)
        o_rows = sc.sb("o_rows", [P, NT, E], F32)
        pT = [sc.sb(f"pT{i}", [P, 2, NT, N], F16) for i in range(2)]

        projections = [("q", 0), ("q", 1)] + ([("k", 0), ("v", 0), ("k", 1), ("v", 1)] if from_ctx
                                              else [("kv", 0), ("kv", 1)])
        NP_ = len(projections)
        stacks = [("q", 0), ("q", 1), ("k", 0), ("k", 1)]
        def blocks_of(kind):
            return QB if kind == "q" else KB
        stack_groups = []
        for i, (kind, n) in enumerate(stacks):
            nb = blocks_of(kind)
            for b0 in range(0, nb, 8):
                stack_groups.append((i, kind, n, b0, min(8, nb - b0)))
        NSG = len(stack_groups)
        assert NSG % 2 == 0 and H % 2 == 0
        y_steps = [(n, k) for n in range(NT) for k in range(KE)]
        k_steps = [(i, k) for i, (kind, n) in enumerate(projections) for k in range(KE if kind == "q" else KSRC)]
        OT_HEAD, Y_HEAD, Y_RATE = 1, 3, 32 // H
        y_head = [Y_HEAD + j // Y_RATE for j in range(len(y_steps))]
        LN_HEAD = [y_head[KE * (n + 1) - 1] + 2 for n in range(NT)]
        X_HEAD = LN_HEAD[-1] + 2
        step_head = [X_HEAD + 2 + j // Y_RATE for j in range(len(k_steps))]
        done_head = [max(h for (i, k), h in zip(k_steps, step_head) if i == p) for p in range(len(projections))]
        LOOPS = max(H + 3, done_head[-1] + 3)
        s = Names()
        x_counters(sc, s)
        s.t_ready = sc.counter("t_ready", H)
        s.t_hi = sc.counter("t_hi", H)
        s.t_lo = sc.counter("t_lo", H)
        s.st_turned = sc.counter("st_turned", NSG)
        s.st_even = sc.counter("st_even", NSG // 2)
        s.st_odd = sc.counter("st_odd", NSG // 2)
        s.v_ready = sc.counter("v_ready", 1)
        s.ot_ready = sc.counter("ot_ready", NT)
        s.ot_hi = sc.counter("ot_hi", NT)
        s.ot_lo = sc.counter("ot_lo", NT)
        s.pr_ready = sc.counter("pr_ready", NP_)
        s.pr_hi = sc.counter("pr_hi", NT if from_ctx else NP_)
        s.pr_done = sc.counter("pr_done", NP_)
        s.rot_ready = sc.counter("rot_ready", 4)
        s.rot_hi = sc.counter("rot_hi", 4)
        s.stack_ready = sc.counter("stack_ready", 4)
        s.s_ready = sc.counter("s_ready", H)
        s.m_ready = sc.counter("m_ready", H)
        s.e_ready = sc.counter("e_ready", H)
        s.pv_done = sc.counter("pv_done", H)
        s.o_ready = sc.counter("o_ready", NT)
        s.y_ready = sc.counter("y_ready", NT)
        s.chain = sc.counter("chain", NT * LN_STEPS)
        s.inv_ready = sc.counter("inv_ready", 1)
        ln_counters(sc, s)
        zeroed = sc.sem("zeroed")
        SB, Y = G.psS, G.psP
        TH = [t[:, :].bitcast(F16) for t in G.psT + G.psS]

        def turned_before(i):
            return sum(kind in "qk" for kind, n in projections[:i])

        def tile_at(b, n):
            return bass.ds(b * N + n * P, P)

        sc.start_counters()
        with nc.Block() as block:
            @block.sync
            def _(sp):
                fetch_all_x(sp, s, G, xcur)

            @block.gpsimd
            def _(pool):
                if from_ctx:
                    for part in cT:
                        pool.memset(part[:, :, B * N:(B + 1) * N], 0.0)
                    for which in range(2):
                        pool.memset(rope[:, which, :, B * NT:(B + 1) * NT, :], 0.0)
                pool.memset(q_stack[:, :, :, 3, :], 0.0)
                pool.memset(k_stack[:, :, :, 3, :], 0.0).then_inc(zeroed, 1)

                def rotate(b):
                    of_proj = {"q": [0, 1], "k": [2, 4]}
                    for i, (kind, n) in enumerate(stacks):
                        pool.wait_ge(*s.pr_done.count(b, of_proj[kind][n] + 1))
                        pool.tensor_tensor(rot[:, i % 2, :], c_part[:, :], s_part[:, :], ALU.add)\
                            .then_inc(s.rot_ready.handle, 1)
                        st, at = (q_stack, 1) if kind == "q" else (k_stack, 2)
                        pool.wait_ge(*s.rot_hi.count(b, i + 1))
                        pool.tensor_tensor(st[:, n, :, at, :], rot[:, i % 2, :].rearrange("p (h d) -> p h d", d=D),
                                           st[:, n, :, 0, :], ALU.subtract).then_inc(s.stack_ready.handle, 1)

                def tail(b):
                    for n in range(NT):
                        rstd_on_pool(pool, s, b, n, G)

                if from_ctx:
                    rotate(0)
                    rotate(1)
                with pool.Fori(0, B - 1) as b:
                    tail(b)
                    if from_ctx:
                        rotate(b + 2)
                tail(B - 1)

            @block.tensor
            def _(pe):
                def project(b, i, k):
                    kind, n = projections[i]
                    if k == 0 and i >= 2:
                        pe.wait_ge(*s.pr_done.count(b, i - 1))
                    if k == 0 and i < 2:
                        pe.wait_ge(*s.x_lo.count(b, NT))
                    a, at = xT, slice(n * P, (n + 1) * P)
                    if kind == "q":
                        w, cols, K = wq, slice(0, E), KE
                    else:
                        w, K = wkv, KSRC
                        cols = {"k": slice(0, KW), "v": slice(KW, 2 * KW), "kv": slice(0, 2 * KW)}[kind]
                        if from_ctx:
                            a, at = cT, tile_at(b, n)
                    width = cols.stop - cols.start
                    last = three(pe, G.psP[i % 2][:, 0:width], a[0][:, k, at], a[1][:, k, at],
                                 w[0][:, k, cols], w[1][:, k, cols], k == 0, k == K - 1)
                    if k == K - 1:
                        last.then_inc(s.pr_ready.handle, 1)

                def turn_stacks(b):
                    for g, (i, kind, n, b0, nb) in enumerate(stack_groups):
                        st = q_stack if kind == "q" else k_stack
                        flat = st[:, n, :, :, :].rearrange("p h a d -> p (h a d)")
                        pe.wait_ge(*(s.stack_ready if from_ctx else s.pr_done).count(b, i + 1))
                        if g >= 4:
                            pe.wait_ge(*(s.st_odd if g % 2 else s.st_even).count(b, g // 2 - 1))
                        for j in range(nb):
                            last = pe.transpose(TH[g % 4][:, j * P:(j + 1) * P], flat[:, (b0 + j) * P:(b0 + j + 1) * P],
                                                G.ident_h[:, :])
                        last.then_inc(s.st_turned.handle, 1)

                def turn_o(b):
                    for n in range(NT):
                        for k in range(KE):
                            last = pe.transpose(G.psP[n][:, k * P:(k + 1) * P], o_rows[:, n, k * P:(k + 1) * P],
                                                G.ident[:, :])
                        last.then_inc(s.ot_ready.handle, 1)

                def output(b, n, k):
                    if k == 0:
                        pe.wait_ge(*s.ot_lo.count(b, NT))
                    three(pe, Y[n][:, :], oT[0][:, k, n * P:(n + 1) * P],
                          oT[1][:, k, n * P:(n + 1) * P], wo[0][:, k, :], wo[1][:, k, :], k == 0, False)
                    if k == KE - 1:
                        pe.matmul(Y[n][:, :], G.ones_h[0:1, :], bias[0][0:1, 0, :], start=False, stop=False,
                                  skip_group_check=True)
                        pe.matmul(Y[n][:, :], G.ones_h[0:1, :], bias[1][0:1, 0, :], start=False, stop=True,
                                  skip_group_check=True).then_inc(s.y_ready.handle, 1)

                def heads(b, tail, front):
                    def scores(h):
                        pe.wait_ge(*s.e_ready.count(b, h - NS + 1))
                        S = SB[h % NS]
                        hk = h * KVH // H
                        base, kbase = (h % HB) * GD, (hk % HB) * GD
                        assert base == kbase
                        for n in range(NT):
                            w = (n + 1) * P if causal else N
                            last = pe.matmul(S[:, n * N:n * N + w], qS[base:base + GD, h // HB, n * P:(n + 1) * P],
                                             kS[base:base + GD, hk // HB, 0:w], start=True, stop=not causal,
                                             skip_group_check=True)
                            if causal:
                                last = pe.matmul(S[:, n * N + w - P:n * N + w], G.ident_b[:, :], G.causal[:, :],
                                                 start=False, stop=True, skip_group_check=True)
                        last.then_inc(s.s_ready.handle, 1)

                    def turn_p(h):
                        T = G.psT[h % 2]
                        pe.wait_ge(*s.e_ready.count(b, h + 1))
                        if h >= 2:
                            pe.wait_ge(*s.t_lo.count(b, h - 1))
                        pr = prob[:, h % NPB, :, :]
                        for m in range(NT):
                            for n in range(m if causal else 0, NT):
                                last = pe.transpose(T[:, m * N + n * P:m * N + (n + 1) * P],
                                                    pr[:, n, m * P:(m + 1) * P], G.ident[:, :])
                        last.then_inc(s.t_ready.handle, 1)

                    def pv(h):
                        pe.wait_ge(*s.t_lo.count(b, h + 1))
                        hk, r = h * KVH // H, h % 2
                        for n in range(NT):
                            ms = range(n + 1 if causal else NT)
                            for m in ms:
                                last = three(pe, G.psO[n][:, h * D:(h + 1) * D], pT[0][:, r, m, n * P:(n + 1) * P],
                                             pT[1][:, r, m, n * P:(n + 1) * P], v[0][:, m, hk * D:(hk + 1) * D],
                                             v[1][:, m, hk * D:(hk + 1) * D], m == 0, m == ms[-1])
                        last.then_inc(s.pv_done.handle, 1)

                    pe.wait_ge(*s.st_even.count(b, NSG // 2))
                    pe.wait_ge(*s.st_odd.count(b, NSG // 2))
                    for i in range(LOOPS):
                        if i < H:
                            scores(i)
                        if 2 <= i < H + 2:
                            turn_p(i - 2)
                        if i == 3:
                            pe.wait_ge(*s.v_ready.count(b, 1))
                            pe.wait_ge(*s.o_ready.count(b, 0))
                        if 3 <= i < H + 3:
                            pv(i - 3)
                        if tail is not None:
                            if i == OT_HEAD:
                                pe.wait_ge(*s.o_ready.count(b, 0))
                                pe.wait_ge(*s.pr_done.count(b, NP_))
                                turn_o(tail)
                            for (n, k), head in zip(y_steps, y_head):
                                if i == head:
                                    output(tail, n, k)
                        if i == X_HEAD:
                            pe.wait_ge(*s.x_done.count(b, 0))
                            pe.wait_ge(*s.pr_done.count(b, NP_))
                            turn_x(pe, front, s, G, xcur, G.psP)
                        for (p, k), head in zip(k_steps, step_head):
                            if i == head:
                                project(front, p, k)
                    turn_stacks(front)

                pe.wait_ge(zeroed, 1)
                turn_x(pe, 0, s, G, xcur, G.psP)
                for i, k in k_steps:
                    project(0, i, k)
                turn_stacks(0)
                heads(0, None, 1)
                with pe.Fori(0, B - 1) as b:
                    heads(b + 1, b, b + 2)
                pe.wait_ge(*s.o_ready.count(B, 0))
                pe.wait_ge(*s.pr_done.count(B, NP_))
                turn_o(B - 1)
                for n, k in y_steps:
                    output(B - 1, n, k)

            @block.scalar
            def _(act):
                def stack_hi(kind, n, src, scale):
                    heads = H if kind == "q" else KVH
                    out = q_stack[:, n, :, 0:3:2, :] if kind == "q" else k_stack[:, n, :, 0:2, :]
                    view = src.rearrange("p (h a d) -> p h a d", a=1, d=D)
                    for a in range(2):
                        last = act.mul(out[:, :, a, :], view[:, :, 0, :], scale)
                    return last

                def high_of(b, i):
                    kind, n = projections[i]
                    if from_ctx and kind in "qk":
                        st = turned_before(i)
                        act.wait_ge(*s.rot_ready.count(b, st + 1))
                        stack_hi(kind, n, rot[:, st % 2, :], 1.0).then_inc(s.rot_hi.handle, 1)
                        return
                    act.wait_ge(*s.pr_ready.count(b, i + 1))
                    act.wait_ge(*s.v_ready.count(b, 0))
                    ps = G.psP[i % 2]
                    if kind == "q":
                        last = stack_hi("q", n, ps[:, :], SCALE)
                    elif kind == "v":
                        last = act.copy(v_next[0][:, n, :], ps[:, 0:KW])
                    else:
                        stack_hi("k", n, ps[:, 0:KW], 1.0)
                        last = act.copy(v_next[0][:, n, :], ps[:, KW:2 * KW])
                    last.then_inc(s.pr_hi.handle, 1)

                def copy_odd(b):
                    for g in range(1, NSG, 2):
                        i, kind, n, b0, nb = stack_groups[g]
                        out = qS if kind == "q" else kS
                        act.wait_ge(*s.st_turned.count(b, g + 1))
                        act.copy(out[:, b0:b0 + nb, n * P:(n + 1) * P],
                                 TH[g % 4][:, 0:nb * P].rearrange("p (k t) -> p k t", k=nb)).then_inc(s.st_odd.handle, 1)

                def high_of_o(b):
                    for n in range(NT):
                        act.wait_ge(*s.ot_ready.count(b, n + 1))
                        act.copy(oT[0][:, :, n * P:(n + 1) * P], G.psP[n][:, :].rearrange("p (k t) -> p k t", k=KE))\
                            .then_inc(s.ot_hi.handle, 1)

                def heads(b, tail, front):
                    def expo(h):
                        act.wait_ge(*s.m_ready.count(b, h + 1))
                        if h >= NPB:
                            act.wait_ge(*s.t_ready.count(b, h - NPB + 1))
                        S, r = SB[h % NS], h % NPB
                        for n in range(NT):
                            w = (n + 1) * P if causal else N
                            last = act.activation(prob[:, r, n, 0:w], S[:, n * N:n * N + w], ACT.Exp,
                                                  bias=negmax[:, r, n:n + 1], accum_out=sums[:, n, h:h + 1])
                        last.then_inc(s.e_ready.handle, 1)

                    def hi_p(h):
                        T, r = G.psT[h % 2], h % 2
                        act.wait_ge(*s.t_ready.count(b, h + 1))
                        if h >= 2:
                            act.wait_ge(*s.pv_done.count(b, h - 1))
                        if causal:
                            act.copy(pT[0][:, r, 0, :], T[:, 0:N])
                            last = act.copy(pT[0][:, r, 1, P:N], T[:, N + P:2 * N])
                        else:
                            last = act.copy(pT[0][:, r, :, :], T[:, :].rearrange("p (m n) -> p m n", m=NT))
                        last.then_inc(s.t_hi.handle, 1)

                    for i in range(LOOPS):
                        if 2 <= i < H + 2:
                            hi_p(i - 2)
                        if i < H:
                            expo(i)
                        if i == OT_HEAD and tail is not None:
                            high_of_o(tail)
                        if i == X_HEAD:
                            x_high(act, front, s, xT, G.psP)
                        for p in range(NP_):
                            if i == done_head[p] + (2 if from_ctx and projections[p][0] != "v" else 1):
                                high_of(front, p)
                    copy_odd(front)

                x_high(act, 0, s, xT, G.psP)
                for i in range(NP_):
                    high_of(0, i)
                copy_odd(0)
                heads(0, None, 1)
                with act.Fori(0, B - 1) as b:
                    heads(b + 1, b, b + 2)
                high_of_o(B - 1)

            @block.vector
            def _(dve):
                def low_of(b, i):
                    kind, n = projections[i]
                    ps = G.psP[i % 2]
                    if from_ctx and kind in "qk":
                        which = 0 if kind == "q" else 1
                        dve.wait_ge(*s.pr_ready.count(b, i + 1))
                        dve.wait_ge(*s.rot_ready.count(b, turned_before(i)))
                        tab = rope[:, which, :, bass.ds(b * NT + n, 1), :]
                        dve.tensor_tensor(c_part[:, :].rearrange("p (h d) -> p h d", d=D),
                                          ps[:, :].rearrange("p (h d) -> p h d", d=D),
                                          tab[:, 0, :, :].broadcast_to([P, H, D]), ALU.mult)
                        pairs = ps[:, :].rearrange("p (h j e) -> p h j e", j=D // 2, e=2)
                        out = s_part[:, :].rearrange("p (h j e) -> p h j e", j=D // 2, e=2)
                        sin = tab[:, 1, :, :].rearrange("p a (j e) -> p a j e", e=2)
                        for e in range(2):
                            last = dve.tensor_tensor(out[:, :, :, e], pairs[:, :, :, 1 - e],
                                                     sin[:, :, :, e].broadcast_to([P, H, D // 2]), ALU.mult)
                        last.then_inc(s.pr_done.handle, 1)
                        return
                    dve.wait_ge(*s.pr_hi.count(b, i + 1 - (turned_before(i) if from_ctx else 0)))
                    dve.wait_ge(*s.v_ready.count(b, 0))
                    view = ps[:, :].rearrange("p (h d) -> p h d", d=D)
                    if kind == "q":
                        dve.scalar_tensor_tensor(q_stack[:, n, :, 1, :], view, SCALE, q_stack[:, n, :, 0, :],
                                                 ALU.mult, ALU.subtract).then_inc(s.pr_done.handle, 1)
                    elif kind == "v":
                        dve.tensor_tensor(v_next[1][:, n, :], ps[:, 0:KW], v_next[0][:, n, :], ALU.subtract)\
                            .then_inc(s.pr_done.handle, 1)
                    else:
                        dve.tensor_tensor(v_next[1][:, n, :], ps[:, KW:2 * KW], v_next[0][:, n, :], ALU.subtract)
                        dve.tensor_tensor(k_stack[:, n, :, 2, :], view[:, 0:KVH, :], k_stack[:, n, :, 0, :],
                                          ALU.subtract).then_inc(s.pr_done.handle, 1)

                def copy_even(b):
                    for g in range(0, NSG, 2):
                        i, kind, n, b0, nb = stack_groups[g]
                        out = qS if kind == "q" else kS
                        dve.wait_ge(*s.st_turned.count(b, g + 1))
                        dve.tensor_copy(out[:, b0:b0 + nb, n * P:(n + 1) * P],
                                        TH[g % 4][:, 0:nb * P].rearrange("p (k t) -> p k t", k=nb))\
                            .then_inc(s.st_even.handle, 1)

                def copy_v(b):
                    dve.wait_ge(*s.pr_done.count(b, NP_))
                    dve.tensor_copy(v[0][:, :, :], v_next[0][:, :, :])
                    dve.tensor_copy(v[1][:, :, :], v_next[1][:, :, :]).then_inc(s.v_ready.handle, 1)

                def low_of_o(b):
                    for n in range(NT):
                        dve.wait_ge(*s.ot_hi.count(b, n + 1))
                        at = slice(n * P, (n + 1) * P)
                        dve.tensor_tensor(oT[1][:, :, at], G.psP[n][:, :].rearrange("p (k t) -> p k t", k=KE),
                                          oT[0][:, :, at], ALU.subtract).then_inc(s.ot_lo.handle, 1)

                def heads(b, tail, front):
                    def rowmax(h):
                        S, r = SB[h % NS], h % NPB
                        dve.wait_ge(*s.s_ready.count(b, h + 1))
                        if h >= NPB:
                            dve.wait_ge(*s.e_ready.count(b, h - NPB + 1))
                        if causal:
                            dve.tensor_reduce(negmax[:, r, 0:1], S[:, 0:P], X_AXIS, ALU.max, negate=True)
                            last = dve.tensor_reduce(negmax[:, r, 1:2], S[:, N:2 * N], X_AXIS, ALU.max, negate=True)
                        else:
                            last = dve.tensor_reduce(negmax[:, r, :], S[:, :].rearrange("p (n m) -> p n m", n=NT),
                                                     X_AXIS, ALU.max, negate=True)
                        last.then_inc(s.m_ready.handle, 1)

                    def lo_p(h):
                        T, r = G.psT[h % 2], h % 2
                        dve.wait_ge(*s.t_hi.count(b, h + 1))
                        if causal:
                            dve.tensor_tensor(pT[1][:, r, 0, :], T[:, 0:N], pT[0][:, r, 0, :], ALU.subtract)
                            last = dve.tensor_tensor(pT[1][:, r, 1, P:N], T[:, N + P:2 * N], pT[0][:, r, 1, P:N],
                                                     ALU.subtract)
                        else:
                            last = dve.tensor_tensor(pT[1][:, r, :, :], T[:, :].rearrange("p (m n) -> p m n", m=NT),
                                                     pT[0][:, r, :, :], ALU.subtract)
                        last.then_inc(s.t_lo.handle, 1)

                    steps = Steps(dve, s.chain, tail)
                    for i in range(LOOPS):
                        if i < H:
                            rowmax(i)
                        if 2 <= i < H + 2:
                            lo_p(i - 2)
                        if tail is not None:
                            if i == OT_HEAD + 1:
                                low_of_o(tail)
                            for n in range(NT):
                                if i == LN_HEAD[n]:
                                    add_and_measure(dve, s, tail, n, Y[n][:, :], s.y_ready, G, steps)
                                if i == LN_HEAD[n] + 1:
                                    normalize(dve, s, tail, n, G)
                        if i == X_HEAD + 1:
                            x_low(dve, front, s, xT, G.psP)
                        for p in range(NP_):
                            if i == done_head[p] + (1 if from_ctx and projections[p][0] != "v" else 2):
                                low_of(front, p)
                        if i == H:
                            dve.wait_ge(*s.e_ready.count(b, H))
                            dve.reciprocal(inv[:, :, :], sums[:, :, :]).then_inc(s.inv_ready.handle, 1)
                    copy_even(front)
                    dve.wait_ge(*s.inv_ready.count(b, 1))
                    dve.wait_ge(*s.pv_done.count(b, H))
                    for n in range(NT):
                        dve.tensor_tensor(o_rows[:, n, :].rearrange("p (h d) -> p h d", d=D),
                                          G.psO[n][:, :].rearrange("p (h d) -> p h d", d=D),
                                          inv[:, n, :].rearrange("p (h a) -> p h a", a=1).broadcast_to([P, H, D]),
                                          ALU.mult).then_inc(s.o_ready.handle, 1)
                    copy_v(front)

                dve.wait_ge(zeroed, 1)
                x_low(dve, 0, s, xT, G.psP)
                for i in range(NP_):
                    low_of(0, i)
                copy_even(0)
                copy_v(0)
                heads(0, None, 1)
                with dve.Fori(0, B - 1) as b:
                    heads(b + 1, b, b + 2)
                low_of_o(B - 1)
                steps = Steps(dve, s.chain, B - 1)
                for n in range(NT):
                    add_and_norm(dve, s, B - 1, n, Y[n][:, :], s.y_ready, G, steps)
                steps.check()


def xattn0(nc, G, W):
    small_attention(nc, G, W, "c0", 32, 16, 32, False, True, W["L0_xattn_Wq"], W["L0_xattn_Wkv"], W["L0_xattn_Wout"],
                    W["L0_xattn_bout"])


def attn1(nc, G, W):
    small_attention(nc, G, W, "a1", 16, 32, 4, True, False, W["L1_attn_Wq"], W["L1_attn_Wkv"], W["L1_attn_Wo"], W["L1_attn_bo"])


def ffn0(nc, G, W):
    HID = 1408
    TH_ = HID // P
    NE, R = 8, 16
    NU = 4
    with Scope(nc, "f0") as sc:
        def pair(name, shape):
            return [sc.sb(f"{name}{i}", shape, F16) for i in range(2)]

        wug = pair("wug", [P, KE, 2 * HID])
        wA = pair("wA", [P, KE, 2 * P])
        wB = pair("wB", [P, 1, 2 * HID])
        wd = pair("wd", [P, TH_, E])
        dA = pair("dA", [P, TH_, P])
        dB = pair("dB", [P, 1, E])
        wr = pair("wr", [P, KE, NE])
        load_and_split(nc, sc, G, [(kt_view(d), w[0][:, :, :], w[1][:, :, :]) for d, w in (
            (W["f0_up_gateT"], wug), (W["f0_A"], wA), (W["f0_B"], wB), (W["f0_downT"], wd), (W["f0_dA"], dA), (W["f0_dB"], dB),
            (W["f0_router"], wr))])

        xT = pair("xT", [P, KE, N])
        xcur = sc.sb("xcur", [P, NT, E], F32)
        expert_of = sc.sb("expert_of", [P, P], F32)
        row_pick = sc.sb("row_pick", [2, 2, P], F16)
        logits = sc.sb("logits", [P, NT, NE], F32)
        top = sc.sb("top", [P, NT, 8], F32)
        top_at = sc.sb("top_at", [P, NT, 8], U32)
        top_f = sc.sb("top_f", [P, NT, 8], F32)
        picked = sc.sb("picked", [P, 2, NT, P], F16)
        mask = sc.sb("mask", [P, 2, N], F16)
        dmask = sc.sb("dmask", [P, N], F16)
        wneg = sc.sb("wneg", [2, 1], F32)
        wexp = sc.sb("wexp", [2, N], F32)
        wsum = sc.sb("wsum", [2, 1], F32)
        winv = sc.sb("winv", [2, 1], F32)
        wts = pair("wts", [2, N])
        c = sc.sb("c", [P, 2, N], F32)
        act_a = sc.sb("act_a", [P, 2, N], F32)
        am = sc.sb("am", [P, 2, 2, N], F32)
        a_part = pair("a_part", [P, 2, 2, N])
        sil = sc.sb("sil", [P, 2, 2, N], F32)
        h = sc.sb("h", [P, 2, 2, N], F32)
        ch = sc.sb("ch", [P, 2, 3, N], F32)
        chs = pair("chs", [P, 2, 3, N])
        zm = sc.sb("zm", [P, 2, N], F32)
        zs = pair("zs", [P, N])

        U = [G.psS[0], G.psS[1], G.psP[1], G.psP[0]]
        Z, Y = G.psO[1], G.psT
        TM = G.psP[0][:, :].bitcast(F16)
        s = Names()
        x_counters(sc, s)
        s.logits_ready = sc.counter("logits_ready", 1)
        s.a_ready = sc.counter("a_ready", 1)
        s.top_ready = sc.counter("top_ready", 1)
        s.top_turned = sc.counter("top_turned", 1)
        s.wneg_ready = sc.counter("wneg_ready", 1)
        s.wexp_ready = sc.counter("wexp_ready", 1)
        s.wts_ready = sc.counter("wts_ready", 1)
        s.c_wide = sc.counter("c_wide", 1)
        s.c_ready = sc.counter("c_ready", 1)
        s.picked_ready = sc.counter("picked_ready", 1)
        s.mask_turned = sc.counter("mask_turned", 1)
        s.mask_ready = sc.counter("mask_ready", 1)
        s.act_a_ready = sc.counter("act_a_ready", 1)
        s.a_split0 = sc.counter("a_split0", 1)
        s.a_split1 = sc.counter("a_split1", 1)
        s.base_ready = sc.counter("base_ready", TH_)
        s.delta_ready = sc.counter("delta_ready", TH_)
        s.sil0 = sc.counter("sil0", TH_)
        s.sil1 = sc.counter("sil1", TH_)
        s.h0 = sc.counter("h0", TH_)
        s.h1 = sc.counter("h1", TH_)
        s.ch_ready = sc.counter("ch_ready", TH_)
        s.ch_hi = sc.counter("ch_hi", TH_)
        s.ch_lo = sc.counter("ch_lo", TH_)
        s.down_done = sc.counter("down_done", TH_)
        s.z_ready = sc.counter("z_ready", 1)
        s.z_parts = sc.counter("z_parts", 1)
        s.y_ready = sc.counter("y_ready", NT)
        s.chain = sc.counter("chain", 1 + 2 * NT + 2 + 3 + 3 + NT * LN_STEPS)
        s.pool_chain = sc.counter("pool_chain", 1 + TH_)
        ln_counters(sc, s)
        consts = sc.sem("consts")
        sc.start_counters()

        with nc.Block() as block:
            @block.sync
            def _(sp):
                sp.dma_start(expert_of[:, :], W["expert_of"]).then_inc(consts, 16)
                sp.dma_start(row_pick[:, :, :], W["row_pick"]).then_inc(consts, 16)
                fetch_all_x(sp, s, G, xcur)

            @block.gpsimd
            def _(pool):
                with pool.Fori(0, B) as b:
                    steps = Steps(pool, s.pool_chain, b)
                    pool.wait_ge(*s.act_a_ready.count(b, 1))
                    pool.wait_ge(*s.mask_ready.count(b, 1))
                    m = mask[:, 0:1, :].broadcast_to([P, 2, N])
                    pool.tensor_tensor(am[:, 0, :, :], act_a[:, :, :], m, ALU.mult)
                    steps.done(pool.tensor_tensor(a_part[0][:, 0, :, :], act_a[:, :, :], m, ALU.mult))
                    pool.tensor_tensor(a_part[1][:, 0, :, :], am[:, 0, :, :], a_part[0][:, 0, :, :], ALU.subtract)\
                        .then_inc(s.a_split0.handle, 1)
                    pool.wait_ge(*s.c_ready.count(b, 1))
                    for t in range(TH_):
                        r = t % 2
                        pool.wait_ge(*s.ch_lo.count(b, t - 1))
                        pool.wait_ge(*s.h0.count(b, t + 1))
                        pool.tensor_tensor(ch[:, r, 0, :], h[:, 0, r, :], c[:, 0, :], ALU.mult)
                        pool.wait_ge(*s.h1.count(b, t + 1))
                        steps.done(pool.tensor_tensor(ch[:, r, 1, :], h[:, 1, r, :], c[:, 1, :], ALU.mult))
                        pool.tensor_tensor(ch[:, r, 2, :], ch[:, r, 0, :], ch[:, r, 1, :], ALU.add)\
                            .then_inc(s.ch_ready.handle, 1)
                    steps.check()
                    for n in range(NT):
                        rstd_on_pool(pool, s, b, n, G)

            @block.tensor
            def _(pe):
                turn_x(pe, 0, s, G, xcur, G.psS)
                with pe.Fori(0, B) as b:
                    def base(t):
                        for u in range(2):
                            cols = slice(u * HID + t * P, u * HID + (t + 1) * P)
                            for k in range(KE):
                                three(pe, U[t % NU][:, u * N:(u + 1) * N], wug[0][:, k, cols], wug[1][:, k, cols],
                                      xT[0][:, k, :], xT[1][:, k, :], k == 0 and u == 0, False)

                    def low_rank(t, i):
                        for u in range(2):
                            cols = slice(u * HID + t * P, u * HID + (t + 1) * P)
                            last = three(pe, U[t % NU][:, u * N:(u + 1) * N], wB[0][:, 0, cols], wB[1][:, 0, cols],
                                         a_part[0][:, i, u, :], a_part[1][:, i, u, :], False, True)
                        return last

                    pe.wait_ge(*s.x_lo.count(b, NT))
                    for n in range(NT):
                        at = slice(n * P, (n + 1) * P)
                        for k in range(KE):
                            three(pe, G.psP[0][:, n * NE:(n + 1) * NE], xT[0][:, k, at], xT[1][:, k, at],
                                  wr[0][:, k, :], wr[1][:, k, :], k == 0, False)
                            last = pe.matmul(G.psP[0][:, n * NE:(n + 1) * NE], xT[1][:, k, at], wr[1][:, k, :],
                                             start=False, stop=k == KE - 1, skip_group_check=True)
                    last.then_inc(s.logits_ready.handle, 1)
                    for u in range(2):
                        for k in range(KE):
                            last = three(pe, G.psP[1][:, u * N:(u + 1) * N], wA[0][:, k, u * P:(u + 1) * P],
                                         wA[1][:, k, u * P:(u + 1) * P], xT[0][:, k, :], xT[1][:, k, :],
                                         k == 0, k == KE - 1)
                    last.then_inc(s.a_ready.handle, 1)
                    base(0)
                    pe.wait_ge(*s.top_ready.count(b, 1))
                    pe.matmul(G.psO[1][:, 0:NE], G.ident_h[:, :], G.ident_h[:, 0:NE], start=True, stop=True)
                    for n in range(NT):
                        last = pe.transpose(G.psO[0][0:2, n * P:(n + 1) * P], top[:, n, 0:2], G.ident[:, :])
                    last.then_inc(s.top_turned.handle, 1)
                    base(1)
                    pe.wait_ge(*s.picked_ready.count(b, 1))
                    for j in range(2):
                        for n in range(NT):
                            last = pe.transpose(TM[:, (j * NT + n) * P:(j * NT + n + 1) * P], picked[:, j, n, :],
                                                G.ident_h[:, :])
                    last.then_inc(s.mask_turned.handle, 1)
                    pe.wait_ge(*s.act_a_ready.count(b, 1))
                    base(2)
                    pe.wait_ge(*s.mask_ready.count(b, 1))
                    base(3)
                    pe.wait_ge(*s.a_split0.count(b, 1))
                    for i in range(TH_ + 3):
                        if i < TH_:
                            low_rank(i, 0).then_inc(s.base_ready.handle, 1)
                        if i == 1:
                            pe.wait_ge(*s.a_split1.count(b, 1))
                        if 1 <= i <= TH_:
                            pe.wait_ge(*s.h0.count(b, i))
                            low_rank(i - 1, 1).then_inc(s.delta_ready.handle, 1)
                        if i == 1:
                            pe.wait_ge(*s.wts_ready.count(b, 1))
                            pe.matmul(G.psO[1][:, 0:NE], G.ident_h[:, :], G.ident_h[:, 0:NE], start=True, stop=True)
                            for j in range(2):
                                for part in range(2):
                                    last = pe.matmul(G.psO[1][:, j * N:(j + 1) * N], row_pick[:, j, :],
                                                     wts[part][:, :], start=part == 0, stop=part == 1,
                                                     skip_group_check=True)
                            last.then_inc(s.c_wide.handle, 1)
                        if i >= 2 and i + 2 < TH_:
                            pe.wait_ge(*s.h1.count(b, i - 1))
                            base(i + 2)
                        if i == TH_ + 2:
                            pe.wait_ge(*s.h1.count(b, TH_))
                            turn_x(pe, b + 1, s, G, xcur, G.psS)
                        if i == 3:
                            pe.wait_ge(*s.c_ready.count(b, 1))
                            pe.wait_ge(*s.x_done.count(b, 0))
                        if i >= 3:
                            t = i - 3
                            pe.wait_ge(*s.ch_lo.count(b, t + 1))
                            for j in range(2):
                                last = three(pe, Z[:, j * N:(j + 1) * N], dA[0][:, t, :], dA[1][:, t, :],
                                             chs[0][:, t % 2, j, :], chs[1][:, t % 2, j, :], t == 0 and j == 0,
                                             t == TH_ - 1)
                            if t == TH_ - 1:
                                last.then_inc(s.z_ready.handle, 1)
                            for n in range(NT):
                                at = slice(n * P, (n + 1) * P)
                                last = three(pe, Y[n][:, :], chs[0][:, t % 2, 2, at], chs[1][:, t % 2, 2, at],
                                             wd[0][:, t, :], wd[1][:, t, :], t == 0, False)
                            last.then_inc(s.down_done.handle, 1)
                    pe.wait_ge(*s.z_parts.count(b, 1))
                    for n in range(NT):
                        at = slice(n * P, (n + 1) * P)
                        three(pe, Y[n][:, :], zs[0][:, at], zs[1][:, at], dB[0][:, 0, :], dB[1][:, 0, :], False, True)\
                            .then_inc(s.y_ready.handle, 1)

            @block.scalar
            def _(act):
                x_high(act, 0, s, xT, G.psS)
                with act.Fori(0, B) as b:
                    act.wait_ge(*s.a_ready.count(b, 1))
                    act.copy(act_a[:, :, :], G.psP[1][:, :].rearrange("p (u n) -> p u n", u=2))\
                        .then_inc(s.act_a_ready.handle, 1)
                    act.wait_ge(*s.wneg_ready.count(b, 1))
                    act.activation(wexp[:, :], G.psO[0][0:2, 0:N], ACT.Exp, bias=wneg[:, :], accum_out=wsum[:, :])\
                        .then_inc(s.wexp_ready.handle, 1)
                    for i in range(TH_ + 2):
                        if i < TH_:
                            act.wait_ge(*s.base_ready.count(b, i + 1))
                            act.wait_ge(*s.h0.count(b, i - 1))
                            act.activation(sil[:, 0, i % 2, :], U[i % NU][:, 0:N], ACT.Silu)\
                                .then_inc(s.sil0.handle, 1)
                        if 1 <= i <= TH_:
                            t = i - 1
                            act.wait_ge(*s.delta_ready.count(b, t + 1))
                            act.wait_ge(*s.h1.count(b, t - 1))
                            act.activation(sil[:, 1, t % 2, :], U[t % NU][:, 0:N], ACT.Silu)\
                                .then_inc(s.sil1.handle, 1)
                        if i == 1:
                            act.wait_ge(*s.c_wide.count(b, 1))
                            act.copy(c[:, :, :], G.psO[1][:, :].rearrange("p (j n) -> p j n", j=2))\
                                .then_inc(s.c_ready.handle, 1)
                        if i >= 2:
                            t = i - 2
                            act.wait_ge(*s.ch_ready.count(b, t + 1))
                            act.wait_ge(*s.down_done.count(b, t - 1))
                            act.copy(chs[0][:, t % 2, :, :], ch[:, t % 2, :, :]).then_inc(s.ch_hi.handle, 1)
                    x_high(act, b + 1, s, xT, G.psS)

            @block.vector
            def _(dve):
                dve.wait_ge(consts, 32)
                x_low(dve, 0, s, xT, G.psS)
                with dve.Fori(0, B) as b:
                    steps = Steps(dve, s.chain, b)
                    dve.wait_ge(*s.logits_ready.count(b, 1))
                    steps.done(dve.tensor_copy(logits[:, :, :], G.psP[0][:, 0:NT * NE].rearrange("p (n e) -> p n e", n=NT)))
                    for n in range(NT):
                        dve.memset(G.junk[:, :], 0.0)
                        steps.done(dve.max(top[:, n, :], logits[:, n, :]))
                        dve.memset(G.junk[:, :], 0.0)
                        steps.done(dve.max_index(top_at[:, n, :], top[:, n, :], logits[:, n, :]))
                    dve.tensor_copy(top_f[:, :, :], top_at[:, :, :]).then_inc(s.top_ready.handle, 1)
                    dve.wait_ge(*s.top_ready.count(b, 1))
                    for j in range(2):
                        for n in range(NT):
                            last = dve.tensor_scalar(picked[:, j, n, :], expert_of[:, :], top_f[:, n, j:j + 1], 2.0,
                                                     ALU.is_equal, ALU.mult)
                    last.then_inc(s.picked_ready.handle, 1)
                    dve.wait_ge(*s.top_turned.count(b, 1))
                    dve.tensor_reduce(wneg[:, :], G.psO[0][0:2, 0:N], X_AXIS, ALU.max, negate=True)\
                        .then_inc(s.wneg_ready.handle, 1)
                    dve.wait_ge(*s.mask_turned.count(b, 1))
                    dve.tensor_copy(mask[:, :, :], TM[:, 0:2 * N].rearrange("p (j n) -> p j n", j=2))\
                        .then_inc(s.mask_ready.handle, 1)
                    dve.wait_ge(*s.mask_ready.count(b, 1))
                    steps.done(dve.tensor_tensor(dmask[:, :], mask[:, 1, :], mask[:, 0, :], ALU.subtract))
                    dve.wait_ge(*s.act_a_ready.count(b, 1))
                    m = dmask[:, :].rearrange("p (a n) -> p a n", a=1).broadcast_to([P, 2, N])
                    dve.tensor_tensor(am[:, 1, :, :], act_a[:, :, :], m, ALU.mult)
                    steps.done(dve.tensor_tensor(a_part[0][:, 1, :, :], act_a[:, :, :], m, ALU.mult))
                    dve.tensor_tensor(a_part[1][:, 1, :, :], am[:, 1, :, :], a_part[0][:, 1, :, :], ALU.subtract)\
                        .then_inc(s.a_split1.handle, 1)
                    dve.wait_ge(*s.wexp_ready.count(b, 1))
                    steps.done(dve.reciprocal(winv[:, :], wsum[:, :]))
                    steps.done(dve.tensor_scalar(wexp[:, :], wexp[:, :], winv[:, 0:1], None, ALU.mult))
                    steps.done(dve.tensor_copy(wts[0][:, :], wexp[:, :]))
                    dve.tensor_tensor(wts[1][:, :], wexp[:, :], wts[0][:, :], ALU.subtract)\
                        .then_inc(s.wts_ready.handle, 1)
                    for i in range(TH_ + 2):
                        if i < TH_:
                            dve.wait_ge(*s.sil0.count(b, i + 1))
                            dve.wait_ge(*s.ch_ready.count(b, i - 1))
                            dve.tensor_tensor(h[:, 0, i % 2, :], U[i % NU][:, N:2 * N], sil[:, 0, i % 2, :], ALU.mult)\
                                .then_inc(s.h0.handle, 1)
                        if 1 <= i <= TH_:
                            t = i - 1
                            dve.wait_ge(*s.sil1.count(b, t + 1))
                            dve.tensor_tensor(h[:, 1, t % 2, :], U[t % NU][:, N:2 * N], sil[:, 1, t % 2, :], ALU.mult)\
                                .then_inc(s.h1.handle, 1)
                        if i >= 2:
                            t = i - 2
                            dve.wait_ge(*s.ch_hi.count(b, t + 1))
                            dve.tensor_tensor(chs[1][:, t % 2, :, :], ch[:, t % 2, :, :], chs[0][:, t % 2, :, :],
                                              ALU.subtract).then_inc(s.ch_lo.handle, 1)
                    x_low(dve, b + 1, s, xT, G.psS)
                    dve.wait_ge(*s.z_ready.count(b, 1))
                    steps.done(dve.tensor_tensor(zm[:, :, :], Z[:, :].rearrange("p (j n) -> p j n", j=2),
                                                 mask[:, :, :], ALU.mult))
                    steps.done(dve.tensor_tensor(zm[:, 0, :], zm[:, 0, :], zm[:, 1, :], ALU.add))
                    steps.done(dve.tensor_copy(zs[0][:, :], zm[:, 0, :]))
                    dve.tensor_tensor(zs[1][:, :], zm[:, 0, :], zs[0][:, :], ALU.subtract)\
                        .then_inc(s.z_parts.handle, 1)
                    for n in range(NT):
                        add_and_measure(dve, s, b, n, Y[n][:, :], s.y_ready, G, steps)
                    for n in range(NT):
                        normalize(dve, s, b, n, G)
                    steps.check()


def xattn1(nc, G, W):
    H, KVH, D = 16, 8, 128
    NS, NPB = 2, 3
    SCALE = float(1.0 / np.sqrt(np.float32(D)))
    with Scope(nc, "c1") as sc:
        def pair(name, shape):
            return [sc.sb(f"{name}{i}", shape, F16) for i in range(2)]

        wq = pair("wq", [P, KE, H * D])
        wk = pair("wk", [P, KC, KVH * D])
        wv = pair("wv", [P, KC, KVH * D])
        wo = pair("wo", [P, H, E])
        cT = pair("cT", [P, KC, B * N])
        load_and_split(nc, sc, G, [(kt_view(d), w[0][:, :, :], w[1][:, :, :]) for d, w in (
            (W["L1_xattn_Wq"], wq), (W["L1_xattn_Wk"], wk), (W["L1_xattn_Wv"], wv), (W["L1_xattn_Wo"], wo), (W["ctxT"], cT))])

        xT = pair("xT", [P, KE, N])
        qT = pair("qT", [P, H, N])
        oT = qT
        kT = pair("kT", [P, KVH, N])
        v = pair("v", [P, NT, KVH * D])
        xcur = sc.sb("xcur", [P, NT, E], F32)
        prob = sc.sb("prob", [P, NPB, NT, N], F32)
        sums = sc.sb("sums", [P, NPB, NT], F32)
        inv = sc.sb("inv", [P, NPB, NT], F32)
        negmax = sc.sb("negmax", [P, NPB, NT], F32)
        pT = pair("pT", [P, 2, NT, N])
        seen_col8 = sc.sb("seen_col8", [P, B * NT], U8)
        seen_row8 = sc.sb("seen_row8", [1, B * N], U8)
        seen_col = sc.sb("seen_col", [P, (B + 1) * NT], F32)
        seen_now = sc.sb("seen_now", [P, NT], F32)
        hide_row = sc.sb("hide_row", [1, B * N], BF16)
        ones_b = sc.sb("ones_b", [1, P], BF16)

        NQ, NK, NV = H // 2, KVH // 2, NT * 2
        NPR = NQ + NK + NV
        s = Names()
        x_counters(sc, s)
        s.seen_ready = sc.counter("seen_ready", 1)
        s.t_ready = sc.counter("t_ready", H)
        s.t_hi = sc.counter("t_hi", H)
        s.t_lo = sc.counter("t_lo", H)
        s.pr_ready = sc.counter("pr_ready", NPR)
        s.pr_hi = sc.counter("pr_hi", NPR)
        s.pr_lo = sc.counter("pr_lo", NPR)
        s.s_ready = sc.counter("s_ready", H)
        s.m_ready = sc.counter("m_ready", H)
        s.e_ready = sc.counter("e_ready", H)
        s.i_ready = sc.counter("i_ready", H)
        s.p_ready = sc.counter("p_ready", H)
        s.o_ready = sc.counter("o_ready", H)
        s.o_hi = sc.counter("o_hi", H)
        s.o_lo = sc.counter("o_lo", H)
        s.y_ready = sc.counter("y_ready", NT)
        s.chain = sc.counter("chain", NT * LN_STEPS)
        ln_counters(sc, s)
        landed, masks_ready = sc.sem("landed"), sc.sem("masks_ready")
        SB, Y = G.psS, G.psP
        PR = [G.psO[0], G.psO[1], G.psP[0], G.psP[1]]
        sc.start_counters()

        with nc.Block() as block:
            @block.sync
            def _(sp):
                sp.dma_start(seen_row8[0:1, :], W["seen"].rearrange("(a b) n -> a (b n)", a=1)).then_inc(landed, 16)
                sp.dma_start(seen_col8[:, :], W["seen_cols"]).then_inc(landed, 16)
                fetch_all_x(sp, s, G, xcur)

            @block.gpsimd
            def _(pool):
                pool.wait_ge(masks_ready, 3)

                def see(b):
                    pool.wait_ge(*s.pr_lo.count(b, 0))
                    pool.tensor_copy(seen_now[:, :], seen_col[:, bass.ds(b * NT, NT)]).then_inc(s.seen_ready.handle, 1)

                see(0)
                with pool.Fori(0, B) as b:
                    see(b + 1)
                    for h in range(H):
                        pool.wait_ge(*s.i_ready.count(b, h + 1))
                        pool.tensor_tensor(
                            prob[:, h % NPB, :, :], prob[:, h % NPB, :, :],
                            inv[:, h % NPB, :].rearrange("p (n a) -> p n a", a=1).broadcast_to([P, NT, N]),
                            ALU.mult).then_inc(s.p_ready.handle, 1)
                    for n in range(NT):
                        rstd_on_pool(pool, s, b, n, G)

            @block.tensor
            def _(pe):
                def turn(b, g, blocks):
                    pe.wait_ge(*s.t_lo.count(b, g - 1))
                    for out, src in blocks:
                        last = pe.transpose(out, src, G.ident[:, :])
                    last.then_inc(s.t_ready.handle, 1)

                pe.wait_ge(masks_ready, 3)
                turn_x(pe, 0, s, G, xcur, G.psS)
                with pe.Fori(0, B) as b:
                    ctx_at = bass.ds(b * N, N)
                    for i in range(NPR):
                        if i == 2:
                            pe.wait_ge(*s.x_done.count(b, 0))
                        if i >= 4:
                            pe.wait_ge(*s.pr_lo.count(b, i - 3))
                        out = PR[i % 4]
                        if i < NK:
                            for j in range(2):
                                cols = slice((2 * i + j) * D, (2 * i + j + 1) * D)
                                for k in range(KC):
                                    last = three(pe, out[:, j * N:(j + 1) * N], wk[0][:, k, cols], wk[1][:, k, cols],
                                                 cT[0][:, k, ctx_at], cT[1][:, k, ctx_at], k == 0, k == KC - 1)
                        elif i < NK + NV:
                            n, cc = divmod(i - NK, 2)
                            at = bass.ds(b * N + n * P, P)
                            cols = slice(cc * E, (cc + 1) * E)
                            for k in range(KC):
                                last = three(pe, out[:, :], cT[0][:, k, at], cT[1][:, k, at], wv[0][:, k, cols],
                                             wv[1][:, k, cols], k == 0, k == KC - 1)
                        else:
                            if i == NK + NV:
                                pe.wait_ge(*s.x_lo.count(b, NT))
                            for j in range(2):
                                hq = 2 * (i - NK - NV) + j
                                for k in range(KE):
                                    last = three(pe, out[:, j * N:(j + 1) * N], wq[0][:, k, hq * D:(hq + 1) * D],
                                                 wq[1][:, k, hq * D:(hq + 1) * D], xT[0][:, k, :], xT[1][:, k, :],
                                                 k == 0, k == KE - 1)
                        last.then_inc(s.pr_ready.handle, 1)

                    def scores(h):
                        if h >= NS:
                            pe.wait_ge(*s.e_ready.count(b, h - NS + 1))
                        S, hk = SB[h % NS], h // 2
                        for n in range(NT):
                            out = S[:, n * N:(n + 1) * N]
                            three(pe, out, qT[0][:, h, n * P:(n + 1) * P], qT[1][:, h, n * P:(n + 1) * P],
                                  kT[0][:, hk, :], kT[1][:, hk, :], True, False)
                            last = pe.matmul(out, ones_b[0:1, :], hide_row[0:1, ctx_at], start=False, stop=True,
                                             skip_group_check=True)
                        last.then_inc(s.s_ready.handle, 1)

                    def turn_p(h):
                        T = G.psT[h % 2]
                        pe.wait_ge(*s.p_ready.count(b, h + 1))
                        turn(b, h, [(T[:, m * N + n * P:m * N + (n + 1) * P], prob[:, h % NPB, n, m * P:(m + 1) * P])
                                    for m in range(NT) for n in range(NT)])

                    def pv(h):
                        if h >= 2:
                            pe.wait_ge(*s.o_lo.count(b, h - 1))
                        pe.wait_ge(*s.t_lo.count(b, h + 1))
                        r, cols = h % 2, slice((h // 2) * D, (h // 2 + 1) * D)
                        for m in range(NT):
                            last = three(pe, G.psO[r][:, 0:N], v[0][:, m, cols], v[1][:, m, cols],
                                         pT[0][:, r, m, :], pT[1][:, r, m, :], m == 0, m == NT - 1)
                        last.then_inc(s.o_ready.handle, 1)

                    def project(h):
                        pe.wait_ge(*s.o_lo.count(b, h + 1))
                        for n in range(NT):
                            last = three(pe, Y[n][:, :], oT[0][:, h, n * P:(n + 1) * P],
                                         oT[1][:, h, n * P:(n + 1) * P], wo[0][:, h, :], wo[1][:, h, :],
                                         h == 0, h == H - 1)
                            if h == H - 1:
                                last.then_inc(s.y_ready.handle, 1)

                    pe.wait_ge(*s.pr_lo.count(b, NPR))
                    for i in range(H + 5):
                        if i < H:
                            scores(i)
                        if 2 <= i < H + 2:
                            turn_p(i - 2)
                        if 3 <= i < H + 3:
                            pv(i - 3)
                        if i == H + 2:
                            pe.wait_ge(*s.e_ready.count(b, H))
                            turn_x(pe, b + 1, s, G, xcur, G.psS)
                        if i >= 5:
                            project(i - 5)

            @block.scalar
            def _(act):
                act.wait_ge(masks_ready, 3)
                x_high(act, 0, s, xT, G.psS)
                with act.Fori(0, B) as b:
                    act.wait_ge(*s.seen_ready.count(b, 1))
                    for i in range(NPR):
                        act.wait_ge(*s.pr_ready.count(b, i + 1))
                        out = PR[i % 4][:, :]
                        two = out.rearrange("p (j n) -> p j n", j=2)
                        if i < NK:
                            last = act.copy(kT[0][:, 2 * i:2 * i + 2, :], two)
                        elif i < NK + NV:
                            n, cc = divmod(i - NK, 2)
                            last = act.mul(v[0][:, n, cc * E:(cc + 1) * E], out, seen_now[:, n:n + 1])
                        else:
                            j = i - NK - NV
                            last = act.mul(qT[0][:, 2 * j:2 * j + 2, :], two, SCALE)
                        last.then_inc(s.pr_hi.handle, 1)

                    def expo(h):
                        act.wait_ge(*s.m_ready.count(b, h + 1))
                        if h >= NPB:
                            act.wait_ge(*s.t_ready.count(b, h - NPB + 1))
                        S, r = SB[h % NS], h % NPB
                        for n in range(NT):
                            last = act.activation(prob[:, r, n, :], S[:, n * N:(n + 1) * N], ACT.Exp,
                                                  bias=negmax[:, r, n:n + 1], accum_out=sums[:, r, n:n + 1])
                        last.then_inc(s.e_ready.handle, 1)

                    def hi_p(h):
                        act.wait_ge(*s.t_ready.count(b, h + 1))
                        if h >= 2:
                            act.wait_ge(*s.o_ready.count(b, h - 1))
                        act.copy(pT[0][:, h % 2, :, :], G.psT[h % 2][:, :].rearrange("p (m n) -> p m n", m=NT))\
                            .then_inc(s.t_hi.handle, 1)

                    def hi_o(h):
                        act.wait_ge(*s.o_ready.count(b, h + 1))
                        act.copy(oT[0][:, h, :], G.psO[h % 2][:, 0:N]).then_inc(s.o_hi.handle, 1)

                    for i in range(H + 3):
                        if 2 <= i < H + 2:
                            hi_p(i - 2)
                        if i < H:
                            expo(i)
                        if i >= 3:
                            hi_o(i - 3)
                    x_high(act, b + 1, s, xT, G.psS)

            @block.vector
            def _(dve):
                dve.wait_ge(landed, 32)
                dve.memset(seen_col[:, B * NT:(B + 1) * NT], 0.0)
                dve.tensor_copy(seen_col[:, 0:B * NT], seen_col8[:, :]).then_inc(masks_ready, 1)
                dve.tensor_scalar(hide_row[:, :], seen_row8[:, :], -1.0, -MASKED, ALU.add, ALU.mult)\
                    .then_inc(masks_ready, 1)
                dve.memset(ones_b[:, :], 1.0).then_inc(masks_ready, 1)
                dve.wait_ge(masks_ready, 3)
                x_low(dve, 0, s, xT, G.psS)
                with dve.Fori(0, B) as b:
                    steps = Steps(dve, s.chain, b)
                    dve.wait_ge(*s.seen_ready.count(b, 1))
                    for i in range(NPR):
                        dve.wait_ge(*s.pr_hi.count(b, i + 1))
                        out = PR[i % 4][:, :]
                        two = out.rearrange("p (j n) -> p j n", j=2)
                        if i < NK:
                            at = (slice(None), slice(2 * i, 2 * i + 2), slice(None))
                            last = dve.tensor_tensor(kT[1][at], two, kT[0][at], ALU.subtract)
                        elif i < NK + NV:
                            n, cc = divmod(i - NK, 2)
                            cols = slice(cc * E, (cc + 1) * E)
                            last = dve.scalar_tensor_tensor(v[1][:, n, cols], out, seen_now[:, n:n + 1],
                                                            v[0][:, n, cols], ALU.mult, ALU.subtract)
                        else:
                            j = i - NK - NV
                            at = (slice(None), slice(2 * j, 2 * j + 2), slice(None))
                            last = dve.scalar_tensor_tensor(qT[1][at], two, SCALE, qT[0][at], ALU.mult, ALU.subtract)
                        last.then_inc(s.pr_lo.handle, 1)

                    def rowmax(h):
                        dve.wait_ge(*s.s_ready.count(b, h + 1))
                        if h >= NPB:
                            dve.wait_ge(*s.e_ready.count(b, h - NPB + 1))
                        dve.tensor_reduce(negmax[:, h % NPB, :], SB[h % NS][:, :].rearrange("p (n m) -> p n m", n=NT),
                                          X_AXIS, ALU.max, negate=True).then_inc(s.m_ready.handle, 1)

                    def invert(h):
                        dve.wait_ge(*s.e_ready.count(b, h + 1))
                        if h >= NPB:
                            dve.wait_ge(*s.p_ready.count(b, h - NPB + 1))
                        dve.reciprocal(inv[:, h % NPB, :], sums[:, h % NPB, :]).then_inc(s.i_ready.handle, 1)

                    def lo_p(h):
                        dve.wait_ge(*s.t_hi.count(b, h + 1))
                        dve.tensor_tensor(pT[1][:, h % 2, :, :], G.psT[h % 2][:, :].rearrange("p (m n) -> p m n", m=NT),
                                          pT[0][:, h % 2, :, :], ALU.subtract).then_inc(s.t_lo.handle, 1)

                    def lo_o(h):
                        dve.wait_ge(*s.o_hi.count(b, h + 1))
                        dve.tensor_tensor(oT[1][:, h, :], G.psO[h % 2][:, 0:N], oT[0][:, h, :], ALU.subtract)\
                            .then_inc(s.o_lo.handle, 1)

                    for i in range(H + 3):
                        if i < H:
                            rowmax(i)
                        if 1 <= i <= H:
                            invert(i - 1)
                        if 2 <= i < H + 2:
                            lo_p(i - 2)
                        if i >= 3:
                            lo_o(i - 3)
                    x_low(dve, b + 1, s, xT, G.psS)
                    for n in range(NT):
                        add_and_measure(dve, s, b, n, Y[n][:, :], s.y_ready, G, steps)
                    for n in range(NT):
                        normalize(dve, s, b, n, G)
                    steps.check()


def ternary_weights(nc, sc, G, drams, out, c127):
    WORDS = 8192
    with ExitStack() as stack:
        raw = stack.enter_context(nc.sbuf_tensor("f1_raw", [P, 3, WORDS], F32))

        def small(name, shape):
            return stack.enter_context(nc.sbuf_tensor(f"f1_{name}", shape, F32))

        part = small("part", [P, 3, 16])
        total = small("total", [P, 4])
        s_mean = small("s_mean", [P, 3])
        thr = small("thr", [P, 3])
        logs = small("logs", [P, 2, 3])
        sem = {k: sc.sem(k) for k in ("raw0", "raw1", "raw2", "w_step", "total_done", "logs_done", "signs_done", "abs_done")}
        with nc.Block() as block:
            @block.sync
            def _(sp):
                for i, d in enumerate(drams):
                    v = kt_view(d)
                    k = v.shape[1]
                    sp.dma_start(raw[:, i, :].rearrange("p (k n) -> p k n", k=k), v).then_inc(sem[f"raw{i}"], 16)

            @block.tensor
            def _(pe):
                pe.wait_ge(sem["w_step"], 7)
                pe.matmul(G.psP[0][:, 0:4], G.ones[:, 0:P], total[:, :], start=True, stop=True)\
                    .then_inc(sem["total_done"], 1)

            @block.scalar
            def _(act):
                for i in range(3):
                    act.wait_ge(sem[f"raw{i}"], 16)
                    act.activation(out[i], raw[:, i, :], ACT.Sign).then_inc(sem["signs_done"], 1)
                    act.wait_ge(sem["signs_done"], i + 1)
                    act.wait_ge(sem["w_step"], 2 * i + 2)
                    act.activation(raw[:, i, :], raw[:, i, :], ACT.Abs).then_inc(sem["abs_done"], 1)
                act.wait_ge(sem["w_step"], 8)
                act.activation(logs[:, 0, :], s_mean[:, :], ACT.Ln, bias=1.0)
                act.activation(logs[:, 1, :], s_mean[:, :], ACT.Ln, bias=1.0, scale=-1.0)\
                    .then_inc(sem["logs_done"], 1)

            @block.vector
            def _(dve):
                n = 0

                def then(ins):
                    nonlocal n
                    n += 1
                    ins.then_inc(sem["w_step"], 1)
                    dve.wait_ge(sem["w_step"], n)
                then(dve.memset(total[:, :], 0.0))
                for i in range(3):
                    dve.wait_ge(sem[f"raw{i}"], 16)
                    then(dve.tensor_reduce(part[:, i, :], raw[:, i, :].rearrange("p (a n) -> p a n", a=16), X_AXIS,
                                           ALU.add, apply_absolute_value=True))
                    then(dve.tensor_reduce(total[:, i:i + 1], part[:, i, :], X_AXIS, ALU.add))
                dve.wait_ge(sem["total_done"], 1)
                then(dve.tensor_scalar(s_mean[:, :], G.psP[0][:, 0:3], 1.0 / (P * WORDS), None, ALU.mult))
                then(dve.tensor_scalar(thr[:, :], s_mean[:, :], 1e-8, float(np.arctanh(0.5)), ALU.add, ALU.mult))
                for i in range(3):
                    dve.wait_ge(sem["abs_done"], i + 1)
                    dve.scalar_tensor_tensor(out[i], raw[:, i, :], thr[:, i:i + 1], out[i], ALU.is_gt, ALU.mult)
                dve.wait_ge(sem["logs_done"], 1)
                then(dve.tensor_tensor(logs[:, 0, :], logs[:, 0, :], logs[:, 1, :], ALU.subtract))
                dve.tensor_scalar(c127[:, :], logs[:, 0, :], 0.5 / 127.0, None, ALU.mult)


def ffn1(nc, G, W):
    HID = 2048
    NCH = HID // E
    KH = HID // P
    ROUND = float(1.5 * 2 ** 23)
    with Scope(nc, "f1") as sc:
        wq = [sc.sb(f"wq{i}", [P, 8192], F16) for i in range(3)]
        w12 = [w[:, :].rearrange("p (k n) -> p k n", k=KE) for w in wq[:2]]
        w3 = wq[2][:, :].rearrange("p (k n) -> p k n", k=KH)
        c127 = sc.sb("c127", [P, 3], F32)
        ternary_weights(nc, sc, G, (W["L1_ffn_w1T"], W["L1_ffn_w2T"], W["L1_ffn_w3T"]), [w[:, :] for w in wq], c127)

        g12 = sc.sb("g12", [P, 2, E], F32)
        g3 = sc.sb("g3", [P, HID], F32)
        xcur = sc.sb("xcur", [P, NT, E], F32)
        squares = sc.sb("squares", [P, E], F32)
        x_squares = sc.sb("x_squares", [P, E], F32)
        ssx = sc.sb("ssx", [P, NT], F32)
        msx = sc.sb("msx", [P, NT], F32)
        rx = sc.sb("rx", [P, NT], F32)
        xn = sc.sb("xn", [P, NT, 2, E], F32)
        xr = sc.sb("xr", [P, NT, 2 * E], F16)
        mx = sc.sb("mx", [P, NT, 2], F32)
        qx = sc.sb("qx", [P, NT, 2], F32)
        ax = sc.sb("ax", [P, NT, 2], F32)
        xq = sc.sb("xq", [P, 2, KE, N], F16)
        sil = sc.sb("sil", [P, 2, E], F32)
        h = sc.sb("h", [P, 2, E], F32)
        hg = sc.sb("hg", [P, NT, HID], F32)
        hr = sc.sb("hr", [P, NT, HID], F16)
        ssh = sc.sb("ssh", [P, NT, NCH], F32)
        mxh = sc.sb("mxh", [P, NT, NCH], F32)
        hs = sc.sb("hs", [P, NT, 8], F32)
        rh = sc.sb("rh", [P, NT], F32)
        hq = sc.sb("hq", [P, KH, N], F16)

        U = [G.psS[0], G.psS[1], G.psP[0], G.psP[1]]
        NJ = NT * NCH
        s = Names()
        s.xcur_ready = sc.counter("xcur_ready", 16)
        s.ssx_ready = sc.counter("ssx_ready", NT)
        s.msx_ready = sc.counter("msx_ready", NT)
        s.rx_ready = sc.counter("rx_ready", NT)
        s.xn_ready = sc.counter("xn_ready", NT)
        s.xr_ready = sc.counter("xr_ready", NT)
        s.xt_ready = sc.counter("xt_ready", NT)
        s.xq_ready = sc.counter("xq_ready", NT)
        s.u_ready = sc.counter("u_ready", NJ)
        s.sil_ready = sc.counter("sil_ready", NJ)
        s.h_ready = sc.counter("h_ready", NJ)
        s.sq_ready = sc.counter("sq_ready", NJ)
        s.hg_ready = sc.counter("hg_ready", NJ)
        s.mh_ready = sc.counter("mh_ready", NT)
        s.rh_ready = sc.counter("rh_ready", NT)
        s.hm_ready = sc.counter("hm_ready", NT)
        s.hr_ready = sc.counter("hr_ready", NT)
        s.ht_ready = sc.counter("ht_ready", 2 * NT)
        s.hq_ready = sc.counter("hq_ready", 2 * NT)
        s.y_ready = sc.counter("y_ready", NT)
        s.chain = sc.counter("chain", NT * 5 + NT * 7 + NT * LN_STEPS)
        s.first_chain = sc.counter("first_chain", NT * 5)
        ln_counters(sc, s)
        landed = sc.sem("landed")
        sc.start_counters()
        TH16 = [t[:, :].bitcast(F16) for t in G.psT]
        XT16 = [t[:, :].bitcast(F16) for t in G.psS]

        with nc.Block() as block:
            @block.sync
            def _(sp):
                for i, g in enumerate((W["L1_ffn_g1"], W["L1_ffn_g2"])):
                    sp.dma_start(g12[:, i, :], g.rearrange("(a n) -> a n", a=1).broadcast_to([P, E]))\
                        .then_inc(landed, 16)
                sp.dma_start(g3[:, :], W["L1_ffn_g3"].rearrange("(a n) -> a n", a=1).broadcast_to([P, HID]))\
                    .then_inc(landed, 16)

                def fetch(b):
                    sp.wait_ge(*s.ssx_ready.count(b, 0))
                    sp.dma_start(xcur[:, :, :], G.x[:, bass.ds(b * NT, NT), :]).then_inc(s.xcur_ready.handle, 16)

                fetch(0)
                with sp.Fori(0, B) as b:
                    fetch(b + 1)
                sp.wait_ge(*s.xcur_ready.count(B, 16))

            @block.gpsimd
            def _(pool):
                pool.wait_ge(landed, 48)

                def x_rms(b):
                    for n in range(NT):
                        pool.wait_ge(*s.msx_ready.count(b, n + 1))
                        pool.tensor_tensor(rx[:, n:n + 1], msx[:, n:n + 1], G.minus_half[:, 0:1], ALU.pow)\
                            .then_inc(s.rx_ready.handle, 1)

                x_rms(0)
                with pool.Fori(0, B) as b:
                    for j in range(NJ):
                        n, c = divmod(j, NCH)
                        pool.wait_ge(*s.h_ready.count(b, j + 1))
                        at = slice(c * E, (c + 1) * E)
                        pool.tensor_tensor(hg[:, n, at], h[:, j % 2, :], g3[:, at], ALU.mult)\
                            .then_inc(s.hg_ready.handle, 1)
                        if j == 1:
                            x_rms(b + 1)
                        if c == NCH - 1:
                            pool.wait_ge(*s.mh_ready.count(b, n + 1))
                            pool.tensor_tensor(rh[:, n:n + 1], hs[:, n, 1:2], G.minus_half[:, 0:1], ALU.pow)\
                                .then_inc(s.rh_ready.handle, 1)
                        if j >= NJ - 1:
                            for n in range(NT):
                                rstd_on_pool(pool, s, b, n, G)

            @block.tensor
            def _(pe):
                def turn_xr(b):
                    for n in range(NT):
                        pe.wait_ge(*s.xr_ready.count(b, n + 1))
                        for k in range(2 * KE):
                            last = pe.transpose(XT16[n][:, k * P:(k + 1) * P], xr[:, n, k * P:(k + 1) * P],
                                                G.ident_h[:, :])
                        last.then_inc(s.xt_ready.handle, 1)

                def up(b, j):
                    n, c = divmod(j, NCH)
                    for i in range(2):
                        for k in range(KE):
                            last = pe.matmul(U[2 * (j % 2) + i][:, :], xq[:, i, k, n * P:(n + 1) * P],
                                             w12[i][:, k, c * E:(c + 1) * E], start=k == 0, stop=k == KE - 1)
                    last.then_inc(s.u_ready.handle, 1)

                def down(b, n):
                    pe.wait_ge(*s.hr_ready.count(b, n + 1))
                    for g in range(2):
                        pe.wait_ge(*s.hq_ready.count(b, 2 * n + g - 1))
                        for k in range(8):
                            kk = g * 8 + k
                            last = pe.transpose(TH16[g][:, k * P:(k + 1) * P], hr[:, n, kk * P:(kk + 1) * P],
                                                G.ident_h[:, :])
                        last.then_inc(s.ht_ready.handle, 1)
                    pe.wait_ge(*s.hq_ready.count(b, 2 * n + 2))
                    pe.wait_ge(*s.x_done.count(b, 0))
                    for k in range(KH):
                        last = pe.matmul(G.psO[n][:, :], hq[:, k, n * P:(n + 1) * P], w3[:, k, :],
                                         start=k == 0, stop=k == KH - 1)
                    last.then_inc(s.y_ready.handle, 1)

                turn_xr(0)
                pe.wait_ge(*s.xq_ready.count(0, NT))
                up(0, 0)
                up(0, 1)
                with pe.Fori(0, B) as b:
                    for j in range(2, NJ):
                        pe.wait_ge(*s.h_ready.count(b, j - 1))
                        up(b, j)
                        if j == 5:
                            down(b, 0)
                    pe.wait_ge(*s.h_ready.count(b, NJ - 1))
                    turn_xr(b + 1)
                    pe.wait_ge(*s.xq_ready.count(b + 1, NT))
                    up(b + 1, 0)
                    pe.wait_ge(*s.h_ready.count(b, NJ))
                    up(b + 1, 1)
                    down(b, 1)

            @block.scalar
            def _(act):

                def x_square(b):
                    act.wait_ge(*s.xcur_ready.count(b, 16))
                    for n in range(NT):
                        act.wait_ge(*s.ssx_ready.count(b, n))
                        act.activation(x_squares[:, :], xcur[:, n, :], ACT.Square, accum_out=ssx[:, n:n + 1])\
                            .then_inc(s.ssx_ready.handle, 1)

                x_square(0)
                with act.Fori(0, B) as b:
                    def square(j):
                        n, c = divmod(j, NCH)
                        act.wait_ge(*s.sq_ready.count(b, j))
                        act.wait_ge(*s.h_ready.count(b, j + 1))
                        act.activation(squares[:, :], h[:, j % 2, :], ACT.Square, accum_out=ssh[:, n, c:c + 1])\
                            .then_inc(s.sq_ready.handle, 1)

                    for j in range(NJ):
                        n = j // NCH
                        act.wait_ge(*s.u_ready.count(b, j + 1))
                        if j >= 2:
                            act.wait_ge(*s.h_ready.count(b, j - 1))
                        act.activation(sil[:, j % 2, :], U[2 * (j % 2)][:, :], ACT.Silu, scale=ax[:, n, 0:1])\
                            .then_inc(s.sil_ready.handle, 1)
                        if j:
                            square(j - 1)
                        if j == 1:
                            x_square(b + 1)
                    square(NJ - 1)

            @block.vector
            def _(dve):
                dve.wait_ge(landed, 48)

                def mean_squares(b):
                    for n in range(NT):
                        dve.wait_ge(*s.ssx_ready.count(b, n + 1))
                        dve.tensor_scalar(msx[:, n:n + 1], ssx[:, n:n + 1], 1.0 / E, 1e-8, ALU.mult, ALU.add)\
                            .then_inc(s.msx_ready.handle, 1)

                def round_x(b, n, steps):
                    dve.wait_ge(*s.rx_ready.count(b, n + 1))
                    for i in range(2):
                        last = dve.scalar_tensor_tensor(xn[:, n, i:i + 1, :], G.x[:, bass.ds(b * NT + n, 1), :],
                                                        rx[:, n:n + 1], g12[:, i:i + 1, :], ALU.mult, ALU.mult)
                    steps.done(last)
                    steps.done(dve.tensor_reduce(mx[:, n, :], xn[:, n, :, :], X_AXIS, ALU.max,
                                                 apply_absolute_value=True))
                    steps.done(dve.tensor_scalar(mx[:, n, :], mx[:, n, :], 1e-4, None, ALU.max))
                    steps.done(dve.reciprocal(qx[:, n, :], mx[:, n, :]))
                    steps.done(dve.tensor_scalar(qx[:, n, :], qx[:, n, :], 127.0, None, ALU.mult))
                    for i in range(2):
                        last = dve.tensor_scalar(xn[:, n, i, :], xn[:, n, i, :], qx[:, n, i:i + 1], ROUND,
                                                 ALU.mult, ALU.add)
                    last.then_inc(s.xn_ready.handle, 1)
                    dve.wait_ge(*s.xn_ready.count(b, n + 1))
                    dve.tensor_scalar(xr[:, n, :], xn[:, n, :, :].rearrange("p i e -> p (i e)"), ROUND, None,
                                      ALU.subtract).then_inc(s.xr_ready.handle, 1)

                def clip_x(b):
                    for n in range(NT):
                        dve.tensor_tensor(ax[:, n, :], mx[:, n, :], c127[:, 0:2], ALU.mult)
                    for n in range(NT):
                        dve.wait_ge(*s.xt_ready.count(b, n + 1))
                        for i in range(2):
                            last = dve.tensor_scalar(
                                xq[:, i, :, n * P:(n + 1) * P],
                                XT16[n][:, i * E:(i + 1) * E].rearrange("p (k t) -> p k t", k=KE),
                                127.0, -128.0, ALU.min, ALU.max)
                        last.then_inc(s.xq_ready.handle, 1)

                mean_squares(0)
                steps = Steps(dve, s.first_chain, 0)
                for n in range(NT):
                    round_x(0, n, steps)
                steps.check()
                clip_x(0)
                with dve.Fori(0, B) as b:
                    steps = Steps(dve, s.chain, b)

                    def absmax(j):
                        n, c = divmod(j, NCH)
                        dve.wait_ge(*s.hg_ready.count(b, j + 1))
                        last = dve.tensor_reduce(mxh[:, n, c:c + 1], hg[:, n, c * E:(c + 1) * E], X_AXIS, ALU.max,
                                                 apply_absolute_value=True)
                        if c == NCH - 1:
                            m = hs[:, n, :]
                            steps.done(last)
                            dve.wait_ge(*s.sq_ready.count(b, j + 1))
                            steps.done(dve.tensor_reduce(m[:, 0:1], ssh[:, n, :], X_AXIS, ALU.add))
                            dve.tensor_scalar(m[:, 1:2], m[:, 0:1], 1.0 / HID, 1e-8, ALU.mult, ALU.add)\
                                .then_inc(s.mh_ready.handle, 1)
                            steps.done(dve.tensor_reduce(m[:, 2:3], mxh[:, n, :], X_AXIS, ALU.max))
                            dve.wait_ge(*s.rh_ready.count(b, n + 1))
                            steps.done(dve.tensor_scalar(m[:, 3:4], m[:, 2:3], rh[:, n:n + 1], 1e-4, ALU.mult, ALU.max))
                            dve.tensor_tensor(m[:, 4:5], m[:, 3:4], c127[:, 2:3], ALU.mult)
                            steps.done(dve.reciprocal(m[:, 5:6], m[:, 3:4]))
                            steps.done(dve.tensor_scalar(m[:, 6:7], m[:, 5:6], rh[:, n:n + 1], 127.0, ALU.mult, ALU.mult))
                            steps.done(dve.tensor_scalar(hg[:, n, :], hg[:, n, :], m[:, 6:7], ROUND, ALU.mult, ALU.add))
                            dve.tensor_scalar(hr[:, n, :], hg[:, n, :], ROUND, None, ALU.subtract)\
                                .then_inc(s.hr_ready.handle, 1)

                    def clip_h(n):
                        for g in range(2):
                            dve.wait_ge(*s.ht_ready.count(b, 2 * n + g + 1))
                            dve.tensor_scalar(hq[:, g * 8:(g + 1) * 8, n * P:(n + 1) * P],
                                              TH16[g][:, :].rearrange("p (k t) -> p k t", k=8), 127.0, -128.0,
                                              ALU.min, ALU.max).then_inc(s.hq_ready.handle, 1)

                    for j in range(NJ):
                        dve.wait_ge(*s.sil_ready.count(b, j + 1))
                        if j >= 2:
                            dve.wait_ge(*s.hg_ready.count(b, j - 1))
                            dve.wait_ge(*s.sq_ready.count(b, j - 1))
                        dve.scalar_tensor_tensor(h[:, j % 2, :], U[2 * (j % 2) + 1][:, :], ax[:, j // NCH, 1:2],
                                                 sil[:, j % 2, :], ALU.mult, ALU.mult).then_inc(s.h_ready.handle, 1)
                        if j:
                            absmax(j - 1)
                        if j == 1:
                            mean_squares(b + 1)
                        if j == 2:
                            round_x(b + 1, 0, steps)
                        if j == 5:
                            clip_h(0)
                            round_x(b + 1, 1, steps)
                    dve.wait_ge(*s.h_ready.count(b, NJ))
                    clip_x(b + 1)
                    absmax(NJ - 1)
                    add_and_norm(dve, s, b, 0, G.psO[0][:, :], s.y_ready, G, steps, hs[:, 0, 4:5])
                    clip_h(1)
                    add_and_norm(dve, s, b, 1, G.psO[1][:, :], s.y_ready, G, steps, hs[:, 1, 4:5])
                    steps.check()


def more_inputs(a):
    def stack_B(w):
        return w.transpose(0, 2, 1).reshape(P, -1)

    seen = a["mask_BxS2_bf1"].view(np.uint8)
    return {
        "L1_ffn_w1T": a["L1_ffn_w1"].T, "L1_ffn_w2T": a["L1_ffn_w2"].T, "L1_ffn_w3T": a["L1_ffn_w3"].T,
        "L1_ffn_g1": a["L1_ffn_g1"], "L1_ffn_g2": a["L1_ffn_g2"], "L1_ffn_g3": a["L1_ffn_g3"],
        "f0_up_gateT": np.concatenate([a["L0_ffn_w_up"], a["L0_ffn_w_gate"]], 0).T,
        "f0_A": np.concatenate([a["L0_ffn_up_A"].reshape(P, E), a["L0_ffn_gate_A"].reshape(P, E)], 0).T,
        "f0_B": np.concatenate([stack_B(a["L0_ffn_up_B"]), stack_B(a["L0_ffn_gate_B"])], 1),
        "f0_downT": a["L0_ffn_w_down"].T, "f0_dA": a["L0_ffn_down_A"].reshape(P, -1).T,
        "f0_dB": stack_B(a["L0_ffn_down_B"]), "f0_router": a["L0_ffn_gate_w"].T,
        "expert_of": np.tile(np.repeat(np.arange(8, dtype=np.float32), 16), (P, 1)),
        "row_pick": np.repeat(np.eye(2, dtype=np.float16)[:, :, None], P, axis=2),
        "seen": seen, "seen_cols": seen.reshape(B * NT, P).T,
        "L1_xattn_Wq": a["L1_xattn_Wq"], "L1_xattn_Wk": a["L1_xattn_Wk"], "L1_xattn_Wv": a["L1_xattn_Wv"],
        "L1_xattn_Wo": a["L1_xattn_Wo"],
        "ctxT": a["ctx_1024"].reshape(B * N, C).T, "fside": a["fside_BxSx2_0"],
        "L0_xattn_Wq": a["L0_xattn_Wq"], "L0_xattn_Wkv": a["L0_xattn_Wkv"],
        "L0_xattn_Wout": a["L0_xattn_Wout"], "L0_xattn_bout": a["L0_xattn_bout"],
        "L1_attn_Wq": a["L1_attn_Wq"], "L1_attn_Wkv": np.concatenate([a["L1_attn_Wk"], a["L1_attn_Wv"]], 1),
        "L1_attn_Wo": a["L1_attn_Wo"], "L1_attn_bo": a["L1_attn_bo"],
    }


def build(nc, W, out, layers=6):
    with ExitStack() as stack:
        G = Names()
        G.STAGE, G.NSTAGE = 1024, 3

        def sb(name, shape, dt):
            return stack.enter_context(nc.sbuf_tensor(name, shape, dt))

        G.x = sb("x_all", [P, (B + 1) * NT, E], F32)
        G.stage = sb("stage", [P, G.NSTAGE, G.STAGE], F32)
        G.ident = sb("ident", [P, P], F32)
        G.ident_b = sb("ident_b", [P, P], BF16)
        G.ident_h = sb("ident_h", [P, P], F16)
        G.causal = sb("causal", [P, P], BF16)
        G.ones = sb("ones", [P, N], F32)
        G.ones_h = sb("ones_h", [P, P], F16)
        G.minus_half = sb("minus_half", [P, 1], F32)
        G.junk = sb("junk", [P, 1], F32)
        G.r = sb("ln_r", [P, NT, E], F32)
        G.stats = sb("ln_stats", [P, NT, 6], F32)
        G.mv = sb("ln_mv", [P, NT, 2], F32)
        G.ve = sb("ln_ve", [P, NT], F32)
        G.rstd = sb("ln_rstd", [P, NT], F32)
        bank = lambda name: stack.enter_context(nc.psum_tensor(name, [P, 512], F32))
        G.psS = [bank("psS0"), bank("psS1")]
        G.psT = [bank("psT0"), bank("psT1")]
        G.psO = [bank("psO0"), bank("psO1")]
        G.psP = [bank("psP0"), bank("psP1")]

        in_done = stack.enter_context(nc.semaphore("in_done"))
        const_step = stack.enter_context(nc.semaphore("const_step"))
        out_done = stack.enter_context(nc.semaphore("out_done"))
        with nc.Block() as block:
            @block.sync
            def _(sp):
                sp.dma_start(G.x[:, 0:B * NT, :], W["x"].rearrange("b (n p) e -> p (b n) e", p=P)).then_inc(in_done, 16)
                sp.wait_ge(in_done, 16)

            @block.gpsimd
            def _(pool):
                pool.memset(G.ident[:, :], 0.0).then_inc(const_step, 1)
                pool.memset(G.causal[:, :], 0.0).then_inc(const_step, 1)
                pool.memset(G.ones[:, :], 1.0)
                pool.memset(G.x[:, B * NT:(B + 1) * NT, :], 0.0)
                pool.memset(G.ones_h[:, :], 1.0)
                pool.memset(G.minus_half[:, :], -0.5)
                pool.wait_ge(const_step, 2)
                pool.affine_select(out=G.ident[:, :], in_=G.ident[:, :], compare_op=ALU.not_equal, fill=1.0,
                                   base=0, pattern=[[-1, P]], channel_multiplier=1).then_inc(const_step, 1)
                pool.affine_select(out=G.causal[:, :], in_=G.causal[:, :], compare_op=ALU.is_ge, fill=MASKED,
                                   base=0, pattern=[[-1, P]], channel_multiplier=1)
                pool.wait_ge(const_step, 3)
                pool.tensor_copy(G.ident_b[:, :], G.ident[:, :])
                pool.tensor_copy(G.ident_h[:, :], G.ident[:, :])

        for layer in LAYERS[:layers]:
            layer(nc, G, W)

        with nc.Block() as block:
            @block.sync
            def _(sp):
                sp.dma_start(out.rearrange("b (n p) e -> p (b n) e", p=P), G.x[:, 0:B * NT, :]).then_inc(out_done, 16)
                sp.wait_ge(out_done, 16)


LAYERS = [attn0, xattn0, ffn0, attn1, xattn1, ffn1]


def kernel(**inputs):
    import concourse.bacc as bacc
    from concourse.bass_utils import run_bass_kernel_spmd as run

    def rope_tables(scale):
        half = 64
        inv = 10000.0 ** (-np.arange(0, 2 * half, 2, dtype=np.float32) / np.float32(2 * half))
        ang = np.arange(N, dtype=np.float32)[:, None] * inv.astype(np.float32)[None, :]
        cos, sin = np.cos(ang), np.sin(ang)
        return (np.stack([np.concatenate([cos, cos], 1), np.concatenate([-sin, sin], 1)]) * scale).astype(np.float32)

    nc = bacc.Bacc("TRN2", target_bir_lowering=False, num_devices=1)
    a = {k: np.asarray(v) for k, v in inputs.items()}
    host = {
        "x": a["x"],
        "L0_attn_WqT": a["L0_attn_Wq"].T, "L0_attn_WkvT": a["L0_attn_Wkv"].T,
        "L0_attn_WhT": np.concatenate([a["L0_attn_Wkvh"], a["L0_attn_Wg"]], 0).T,
        "L0_attn_WoutT": a["L0_attn_Wout"].T,
        "rope_q": rope_tables(1.0 / np.sqrt(128.0)), "rope_k": rope_tables(1.0),
    }
    host.update(more_inputs(a))
    arrays, W = {}, {}
    for name, value in host.items():
        value = np.ascontiguousarray(value)
        arrays[f"in_{name}"] = value
        W[name] = nc.dram_tensor(f"in_{name}", value.shape, mybir.dt.from_np(value.dtype),
                                          kind="ExternalInput").ap()
    out = nc.dram_tensor("out_dram", (B, N, E), F32, kind="ExternalOutput").ap()
    build(nc, W, out)
    r = run(nc, [arrays], core_ids=[0])
    return r.results[0]["out_dram"]
```
